# Optimizing a Trainium2 kernel written in Bass

```python
import numpy as np
import jax
import jax.numpy as jnp

def _softmax(x, axis=-1):
    return jax.nn.softmax(x, axis=axis)

def _gelu(x):
    return jax.nn.gelu(x, approximate=True)

def _silu(x):
    return jax.nn.silu(x)

def _sigmoid(x):
    return jax.nn.sigmoid(x)

def _layernorm(x, axis=-1, eps=1e-05):
    m = jnp.mean(x, axis=axis, keepdims=True)
    v = jnp.var(x, axis=axis, keepdims=True)
    return (x - m) / jnp.sqrt(v + eps)

def _scatter_add(tgt, idx, src, axis=0):
    return tgt.at[idx].add(src)

def _segment_sum(src, seg, n):
    return jax.ops.segment_sum(src, seg, n)
kernel_name = 'mk_gnn_preln_d4_gnn_r8_1b7988'

def setup_inputs(seed: int=0):
    np.random.seed(seed)
    _w = jnp.asarray

    def _rec_inputs():
        import jax
        import jax.numpy as jnp
        _gk = jax.random.key(seed)
        x = -0.000202 + 1 * jax.random.normal(jax.random.fold_in(_gk, 1), (6250, 128), jnp.float32)
        _s = jax.random.randint(jax.random.fold_in(_gk, 2), (50000,), 0, 6250, jnp.int32)
        _d = jax.random.randint(jax.random.fold_in(_gk, 3), (50000,), 0, 6250, jnp.int32)
        _loop = jnp.arange(6250, dtype=jnp.int32)
        src = jnp.concatenate([_s, _d, _loop])
        dst = jnp.concatenate([_d, _s, _loop])
        _o = jnp.argsort(dst, stable=True)
        src = src[_o]
        dst = dst[_o]
        edge_attr_128 = -5.16925e-05 + 1.00005 * jax.random.normal(jax.random.fold_in(_gk, 11), (106250, 128), jnp.float32)
        return (x, src, dst, edge_attr_128)
    x, src, dst, edge_attr_128 = _rec_inputs()

    def _L0_gnn_setup():
        import jax, jax.numpy as jnp
        import numpy as np
        N = 6250
        E = 100000
        F_IN = 128
        F_OUT = 128
        NEG_SLOPE = 0.2
        key = jax.random.key(seed)
        k1, k2, k3, k4 = jax.random.split(key, 4)
        x = jax.random.normal(k1, (N, F_IN), dtype=jnp.float32)
        edge_index = jax.random.randint(k2, (2, E), 0, N, dtype=jnp.int32)
        W = jax.random.normal(k3, (F_OUT, F_IN), dtype=jnp.float32) * 0.05
        a = jax.random.normal(k4, (2 * F_OUT,), dtype=jnp.float32) * 0.05
        return {'x': x, 'edge_index': edge_index, 'W': W, 'a': a}
    _L0_gnn_all = _L0_gnn_setup()
    _L0_gnn_in = {k: v for k, v in _L0_gnn_all.items() if k in ('W', 'a')}
    del _L0_gnn_all

    def _L1_gnn_setup():
        import jax, jax.numpy as jnp
        import numpy as np
        N_NODES = 6250
        N_EDGES = 200000
        DIM = 128
        SLOPE = 0.2
        key = jax.random.key(seed)
        ks = jax.random.split(key, 9)
        indices = jax.random.randint(ks[0], (2, N_EDGES), 0, N_NODES)
        features = jax.random.normal(ks[1], (N_NODES, DIM), dtype=jnp.float32)
        W1_w = jax.random.normal(ks[2], (DIM, DIM), dtype=jnp.float32) * 0.05
        W1_b = jax.random.normal(ks[3], (DIM,), dtype=jnp.float32) * 0.05
        W2_w = jax.random.normal(ks[4], (DIM, DIM), dtype=jnp.float32) * 0.05
        W2_b = jax.random.normal(ks[5], (DIM,), dtype=jnp.float32) * 0.05
        Watt_w = jax.random.normal(ks[6], (DIM, DIM), dtype=jnp.float32) * 0.05
        Watt_b = jax.random.normal(ks[7], (DIM,), dtype=jnp.float32) * 0.05
        a = jax.random.normal(ks[8], (2 * DIM, 1), dtype=jnp.float32) * 0.05
        return {'indices': indices, 'features': features, 'num_nodes': N_NODES, 'W1_w': W1_w, 'W1_b': W1_b, 'W2_w': W2_w, 'W2_b': W2_b, 'Watt_w': Watt_w, 'Watt_b': Watt_b, 'a': a}
    _L1_gnn_all = _L1_gnn_setup()
    _L1_gnn_in = {k: v for k, v in _L1_gnn_all.items() if k in ('W1_w', 'W1_b', 'W2_w', 'W2_b', 'Watt_w', 'Watt_b', 'a')}
    del _L1_gnn_all

    def _L2_gnn_setup():
        import jax, jax.numpy as jnp
        import numpy as np
        N = 6250
        E = 200000
        D = 128
        L = 3
        key = jax.random.key(seed)
        ks = jax.random.split(key, 8)
        x = jax.random.normal(ks[0], (N, D), dtype=jnp.float32)
        edge_index = jax.random.randint(ks[1], (2, E), 0, N, dtype=jnp.int64)
        s = 1.0 / np.sqrt(D)
        W_pre = jax.random.uniform(ks[2], (D, D), jnp.float32, -s, s)
        b_pre = jnp.zeros((D,), jnp.float32)
        W_conv = jax.random.uniform(ks[3], (L, D, D), jnp.float32, -s, s)
        b_conv = jnp.zeros((L, D), jnp.float32)
        s2 = 1.0 / np.sqrt(2 * D)
        W_upd = jax.random.uniform(ks[4], (L, 2 * D, D), jnp.float32, -s2, s2)
        b_upd = jnp.zeros((L, D), jnp.float32)
        return {'x': x, 'edge_index': edge_index, 'W_pre': W_pre, 'b_pre': b_pre, 'W_conv': W_conv, 'b_conv': b_conv, 'W_upd': W_upd, 'b_upd': b_upd}
    _L2_gnn_all = _L2_gnn_setup()
    _L2_gnn_in = {k: v for k, v in _L2_gnn_all.items() if k in ('W_pre', 'b_pre', 'W_conv', 'b_conv', 'W_upd', 'b_upd')}
    del _L2_gnn_all

    def _L3_gnn_setup():
        import jax, jax.numpy as jnp
        import numpy as np
        N_NODES = 6250
        N_EDGES = 100000
        C = 128
        D = 128
        Z = 2 * C + D
        key = jax.random.key(seed)
        ks = jax.random.split(key, 7)
        x = jax.random.normal(ks[0], (N_NODES, C), dtype=jnp.float32)
        edge_index = jax.random.randint(ks[1], (2, N_EDGES), 0, N_NODES, dtype=jnp.int64)
        edge_attr = jax.random.normal(ks[2], (N_EDGES, D), dtype=jnp.float32)
        s = 1.0 / np.sqrt(Z)
        W_f = jax.random.uniform(ks[3], (Z, C), dtype=jnp.float32, minval=-s, maxval=s)
        b_f = jax.random.uniform(ks[4], (C,), dtype=jnp.float32, minval=-s, maxval=s)
        W_s = jax.random.uniform(ks[5], (Z, C), dtype=jnp.float32, minval=-s, maxval=s)
        b_s = jax.random.uniform(ks[6], (C,), dtype=jnp.float32, minval=-s, maxval=s)
        return {'x': x, 'edge_index': edge_index, 'edge_attr': edge_attr, 'W_f': W_f, 'b_f': b_f, 'W_s': W_s, 'b_s': b_s}
    _L3_gnn_all = _L3_gnn_setup()
    _L3_gnn_in = {k: v for k, v in _L3_gnn_all.items() if k in ('W_f', 'b_f', 'W_s', 'b_s')}
    del _L3_gnn_all
    return {'x': x, 'src': src, 'dst': dst, 'edge_attr_128': edge_attr_128, 'L0_gnn_W': _L0_gnn_in['W'], 'L0_gnn_a': _L0_gnn_in['a'], 'L1_gnn_W1_w': _L1_gnn_in['W1_w'], 'L1_gnn_W1_b': _L1_gnn_in['W1_b'], 'L1_gnn_W2_w': _L1_gnn_in['W2_w'], 'L1_gnn_W2_b': _L1_gnn_in['W2_b'], 'L1_gnn_Watt_w': _L1_gnn_in['Watt_w'], 'L1_gnn_Watt_b': _L1_gnn_in['Watt_b'], 'L1_gnn_a': _L1_gnn_in['a'], 'L2_gnn_W_pre': _L2_gnn_in['W_pre'], 'L2_gnn_b_pre': _L2_gnn_in['b_pre'], 'L2_gnn_W_conv': _L2_gnn_in['W_conv'], 'L2_gnn_b_conv': _L2_gnn_in['b_conv'], 'L2_gnn_W_upd': _L2_gnn_in['W_upd'], 'L2_gnn_b_upd': _L2_gnn_in['b_upd'], 'L3_gnn_W_f': _L3_gnn_in['W_f'], 'L3_gnn_b_f': _L3_gnn_in['b_f'], 'L3_gnn_W_s': _L3_gnn_in['W_s'], 'L3_gnn_b_s': _L3_gnn_in['b_s']}

def reference(x, src, dst, edge_attr_128, L0_gnn_W, L0_gnn_a, L1_gnn_W1_w, L1_gnn_W1_b, L1_gnn_W2_w, L1_gnn_W2_b, L1_gnn_Watt_w, L1_gnn_Watt_b, L1_gnn_a, L2_gnn_W_pre, L2_gnn_b_pre, L2_gnn_W_conv, L2_gnn_b_conv, L2_gnn_W_upd, L2_gnn_b_upd, L3_gnn_W_f, L3_gnn_b_f, L3_gnn_W_s, L3_gnn_b_s):
    import jax
    import jax.numpy as jnp

    def _L0_gnn_ref(x, edge_index, W, a):
        import jax, jax.numpy as jnp
        import numpy as np
        N = 6250
        E = 100000
        F_IN = 128
        F_OUT = 128
        NEG_SLOPE = 0.2
        src = edge_index[0]
        dst = edge_index[1]
        h = x @ W.T
        s_src = h @ a[:F_OUT]
        s_dst = h @ a[F_OUT:]
        e = s_src[src] + s_dst[dst]
        e = jnp.where(e > 0, e, NEG_SLOPE * e)
        row_max = jax.ops.segment_max(e, src, num_segments=N)
        row_max = jnp.maximum(row_max, 0.0)
        v = jnp.exp(e - row_max[src])
        row_sum = jax.ops.segment_sum(v, src, num_segments=N)
        row_sum = jnp.where(row_sum == 0, 1.0, row_sum)
        v = v / row_sum[src]
        out = jax.ops.segment_sum(v[:, None] * h[dst], src, num_segments=N)
        return out

    def _L1_gnn_ref(indices, features, num_nodes, W1_w, W1_b, W2_w, W2_b, Watt_w, Watt_b, a):
        import jax, jax.numpy as jnp
        import numpy as np
        N_NODES = 6250
        N_EDGES = 200000
        DIM = 128
        SLOPE = 0.2
        src, dst = (indices[0], indices[1])
        d = W1_w.shape[1]
        h_att = features @ Watt_w + Watt_b
        a1, a2 = (a[:d], a[d:])
        e = jax.nn.leaky_relu(h_att[src] @ a1 + h_att[dst] @ a2, SLOPE)
        e = e - jnp.max(e)
        exp_e = jnp.exp(e)
        denom = jax.ops.segment_sum(exp_e, dst, num_segments=num_nodes)
        alpha = exp_e / (denom[dst] + 1e-09)
        h_msg = features @ W1_w + W1_b
        weighted = h_msg[src] * alpha
        h_neigh = jax.ops.segment_sum(weighted, dst, num_segments=num_nodes)
        h_self = features
        sum_h = h_self + h_neigh
        prod_h = h_self * h_neigh
        return jax.nn.leaky_relu(sum_h + prod_h @ W2_w + W2_b, SLOPE)

    def _L2_gnn_ref(x, edge_index, W_pre, b_pre, W_conv, b_conv, W_upd, b_upd):
        import jax, jax.numpy as jnp
        import numpy as np
        N = 6250
        E = 200000
        D = 128
        L = 3
        h = x @ W_pre + b_pre
        src = edge_index[0]
        dst = edge_index[1]
        loop_mask = (src != dst).astype(h.dtype)[:, None]
        for l in range(L):
            msgs = h[src] * loop_mask
            agg = jax.ops.segment_sum(msgs, dst, num_segments=N)
            x_neigh = agg @ W_conv[l] + b_conv[l]
            h = jnp.concatenate([x_neigh, h], axis=-1) @ W_upd[l] + b_upd[l]
            h = jax.nn.relu(h)
        return h

    def _L3_gnn_ref(x, edge_index, edge_attr, W_f, b_f, W_s, b_s):
        import jax, jax.numpy as jnp
        import numpy as np
        N_NODES = 6250
        N_EDGES = 100000
        C = 128
        D = 128
        Z = 2 * C + D
        src = edge_index[0]
        dst = edge_index[1]
        z = jnp.concatenate([x[dst], x[src], edge_attr], axis=-1)
        gate = jax.nn.sigmoid(z @ W_f + b_f)
        core = jax.nn.softplus(z @ W_s + b_s)
        msg = gate * core
        agg = jax.ops.segment_sum(msg, dst, num_segments=x.shape[0])
        return x + agg
    edge_index = jnp.stack([src, dst])
    h = jnp.maximum(_layernorm(x, axis=-1), 0.0)
    x = x + _L0_gnn_ref(h, edge_index, L0_gnn_W, L0_gnn_a)
    h = jnp.maximum(_layernorm(x, axis=-1), 0.0)
    x = x + _L1_gnn_ref(edge_index, h, 6250, L1_gnn_W1_w, L1_gnn_W1_b, L1_gnn_W2_w, L1_gnn_W2_b, L1_gnn_Watt_w, L1_gnn_Watt_b, L1_gnn_a)
    h = jnp.maximum(_layernorm(x, axis=-1), 0.0)
    x = x + _L2_gnn_ref(h, edge_index, L2_gnn_W_pre, L2_gnn_b_pre, L2_gnn_W_conv, L2_gnn_b_conv, L2_gnn_W_upd, L2_gnn_b_upd)
    h = jnp.maximum(_layernorm(x, axis=-1), 0.0)
    x = x + _L3_gnn_ref(h, edge_index, edge_attr_128, L3_gnn_W_f, L3_gnn_b_f, L3_gnn_W_s, L3_gnn_b_s)
    return x

_drawn_inputs = setup_inputs


def setup_inputs(seed=0):
    import zlib

    import numpy as np

    out = dict(_drawn_inputs(seed))
    spreads = {'L2_gnn_b_pre': (0.0, 0.1), 'L2_gnn_b_conv': (0.0, 0.1), 'L2_gnn_b_upd': (0.0, 0.1)}
    factors = {'L0_gnn_a': 6.926,
     'L1_gnn_W1_b': 200.0,
     'L1_gnn_Watt_w': 200.0,
     'L1_gnn_Watt_b': 64.0,
     'L1_gnn_a': 200.0,
     'L3_gnn_b_f': 6.972,
     'L3_gnn_b_s': 4.523,
     'L1_gnn_W1_w': 50.291,
     'L1_gnn_W2_w': 43.465}
    for name, (base, spread) in spreads.items():
        noise = np.random.default_rng([zlib.crc32(name.encode()), seed]).standard_normal(out[name].shape)
        drawn = base * np.exp(spread * noise) if base else spread * noise
        out[name] = jnp.asarray(drawn.astype(out[name].dtype))
    for name, factor in factors.items():
        out[name] = (out[name] * factor).astype(out[name].dtype)
    return out
```

```python
from contextlib import ExitStack

import concourse.bass as bass
from concourse import mybir

F32 = mybir.dt.float32
BF16 = mybir.dt.bfloat16
I32 = mybir.dt.int32
ALU = mybir.AluOpType
ACT = mybir.ActivationFunctionType
AX = mybir.AxisListType
RMAX = bass.bass_isa.ReduceOp.max

P = 128
N = 6250
E = 106250
D = 128
BLKS = -(-N // P)
TAIL = N - (BLKS - 1) * P
NB = BLKS + 3
BUCKETS = BLKS + 1
COLS = 832
LASTROW = E - (P - 1) * COLS
PADS = P * COLS - E
PADKEY = BLKS * P
U = 4
RING = 4
TILES = 880
BATCHES = TILES // U
assert (E + BLKS * (P - 1)) // P + -(-PADS // P) <= TILES and BATCHES % RING == 0
REC = 4
FAR = -1.0e30
FLOOR = -1.0e28
SLOPE = 0.2
SU = 8
SR = 4
SLAB = NB * 131 + 36
W_ATT = 131
DB = 2
DBATCHES = NB // DB


def steps(eng, count, ring, lag, step):
    for s in range(ring):
        step(s, s)
    with eng.Fori(1, count // ring) as i:
        for r in range(ring):
            step(i * ring + r, r)
    for s in range(count, count + lag):
        step(s, s % ring)


def past(s, lag):
    return not isinstance(s, int) or s >= lag


def within(s, count):
    return not isinstance(s, int) or s < count


def block_registers(nc, eng, words, batch):
    word = eng.value_load(words[0:1, bass.ds(batch, 1)], min_val=0, max_val=0x3F3F3F3F)
    return [nc.s_assert_within(eng.snap((word >> (8 * k)) & 63), 0, BLKS - 1,
                               skip_runtime_bounds_check_because="a tile's block is counted over BLKS - 1 blocks")
            for k in range(U)]


def hold_wait(eng, passed):
    eng.sem_inc(passed, 1)


def gnn(nc, io, out):
    with ExitStack() as ctx:
        def sb(name, shape, dt=F32):
            return ctx.enter_context(nc.sbuf_tensor(name, shape, dt))

        def dram(name, shape, dt=F32):
            return nc.dram_tensor(name, shape, dt, kind="Internal").ap()

        in_use = []

        def sem(name):
            in_use.append(nc.alloc_semaphore(name=name))
            return in_use[-1]

        def release():
            nc.clear_and_free_semaphores(list(in_use))
            in_use.clear()
            nc.all_engine_barrier()

        slab_x = sb("slab_x", [P, SLAB])
        slab_h = sb("slab_h", [P, SLAB])
        slab_acc = sb("slab_acc", [P, SLAB])
        slab_a = sb("slab_a", [P, SLAB])
        slab_b = sb("slab_b", [P, SLAB])
        rows = sb("rows", [P, RING * U * 256])
        rows2 = sb("rows2", [P, RING * U * 128])

        def blocks(slab, width=D, n=NB):
            return slab[:, 0:n * width].rearrange("p (b f) -> p b f", f=width)

        x_v, h_v = blocks(slab_x), blocks(slab_h)

        ident = sb("ident", [P, P])
        quarter = sb("quarter", [P, P])
        quarter_bf = sb("quarter_bf", [P, P], BF16)
        tri = sb("tri", [P, P])
        lane = sb("lane", [P, P])
        lane_bf = sb("lane_bf", [P, P], BF16)
        ones = sb("ones", [P, P])
        stats = sb("stats", [P, 4, NB])

        by_src = {"idx": sb("src_idx", [P, TILES], I32), "lo": sb("src_lo", [P, TILES]),
                  "words": sb("src_words", [1, BATCHES], I32), "same": sb("src_same", [P, TILES])}
        by_dst = {"idx": sb("dst_idx", [P, TILES], I32), "lo": sb("dst_lo", [P, TILES]),
                  "words": sb("dst_words", [1, BATCHES], I32), "same": sb("dst_same", [P, TILES]),
                  "noloop": sb("dst_noloop", [P, TILES]), "edge": sb("dst_edge", [P, TILES], I32)}
        stage_idx = sb("stage_idx", [P, RING, U], I32)
        stage_edge = sb("stage_edge", [P, RING, U], I32)

        sorted_src = dram("sorted_src", [P, TILES * REC])
        sorted_dst = dram("sorted_dst", [P, TILES * REC])
        tab0 = dram("tab0", [NB * P, W_ATT])
        tab1 = dram("tab1", [NB * P, W_ATT])
        tab2 = [dram(f"tab2_{n}", [NB * P, D]) for n in range(3)]
        tab3 = dram("tab3", [NB * P, 2 * D])

        weights, biases = {}, {}
        for name, width in (("l0", W_ATT), ("l1", W_ATT), ("l1w2", D), ("pre", D), ("td", 2 * D), ("ts", 2 * D),
                            ("edge", 2 * D)) + tuple((f"{k}{n}", D) for n in range(3) for k in ("agg", "own")):
            weights[name] = sb(f"w_{name}", [P, width])
        for name, width in (("l0", W_ATT), ("l1", W_ATT), ("l1w2", D), ("pre", D), ("td", 2 * D),
                            ("u0", D), ("u1", D), ("u2", D)):
            biases[name] = sb(f"b_{name}", [P, width])

        def constants():
            loaded, made, filled = sem("c_loaded"), sem("c_made"), sem("c_filled")
            with nc.Block() as block:
                @block.gpsimd
                def _(pool):
                    pool.memset(ident[:], 0.0).then_inc(made, 1)
                    pool.memset(tri[:], 1.0).then_inc(made, 1)
                    pool.iota(lane[:], pattern=[[1, P]], base=0, channel_multiplier=0,
                              allow_small_or_imprecise_dtypes=True).then_inc(made, 1)
                    pool.iota(lane_bf[:], pattern=[[1, P]], base=0, channel_multiplier=0,
                              allow_small_or_imprecise_dtypes=True).then_inc(made, 1)
                    pool.wait_ge(made, 4)
                    pool.affine_select(out=ident[:], in_=ident[:], compare_op=ALU.not_equal, fill=1.0, base=0,
                                       pattern=[[-1, P]], channel_multiplier=1).then_inc(made, 1)
                    pool.affine_select(out=tri[:], in_=tri[:], compare_op=ALU.is_gt, fill=0.0, base=0,
                                       pattern=[[1, P]], channel_multiplier=-1).then_inc(made, 1)

                @block.vector
                def _(dve):
                    dve.memset(ones[:], 1.0)
                    dve.memset(slab_x[:], 0.0).then_inc(filled, 1)
                    dve.wait_ge(made, 5)
                    dve.tensor_scalar(quarter[:], ident[:], 0.25, None, ALU.mult)
                    dve.tensor_scalar(quarter_bf[:], ident[:], 0.25, None, ALU.mult)

                @block.sync
                def _(sp):
                    sp.wait_ge(filled, 1)
                    sp.dma_start(x_v[:, 0:BLKS - 1, :],
                                 io["x"][0:(BLKS - 1) * P, :].rearrange("(b p) f -> p b f", p=P)).then_inc(loaded, 16)
                    sp.dma_start(x_v[0:TAIL, BLKS - 1, :], io["x"][(BLKS - 1) * P:N, :]).then_inc(loaded, 16)
                    sp.wait_ge(loaded, 32)

        def sort_views(home):
            work = slab_b
            col = lambda n: work[:, n * COLS:(n + 1) * COLS]
            return {"record": home[:, 0:COLS * REC].rearrange("p (c w) -> p c w", w=REC),
                    "slot": home[:, COLS * REC:COLS * (REC + 1)].bitcast(I32),
                    "key": col(0).bitcast(I32), "nbr": col(1).bitcast(I32), "blk": col(2), "mask": col(3),
                    "scan": col(4), "pos": col(5), "int": col(6).bitcast(I32), "int2": col(7).bitcast(I32)}

        cnt = sb("cnt", [P, 64])
        base = sb("base", [P, 64])
        start = sb("start", [P, 4])
        start_i = sb("start_i", [P, 1], I32)
        pick = sb("pick", [P, P])

        def place_edges(tag, key_in, nbr_in, home, table, order, with_loops, scatter_of=None):
            v = sort_views(home)
            loaded, ready, chain = sem(f"{tag}_loaded"), sem(f"{tag}_ready"), sem(f"{tag}_chain")
            counted, placed, summed = sem(f"{tag}_counted"), sem(f"{tag}_placed"), sem(f"{tag}_summed")
            picked = sem(f"{tag}_picked")
            cleared, masked, passed = sem(f"{tag}_cleared"), sem(f"{tag}_masked"), sem(f"{tag}_passed")
            fill = rows[:, 0:TILES * REC]
            with ExitStack() as local, nc.Block() as block:
                tot = local.enter_context(nc.psum_tensor(f"{tag}_tot", [P, 512], F32))
                bas = local.enter_context(nc.psum_tensor(f"{tag}_bas", [P, 512], F32))
                til = local.enter_context(nc.psum_tensor(f"{tag}_til", [P, 2, 512], F32))

                @block.sync
                def _(sp):
                    sp.wait_ge(ready, 1)
                    for dst, src in ((v["key"], key_in), (v["nbr"], nbr_in)):
                        sp.dma_start(dst[0:P - 1, :], src[0:(P - 1) * COLS].rearrange("(p c) -> p c", c=COLS)
                                     ).then_inc(loaded, 16)
                        sp.dma_start(dst[P - 1:P, 0:LASTROW],
                                     src[(P - 1) * COLS:E].rearrange("(p c) -> p c", p=1)).then_inc(loaded, 16)
                    sp.wait_ge(ready, 2)
                    sp.dma_start(table[:, :], fill).then_inc(cleared, 16)
                    sp.wait_ge(cleared, 16)

                @block.vector
                def _(dve):
                    count = [0]

                    def link(ins):
                        count[0] += 1
                        ins.then_inc(chain, 1)
                        dve.wait_ge(chain, count[0])

                    dve.memset(v["key"], PADKEY)
                    dve.memset(v["nbr"], PADKEY).then_inc(ready, 1)
                    f = fill.rearrange("p (t w) -> p t w", w=REC)
                    link(dve.memset(f, 0.0))
                    dve.memset(f[:, :, 1:3], -1.0).then_inc(ready, 1)
                    dve.wait_ge(loaded, 64)
                    rec = v["record"]
                    link(dve.tensor_single_scalar(v["int"], v["key"], 7, ALU.logical_shift_right))
                    link(dve.tensor_copy(v["blk"], v["int"]))
                    link(dve.tensor_single_scalar(v["int2"], v["key"], P - 1, ALU.bitwise_and))
                    link(dve.tensor_scalar(v["scan"], v["blk"], float(BLKS), -1000.0, ALU.is_equal, ALU.mult))
                    link(dve.tensor_tensor(rec[:, :, 1], v["int2"], v["scan"], ALU.add))
                    link(dve.tensor_copy(rec[:, :, 0], v["nbr"]))
                    if with_loops:
                        link(dve.tensor_tensor(v["mask"], v["key"], v["nbr"], ALU.is_equal))
                        link(dve.scalar_tensor_tensor(rec[:, :, 2], v["mask"], -1000.0, rec[:, :, 1],
                                                      ALU.mult, ALU.add))
                        dve.wait_ge(placed, 1)
                        link(dve.tensor_scalar(rec[:, :, 3], v["int"], float(E - 1), None, ALU.min))
                    else:
                        link(dve.memset(rec[:, :, 2:4], 0.0))

                    with dve.Fori(0, BUCKETS) as b:
                        dve.tensor_scalar(v["mask"], v["blk"], lane[:, bass.ds(b, 1)], 0.0, ALU.is_equal, ALU.add,
                                          accum_out=cnt[:, bass.ds(b, 1)]).then_inc(masked, 1)
                        dve.wait_ge(masked, b + 1)
                    link(dve.tensor_copy(cnt[:, BUCKETS:BUCKETS + 1], ones[:, 0:1]))
                    dve.tensor_copy(start[:, 3:4], ones[:, 0:1]).then_inc(counted, 1)
                    dve.wait_ge(summed, 1)
                    link(dve.tensor_scalar(start_i[0:BUCKETS, :], tot[0:BUCKETS, 0:1], float(P - 1), None, ALU.add))
                    link(dve.tensor_single_scalar(start_i[0:BUCKETS, :], start_i[0:BUCKETS, :], 7,
                                                  ALU.logical_shift_right))
                    dve.tensor_copy(start[0:BUCKETS, 0:1], start_i[0:BUCKETS, :]).then_inc(counted, 1)
                    dve.wait_ge(summed, 2)
                    link(dve.tensor_copy(start[0:BUCKETS, 1:2], tot[0:BUCKETS, 1:2]))
                    link(dve.tensor_scalar(start[0:BUCKETS, 2:3], start[0:BUCKETS, 1:2], float(P), None, ALU.mult))
                    dve.wait_ge(placed, 2)
                    dve.tensor_scalar(v["pos"][0:BUCKETS, 0:COLS], v["scan"][0:BUCKETS, 0:COLS],
                                      start[0:BUCKETS, 1:2], None, ALU.is_ge)
                    dve.tensor_scalar(v["mask"][0:BUCKETS, 0:TILES - COLS], v["scan"][0:BUCKETS, 0:TILES - COLS],
                                      float(COLS), start[0:BUCKETS, 1:2], ALU.add, ALU.is_ge).then_inc(counted, 1)
                    dve.wait_ge(summed, 3)
                    link(dve.tensor_copy(base[:, 0:BUCKETS], bas[:, 0:BUCKETS]))
                    tb = rows2[:, 0:TILES]
                    dve.tensor_copy(tb[:, 0:512], til[:, 0, :])
                    link(dve.tensor_copy(tb[:, 512:TILES], til[:, 1, 0:TILES - 512]))
                    dve.memset(order["same"][:, 0:1], 0.0)
                    link(dve.tensor_tensor(order["same"][:, 1:TILES], tb[:, 1:TILES], tb[:, 0:TILES - 1],
                                           ALU.is_equal))
                    if with_loops:
                        link(dve.tensor_scalar(order["same"][:, :], order["same"][:, :], 1.0, -FAR,
                                               ALU.subtract, ALU.mult))
                    tbi = rows2[0:1, TILES:2 * TILES].bitcast(I32)
                    link(dve.tensor_copy(tbi, tb[0:1, :]))
                    quad = tbi.rearrange("p (b k) -> p b k", k=U)
                    link(dve.tensor_copy(order["words"][:, :], quad[:, :, 0]))
                    for k in range(1, U):
                        link(dve.tensor_single_scalar(quad[:, :, k], quad[:, :, k], 8 * k, ALU.logical_shift_left))
                        link(dve.tensor_tensor(order["words"][:, :], order["words"][:, :], quad[:, :, k],
                                               ALU.bitwise_or))
                    with dve.Fori(0, BUCKETS) as b:
                        dve.tensor_scalar(v["mask"], v["blk"], lane[:, bass.ds(b, 1)], None, ALU.is_equal
                                          ).then_inc(masked, 1)
                        dve.wait_ge(masked, b * 3 + BUCKETS + 1)
                        dve.tensor_tensor_scan(v["scan"], v["mask"], v["mask"], base[:, bass.ds(b, 1)],
                                               ALU.add, ALU.max).then_inc(masked, 1)
                        dve.wait_ge(masked, b * 3 + BUCKETS + 2)
                        hold_wait(dve, passed)
                        dve.copy_predicated(v["pos"], v["mask"].bitcast(I32), v["scan"]).then_inc(masked, 1)
                        dve.wait_ge(masked, b * 3 + BUCKETS + 3)
                    link(dve.tensor_scalar(v["int"], v["pos"], -1.0, None, ALU.add))
                    link(dve.tensor_single_scalar(v["int2"], v["int"], P - 1, ALU.bitwise_and))
                    link(dve.tensor_single_scalar(v["int"], v["int"], 7, ALU.logical_shift_right))
                    link(dve.scalar_tensor_tensor(v["slot"], v["int2"], float(TILES), v["int"], ALU.mult, ALU.add))

                @block.tensor
                def _(pe):
                    pe.wait_ge(counted, 1)
                    pe.matmul(tot[0:BUCKETS, 0:1], cnt[:, 0:BUCKETS], start[:, 3:4], start=True, stop=True
                              ).then_inc(summed, 1)
                    pe.wait_ge(counted, 2)
                    pe.matmul(tot[0:BUCKETS, 1:2], tri[0:BUCKETS, 0:BUCKETS], start[0:BUCKETS, 0:1],
                              start=True, stop=True).then_inc(summed, 1)
                    pe.wait_ge(counted, 3)
                    pe.matmul(bas[:, 0:BUCKETS], tri[:, :], cnt[:, 0:BUCKETS], start=True, stop=False)
                    pe.matmul(bas[:, 0:BUCKETS], start[0:BUCKETS, 2:3].to_broadcast([BUCKETS, P]),
                              ident[0:BUCKETS, 0:BUCKETS], start=False, stop=True)
                    pk = pick[0:BUCKETS, :]
                    pe.matmul(til[:, 0, :], pk, v["pos"][0:BUCKETS, 0:512], start=True, stop=True)
                    pe.matmul(til[:, 1, 0:COLS - 512], pk, v["pos"][0:BUCKETS, 512:COLS], start=True, stop=True)
                    pe.matmul(til[:, 1, COLS - 512:TILES - 512], pk, v["mask"][0:BUCKETS, 0:TILES - COLS],
                              start=True, stop=True).then_inc(summed, 1)

                @block.gpsimd
                def _(pool):
                    if with_loops:
                        pool.wait_ge(chain, 3)
                        pool.iota(v["int"], pattern=[[1, COLS]], base=0, channel_multiplier=COLS).then_inc(placed, 1)
                    else:
                        pool.memset(pick[:], 1.0).then_inc(placed, 1)
                        pool.wait_ge(placed, 1)
                        pool.affine_select(out=pick[:], in_=pick[:], compare_op=ALU.not_equal, fill=0.0, base=0,
                                           pattern=[[0, P]], channel_multiplier=1).then_inc(picked, 1)
                        pool.wait_ge(picked, 1)
                        pool.affine_select(out=pick[:], in_=pick[:], compare_op=ALU.not_equal, fill=0.0, base=-BLKS,
                                           pattern=[[0, P]], channel_multiplier=1).then_inc(picked, 1)
                        pool.wait_ge(picked, 2)
                    pool.wait_ge(summed, 1)
                    pool.iota(v["scan"], pattern=[[1, COLS]], base=0, channel_multiplier=0,
                              allow_small_or_imprecise_dtypes=True).then_inc(placed, 1)
                    if scatter_of:
                        scatter(pool, *scatter_of)

        scatter_rec = sb("scatter_rec", [P, SR, SU * REC])
        scatter_slot = sb("scatter_slot", [P, SR, SU], I32)

        def scatter(pool, tag, home, table):
            v = sort_views(home)
            staged, passed = sem(f"{tag}_staged"), sem(f"{tag}_passed")
            sent = [sem(f"{tag}_sent{r}") for r in range(SR)]
            record = home[:, 0:COLS * REC]
            target = table[:, :].rearrange("p (t w) -> (p t) w", w=REC)

            def step(s, r):
                if past(s, SR):
                    pool.wait_ge(sent[r], ((s - r) // SR) * (16 * SU) if isinstance(s, int)
                                 else (s - r) * (16 * SU // SR))
                pool.tensor_copy(scatter_rec[:, r, :], record[:, bass.ds(s * (SU * REC), SU * REC)])
                pool.tensor_copy(scatter_slot[:, r, :], v["slot"][:, bass.ds(s * SU, SU)]).then_inc(staged, 1)
                pool.wait_ge(staged, s + 1)
                hold_wait(pool, passed)
                for k in range(SU):
                    pool.indirect_dma_start(
                        out=target, out_offset=bass.IndirectOffsetOnAxis(ap=scatter_slot[:, r, k:k + 1], axis=0),
                        in_=scatter_rec[:, r, k * REC:(k + 1) * REC], in_offset=None).then_inc(sent[r], 16)

            steps(pool, COLS // SU, SR, 0, step)
            for r in range(SR):
                pool.wait_ge(sent[r], 16 * SU * (COLS // SU // SR))

        def load_sorted(tag, table, order, extra=None, with_loops=False):
            got, split = sem(f"{tag}_got"), sem(f"{tag}_split")
            raw = slab_b[:, 0:TILES * REC]
            words = raw.rearrange("p (t w) -> p t w", w=REC)
            with nc.Block() as block:
                @block.sync
                def _(sp):
                    sp.dma_start(raw, table[:, :]).then_inc(got, 16)

                @block.vector
                def _(dve):
                    dve.wait_ge(got, 16)
                    dve.tensor_copy(order["idx"][:, :], words[:, :, 0])
                    dve.tensor_copy(order["lo"][:, :], words[:, :, 1])
                    if with_loops:
                        dve.tensor_copy(order["noloop"][:, :], words[:, :, 2])
                        dve.tensor_copy(order["edge"][:, :], words[:, :, 3])

                if extra:
                    extra(block)

        def load_weights():
            got, multiplied = sem("w_got"), sem("w_multiplied")
            w0 = slab_a[:, 0:128]
            w1t = slab_a[:, 128:256]
            a01 = slab_a[:, 256:260]
            cols = slab_a[:, 260:264]
            wct = slab_a[:, 512:896].rearrange("p (n f) -> p n f", f=D)
            top = slab_a[:, 896:1280].rearrange("p (n f) -> p n f", f=D)
            filled = sem("w_filled")
            with ExitStack() as local, nc.Block() as block:
                ps = [local.enter_context(nc.psum_tensor(f"w_ps{i}", [P, 512], F32)) for i in range(5)]
                loads = [(w0, io["w0"]), (w1t, io["watt_t"]), (a01[:, 0:2], io["a0"]), (a01[:, 2:4], io["a1"]),
                         (weights["l0"][:, 0:D], io["w0_t"]), (weights["l1"][:, 0:D], io["w1"]),
                         (weights["l1w2"][:, :], io["w2"]), (weights["pre"][:, :], io["wpre"]),
                         (cols[:, 0:1], io["batt"]), (cols[:, 1:4], io["bconv_t"])]
                for n in range(3):
                    loads += [(wct[:, n, :], io["wconv_t"][n]), (top[:, n, :], io["wupd"][n, 0:D, :]),
                              (weights[f"own{n}"][:, :], io["wupd"][n, D:2 * D, :]),
                              (biases[f"u{n}"][:, :], io["bupd"][n:n + 1, :].to_broadcast([P, D]))]
                for i, name in enumerate(("td", "ts", "edge")):
                    loads += [(weights[name][:, 0:D], io["wf"][i * D:(i + 1) * D, :]),
                              (weights[name][:, D:2 * D], io["ws"][i * D:(i + 1) * D, :])]
                loads += [(biases["l1"][:, 0:D], io["b1"].to_broadcast([P, D])),
                          (biases["l1w2"][:, :], io["b2"].to_broadcast([P, D])),
                          (biases["pre"][:, :], io["bpre"].to_broadcast([P, D])),
                          (biases["td"][:, 0:D], io["bf"].to_broadcast([P, D])),
                          (biases["td"][:, D:2 * D], io["bs"].to_broadcast([P, D]))]

                @block.sync
                def _(sp):
                    for dst, src in loads:
                        sp.dma_start(dst, src).then_inc(got, 16)

                @block.tensor
                def _(pe):
                    pe.wait_ge(got, 16 * len(loads))
                    pe.matmul(ps[0][:, 0:2], w0, a01[:, 0:2], start=True, stop=True)
                    pe.matmul(ps[1][:, 0:2], w1t, a01[:, 2:4], start=True, stop=True)
                    pe.matmul(ps[1][:, 2:4], cols[:, 0:1].to_broadcast([P, P]), a01[:, 2:4], start=True, stop=True)
                    for n in range(3):
                        pe.matmul(ps[2 + n][:, 0:D], wct[:, n, :], top[:, n, :], start=True, stop=True)
                        last = pe.matmul(ps[2 + n][:, D:2 * D], cols[:, 1 + n:2 + n].to_broadcast([P, P]),
                                         top[:, n, :], start=True, stop=True)
                    last.then_inc(multiplied, 1)

                @block.vector
                def _(dve):
                    dve.memset(biases["l0"][:, :], 0.0).then_inc(filled, 1)
                    dve.memset(weights["l0"][:, D:D + 1], 0.0)
                    dve.memset(weights["l1"][:, D:D + 1], 0.0)
                    dve.memset(biases["l1"][:, D:D + 1], 1.0)
                    dve.wait_ge(filled, 1)
                    dve.memset(biases["l0"][:, D:D + 1], 1.0)
                    dve.wait_ge(multiplied, 1)
                    dve.tensor_copy(weights["l0"][:, D + 1:W_ATT], ps[0][:, 0:2])
                    dve.tensor_copy(weights["l1"][:, D + 1:W_ATT], ps[1][:, 0:2])
                    dve.tensor_copy(biases["l1"][:, D + 1:W_ATT], ps[1][:, 2:4])
                    for n in range(3):
                        dve.tensor_copy(weights[f"agg{n}"][:, :], ps[2 + n][:, 0:D])
                        dve.tensor_tensor(biases[f"u{n}"][:, :], ps[2 + n][:, D:2 * D], biases[f"u{n}"][:, :],
                                          ALU.add)

        def norm(tag):
            chain, rooted = sem(f"{tag}_chain"), sem(f"{tag}_rooted")
            sq = blocks(slab_b)
            mean, var, std, inv = (stats[:, i, :] for i in range(4))
            wide = lambda a: a.unsqueeze(2).to_broadcast([P, NB, D])
            with nc.Block() as block:
                @block.vector
                def _(dve):
                    count = [0]

                    def link(ins):
                        count[0] += 1
                        ins.then_inc(chain, 1)
                        dve.wait_ge(chain, count[0])

                    link(dve.tensor_reduce(mean, x_v, AX.X, ALU.add))
                    link(dve.tensor_scalar(mean, mean, 1.0 / D, None, ALU.mult))
                    link(dve.tensor_tensor(h_v, x_v, wide(mean), ALU.subtract))
                    link(dve.tensor_tensor(sq, h_v, h_v, ALU.mult))
                    link(dve.tensor_reduce(var, sq, AX.X, ALU.add))
                    link(dve.tensor_scalar(var, var, 1.0 / D, 1e-5, ALU.mult, ALU.add))
                    dve.wait_ge(rooted, 1)
                    link(dve.reciprocal(inv, std))
                    link(dve.tensor_tensor(h_v, h_v, wide(inv), ALU.mult))
                    link(dve.tensor_scalar(h_v, h_v, 0.0, None, ALU.max))

                @block.scalar
                def _(act):
                    act.wait_ge(chain, 6)
                    act.activation(std, var, ACT.Sqrt).then_inc(rooted, 1)

        def dense(tag, sources, mats, bias, width, target=None, target2=None, table=None, relu=False):
            staged, turned, copied = sem(f"{tag}_staged"), sem(f"{tag}_turned"), sem(f"{tag}_copied")
            produced, evacuated, added = sem(f"{tag}_produced"), sem(f"{tag}_evacuated"), sem(f"{tag}_added")
            stored = [sem(f"{tag}_stored{r}") for r in range(2)]
            ns = len(sources)
            stage = [rows[:, r * 512:r * 512 + ns * DB * D].rearrange("p (i u f) -> p i u f", i=ns, u=DB)
                     for r in range(2)]
            tsb = [rows[:, 1024 + r * 512:1024 + r * 512 + ns * DB * D].rearrange("p (i f) -> p i f", f=P)
                   for r in range(2)]
            oring = [rows[:, 2048 + r * 512:2048 + r * 512 + DB * width].rearrange("p (u f) -> p u f", u=DB)
                     for r in range(2)]
            with ExitStack() as local, nc.Block() as block:
                tp = [local.enter_context(nc.psum_tensor(f"{tag}_tp{r}", [P, 4, P], F32)) for r in range(2)]
                op = [local.enter_context(nc.psum_tensor(f"{tag}_op{r}", [P, DB, 256], F32)) for r in range(2)]

                @block.scalar
                def _(act):
                    def step(s, r):
                        if within(s, DBATCHES):
                            if past(s, 2):
                                act.wait_ge(turned, s - 1)
                            for i, src in enumerate(sources):
                                last = act.activation(stage[r][:, i, :, :], src[:, bass.ds(s * DB, DB), :], ACT.Copy)
                            last.then_inc(staged, 1)
                        if past(s, 1):
                            q = s - 1
                            act.wait_ge(turned, q + 1)
                            if past(s, 3):
                                act.wait_ge(produced, q - 1)
                            act.activation(tsb[1 - r], tp[1 - r][:, 0:ns * DB, :], ACT.Copy).then_inc(copied, 1)

                    steps(act, DBATCHES, 2, 1, step)

                @block.tensor
                def _(pe):
                    def step(s, r):
                        if within(s, DBATCHES):
                            pe.wait_ge(staged, s + 1)
                            if past(s, 2):
                                pe.wait_ge(copied, s - 1)
                            for i in range(ns):
                                for u in range(DB):
                                    last = pe.transpose(tp[r][:, i * DB + u, :], stage[r][:, i, u, :], ident[:])
                            last.then_inc(turned, 1)
                        if past(s, 1):
                            q = s - 1
                            pe.wait_ge(copied, q + 1)
                            if past(s, 3):
                                pe.wait_ge(evacuated, q - 1)
                            for u in range(DB):
                                for i in range(ns):
                                    last = pe.matmul(op[1 - r][:, u, 0:width], tsb[1 - r][:, i * DB + u, :],
                                                     mats[i][:, :], start=(i == 0), stop=(i == ns - 1))
                            last.then_inc(produced, 1)

                    steps(pe, DBATCHES, 2, 1, step)

                @block.vector
                def _(dve):
                    def step(q, r):
                        dve.wait_ge(produced, q + 1)
                        if target is None and past(q, 2):
                            dve.wait_ge(stored[r], (q - r) * 8)
                        halves = ([(oring[r], 0, width)] if target is None else
                                  [(target[:, bass.ds(q * DB, DB), :], 0, width)] if target2 is None else
                                  [(t[:, bass.ds(q * DB, DB), :], i * D, D) for i, t in enumerate((target, target2))])
                        for dst, at, w in halves:
                            if bias is None:
                                last = dve.tensor_copy(dst, op[r][:, :, at:at + w])
                            else:
                                last = dve.tensor_tensor(dst, op[r][:, :, at:at + w],
                                                         bias[:, at:at + w].unsqueeze(1).to_broadcast([P, DB, w]),
                                                         ALU.add)
                        if relu:
                            last.then_inc(added, 1)
                            dve.wait_ge(added, q + 1)
                            last = dve.tensor_scalar(halves[0][0], halves[0][0], 0.0, None, ALU.max)
                        last.then_inc(evacuated, 1)

                    steps(dve, DBATCHES, 2, 0, step)

                if table is not None:
                    trows = table.rearrange("(b p) f -> p b f", p=P)

                    @block.sync
                    def _(sp):
                        def step(q, r):
                            sp.wait_ge(evacuated, q + 1)
                            src = oring[r] if target is None else target[:, bass.ds(q * DB, DB), :]
                            sp.dma_start(trows[:, bass.ds(q * DB, DB), :], src).then_inc(stored[r], 16)

                        steps(sp, DBATCHES, 2, 0, step)
                        for r in range(2):
                            sp.wait_ge(stored[r], 16 * (DBATCHES // 2))

        def gathers(pool, tag, sources, freed):
            staged, passed = sem(f"{tag}_staged"), sem(f"{tag}_passed")
            got = [sem(f"{tag}_got{r}") for r in range(RING)]

            def step(s, r):
                if past(s, RING):
                    pool.wait_ge(freed, s - (RING - 1))
                for table, idx, stage, ring in sources:
                    last = pool.tensor_copy(stage[:, r, :], idx[:, bass.ds(s * U, U)])
                last.then_inc(staged, 1)
                pool.wait_ge(staged, s + 1)
                hold_wait(pool, passed)
                for k in range(U):
                    for table, idx, stage, ring in sources:
                        pool.indirect_dma_start(
                            out=ring[:, r, k, :], out_offset=None, in_=table,
                            in_offset=bass.IndirectOffsetOnAxis(ap=stage[:, r, k:k + 1], axis=0)).then_inc(got[r], 16)

            return got, lambda: steps(pool, BATCHES, RING, 0, step)

        def arrived(eng, got, s, r, per):
            eng.wait_ge(got[r], (s // RING + 1) * per if isinstance(s, int) else (s - r) * (per // RING) + per)

        def attention(tag, table, order, own, sums, floor_at_zero, maxima=None):
            mask_ready, scored, leaky = sem(f"{tag}_mask"), sem(f"{tag}_scored"), sem(f"{tag}_leaky")
            positive, passed = sem(f"{tag}_positive"), sem(f"{tag}_dve_passed")
            shift, chain, probs = sem(f"{tag}_shift"), sem(f"{tag}_chain"), sem(f"{tag}_probs")
            turned, copied, mixed = sem(f"{tag}_turned"), sem(f"{tag}_copied"), sem(f"{tag}_mixed")
            merged, cleared = sem(f"{tag}_merged"), sem(f"{tag}_cleared")
            ring = rows[:, 0:RING * U * W_ATT].rearrange("p (r k f) -> p r k f", r=RING, k=U)
            at = [0]

            def work(n):
                at[0] += n
                return slab_b[:, at[0] - n:at[0]]

            tiles4 = lambda a: a.rearrange("p (k e) -> p k e", k=U)
            mask = [tiles4(work(U * P // 2).bitcast(BF16)) for _ in range(2)]
            score = [tiles4(work(U * P)) for _ in range(2)]
            prob = [tiles4(work(U * P)) for _ in range(2)]
            prob_t = [tiles4(work(U * P)) for _ in range(2)]
            top = [work(U) for _ in range(2)]
            run = [work(U + 1) for _ in range(2)]
            drop = [work(U) for _ in range(2)]
            minus = [work(U) for _ in range(2)]
            decay = [work(U) for _ in range(2)]
            op0 = ALU.mult if floor_at_zero else ALU.add
            K = 4
            with ExitStack() as local, nc.Block() as block:
                xp = [local.enter_context(nc.psum_tensor(f"{tag}_x{r}", [P, U, P], F32)) for r in range(2)]
                tp = local.enter_context(nc.psum_tensor(f"{tag}_t", [P, U, P], F32))
                op = [local.enter_context(nc.psum_tensor(f"{tag}_o{r}", [P, U, 256], F32)) for r in range(2)]
                got = [None]

                @block.gpsimd
                def _(pool):
                    got[0], run_gathers = gathers(pool, tag, [(table, order["idx"], stage_idx, ring)], mixed)
                    run_gathers()

                @block.vector
                def _(dve):
                    dve.memset(sums, 0.0)
                    if maxima is not None:
                        dve.memset(maxima, FAR)
                    dve.memset(run[1], 0.0).then_inc(cleared, 1)
                    dve.wait_ge(cleared, 1)

                    def step(s, r):
                        r = r % 2
                        if within(s, BATCHES):
                            if past(s, 2):
                                dve.wait_ge(scored, s - 1)
                            for k in range(U):
                                last = dve.tensor_scalar(mask[r][:, k, :], lane_bf[:],
                                                         order["lo"][:, bass.ds(s * U + k, 1)], FAR,
                                                         ALU.not_equal, ALU.mult)
                            last.then_inc(mask_ready, 1)
                        if past(s, 1) and within(s, BATCHES + 1):
                            q, c = s - 1, 1 - r
                            same = order["same"][:, bass.ds(q * U, U)]

                            def link(ins, n):
                                ins.then_inc(chain, 1)
                                dve.wait_ge(chain, q * K + n)

                            dve.wait_ge(positive, q + 1)
                            if past(s, 3):
                                dve.wait_ge(merged, (q - 1) * U)
                            hold_wait(dve, passed)
                            for k in range(U):
                                last = dve.tensor_tensor_reduce(
                                    out=score[c][:, k, :], in0=xp[c][:, k, :], in1=score[c][:, k, :], scale=1.0,
                                    scalar=FLOOR, op0=ALU.add, op1=ALU.max, accum_out=top[c][:, k:k + 1])
                            last.then_inc(leaky, 1)
                            dve.wait_ge(leaky, q + 1)
                            link(dve.tensor_copy(run[c][:, 0:1], run[r][:, U:U + 1]), 1)
                            link(dve.tensor_tensor_scan(run[c][:, 1:U + 1], same, top[c], run[c][:, 0:1],
                                                        op0, ALU.max), 2)
                            link(dve.tensor_tensor(drop[c], run[c][:, 0:U], same, op0), 3)
                            link(dve.tensor_tensor(drop[c], drop[c], run[c][:, 1:U + 1], ALU.subtract), 4)
                            dve.tensor_scalar(minus[c], run[c][:, 1:U + 1], -(1.0 - SLOPE), None, ALU.mult
                                              ).then_inc(shift, 1)
                        if past(s, 2):
                            q = s - 2
                            block_of = block_registers(nc, dve, order["words"], q)
                            dve.wait_ge(mixed, q + 1)
                            for k in range(U):
                                if maxima is not None:
                                    dve.tensor_copy(maxima[:, bass.ds(block_of[k], 1)], run[r][:, k + 1:k + 2])
                                acc = sums[:, bass.ds(block_of[k], 1), :].rearrange("p b f -> p (b f)")
                                dve.scalar_tensor_tensor(acc, acc, decay[r][:, k:k + 1], op[r][:, k, 0:D + 1],
                                                         ALU.mult, ALU.add).then_inc(merged, 1)
                                dve.wait_ge(merged, q * U + k + 1)

                    steps(dve, BATCHES, RING, 2, step)

                @block.tensor
                def _(pe):
                    def step(s, r4):
                        r = r4 % 2
                        if within(s, BATCHES):
                            block_of = block_registers(nc, pe, order["words"], s)
                            pe.wait_ge(mask_ready, s + 1)
                            arrived(pe, got[0], s, r4, 16 * U)
                            if past(s, 2):
                                pe.wait_ge(leaky, s - 1)
                            for k in range(U):
                                pe.matmul(xp[r][:, k, :], mask[r][:, k, :], quarter_bf[:], start=True, stop=False)
                                pe.matmul(xp[r][:, k, :], ring[:, r4, k, D + 1:D + 2].to_broadcast([P, P]),
                                          quarter[:], start=False, stop=False)
                                last = pe.matmul(xp[r][:, k, :], quarter[:],
                                                 own[:, bass.ds(block_of[k], 1)].to_broadcast([P, P]),
                                                 start=False, stop=True)
                            last.then_inc(scored, 1)
                        if past(s, 1):
                            q, c = s - 1, 1 - r
                            pe.wait_ge(probs, q + 1)
                            if past(s, 2):
                                pe.wait_ge(copied, q)
                            for k in range(U):
                                last = pe.transpose(tp[:, k, :], prob[c][:, k, :], ident[:])
                            last.then_inc(turned, 1)
                            pe.wait_ge(copied, q + 1)
                            if past(s, 3):
                                pe.wait_ge(merged, (q - 1) * U)
                            for k in range(U):
                                last = pe.matmul(op[c][:, k, 0:D + 1], prob_t[c][:, k, :],
                                                 ring[:, (r4 - 1) % RING, k, 0:D + 1], start=True, stop=True)
                            last.then_inc(mixed, 1)

                    steps(pe, BATCHES, RING, 1, step)

                @block.scalar
                def _(act):
                    def step(s, r):
                        r = r % 2
                        if within(s, BATCHES):
                            act.wait_ge(scored, s + 1)
                            if past(s, 2):
                                act.wait_ge(probs, s - 1)
                            act.activation(score[r], xp[r][:], ACT.Relu, scale=4.0).then_inc(positive, 1)
                        if past(s, 1):
                            q, c = s - 1, 1 - r
                            act.wait_ge(shift, q + 1)
                            if past(s, 3):
                                act.wait_ge(turned, q - 1)
                                act.wait_ge(merged, (q - 1) * U)
                            act.activation(decay[c], drop[c], ACT.Exp, scale=1.0 - SLOPE)
                            for k in range(U):
                                last = act.activation(prob[c][:, k, :], score[c][:, k, :], ACT.Exp,
                                                      bias=minus[c][:, k:k + 1], scale=1.0 - SLOPE)
                            last.then_inc(probs, 1)
                            act.wait_ge(turned, q + 1)
                            if past(s, 3):
                                act.wait_ge(mixed, q - 1)
                            act.activation(prob_t[c], tp[:], ACT.Copy).then_inc(copied, 1)

                    steps(act, BATCHES, RING, 1, step)

        def spread(tag, table, sums):
            hot_ready, mixed, merged, cleared = (sem(f"{tag}_{n}") for n in ("hot", "mixed", "merged", "cleared"))
            ring = rows[:, 0:RING * U * D].rearrange("p (r k f) -> p r k f", r=RING, k=U)
            hot = [rows2[:, r * U * P:(r + 1) * U * P].rearrange("p (k e) -> p k e", k=U) for r in range(2)]
            with ExitStack() as local, nc.Block() as block:
                op = [local.enter_context(nc.psum_tensor(f"{tag}_o{r}", [P, U, D], F32)) for r in range(2)]
                got = [None]

                @block.gpsimd
                def _(pool):
                    got[0], run_gathers = gathers(pool, tag, [(table, by_dst["idx"], stage_idx, ring)], mixed)
                    run_gathers()

                @block.vector
                def _(dve):
                    dve.memset(sums, 0.0).then_inc(cleared, 1)
                    dve.wait_ge(cleared, 1)

                    def step(s, r):
                        r = r % 2
                        if within(s, BATCHES):
                            if past(s, 2):
                                dve.wait_ge(mixed, s - 1)
                            for k in range(U):
                                last = dve.tensor_scalar(hot[r][:, k, :], lane[:],
                                                         by_dst["noloop"][:, bass.ds(s * U + k, 1)], None,
                                                         ALU.is_equal)
                            last.then_inc(hot_ready, 1)
                        if past(s, 1):
                            q, c = s - 1, 1 - r
                            block_of = block_registers(nc, dve, by_dst["words"], q)
                            dve.wait_ge(mixed, q + 1)
                            for k in range(U):
                                acc = sums[:, bass.ds(block_of[k], 1), :].rearrange("p b f -> p (b f)")
                                dve.tensor_tensor(acc, acc, op[c][:, k, :], ALU.add).then_inc(merged, 1)
                                dve.wait_ge(merged, q * U + k + 1)

                    steps(dve, BATCHES, RING, 1, step)

                @block.tensor
                def _(pe):
                    def step(s, r4):
                        r = r4 % 2
                        pe.wait_ge(hot_ready, s + 1)
                        arrived(pe, got[0], s, r4, 16 * U)
                        if past(s, 2):
                            pe.wait_ge(merged, (s - 1) * U)
                        for k in range(U):
                            last = pe.matmul(op[r][:, k, :], hot[r][:, k, :], ring[:, r4, k, :], start=True, stop=True)
                        last.then_inc(mixed, 1)

                    steps(pe, BATCHES, RING, 0, step)

        def gated(tag, table, edge_rows, own_gate, own_core, sums):
            hot_ready, turned, copied, joined = (sem(f"{tag}_{n}") for n in ("hot", "turned", "copied", "joined"))
            logged, split, gate_ready, sent = (sem(f"{tag}_{n}") for n in ("logged", "split", "gate", "sent"))
            mixed, merged, cleared, chain = (sem(f"{tag}_{n}") for n in ("mixed", "merged", "cleared", "chain"))
            ring = rows[:, :].rearrange("p (r k f) -> p r k f", r=RING, k=U)
            ering = rows2[:, :].rearrange("p (r k f) -> p r k f", r=RING, k=U)
            home = slab_h
            pos = [0]

            def work(n):
                pos[0] += n
                assert pos[0] <= SLAB
                return home[:, pos[0] - n:pos[0]]

            tiles4 = lambda a: a.rearrange("p (k e) -> p k e", k=U)
            hot = [tiles4(work(512)) for _ in range(4)]
            hot_t = tiles4(work(512))
            edge_t = tiles4(work(512))
            soft = [tiles4(work(1024)) for _ in range(2)]
            gate = [a[:, :, 0:D] for a in soft]
            core = [a[:, :, D:2 * D] for a in soft]
            with ExitStack() as local, nc.Block() as block:
                tp = [local.enter_context(nc.psum_tensor(f"{tag}_t{r}", [P, U, P], F32)) for r in range(2)]
                zp = [local.enter_context(nc.psum_tensor(f"{tag}_z{r}", [P, U, 2 * D], F32)) for r in range(2)]
                op = [local.enter_context(nc.psum_tensor(f"{tag}_o{r}", [P, U, D], F32)) for r in range(2)]
                got = [None]

                @block.gpsimd
                def _(pool):
                    got[0], run_gathers = gathers(
                        pool, tag, [(table, by_dst["idx"], stage_idx, ring),
                                    (edge_rows, by_dst["edge"], stage_edge, ering)], joined)
                    run_gathers()

                @block.vector
                def _(dve):
                    dve.memset(sums, 0.0).then_inc(cleared, 1)
                    dve.wait_ge(cleared, 1)

                    def step(s, r4):
                        r = r4 % 2
                        if within(s, BATCHES):
                            if past(s, 4):
                                dve.wait_ge(mixed, s - 3)
                            for k in range(U):
                                last = dve.tensor_scalar(hot[r4][:, k, :], lane[:],
                                                         by_dst["lo"][:, bass.ds(s * U + k, 1)], None, ALU.is_equal)
                            last.then_inc(hot_ready, 1)
                        if past(s, 1) and within(s, BATCHES + 1):
                            q, c = s - 1, 1 - r
                            dve.wait_ge(logged, q + 1)
                            dve.scalar_tensor_tensor(gate[c], zp[c][:, :, 0:D], 0.0, soft[c][:, :, 0:D],
                                                     ALU.min, ALU.subtract)
                            dve.scalar_tensor_tensor(core[c], zp[c][:, :, D:2 * D], 0.0, soft[c][:, :, D:2 * D],
                                                     ALU.max, ALU.add).then_inc(split, 1)
                        if past(s, 2) and within(s, BATCHES + 2):
                            q = s - 2
                            dve.wait_ge(gate_ready, q + 1)
                            dve.wait_ge(split, q + 1)
                            dve.tensor_tensor(core[r], core[r], gate[r], ALU.mult).then_inc(sent, 1)
                        if past(s, 3):
                            q, c = s - 3, 1 - r
                            block_of = block_registers(nc, dve, by_dst["words"], q)
                            dve.wait_ge(mixed, q + 1)
                            for k in range(U):
                                acc = sums[:, bass.ds(block_of[k], 1), :].rearrange("p b f -> p (b f)")
                                dve.tensor_tensor(acc, acc, op[c][:, k, :], ALU.add).then_inc(merged, 1)
                                dve.wait_ge(merged, q * U + k + 1)

                    steps(dve, BATCHES, RING, 3, step)

                @block.tensor
                def _(pe):
                    def step(s, r4):
                        r = r4 % 2
                        if within(s, BATCHES):
                            pe.wait_ge(hot_ready, s + 1)
                            arrived(pe, got[0], s, r4, 2 * 16 * U)
                            if past(s, 1):
                                pe.wait_ge(copied, s)
                            for k in range(U):
                                pe.transpose(tp[0][:, k, :], hot[r4][:, k, :], ident[:])
                                last = pe.transpose(tp[1][:, k, :], ering[:, r4, k, :], ident[:])
                            last.then_inc(turned, 1)
                        if past(s, 2):
                            q = s - 2
                            pe.wait_ge(sent, q + 1)
                            if past(s, 4):
                                pe.wait_ge(merged, (q - 1) * U)
                            for k in range(U):
                                last = pe.matmul(op[r][:, k, :], hot[(r4 + 2) % 4][:, k, :], core[r][:, k, :],
                                                 start=True, stop=True)
                            last.then_inc(mixed, 1)
                        if within(s, BATCHES):
                            block_of = block_registers(nc, pe, by_dst["words"], s)
                            pe.wait_ge(copied, s + 1)
                            if past(s, 2):
                                pe.wait_ge(split, s - 1)
                            for k in range(U):
                                z = zp[r][:, k, :]
                                pe.matmul(z, edge_t[:, k, :], weights["edge"][:, :], start=True, stop=False)
                                pe.matmul(z, ident[:], ring[:, r4, k, :], start=False, stop=False)
                                for half, own in ((0, own_gate), (D, own_core)):
                                    last = pe.matmul(
                                        zp[r][:, k, half:half + D], hot_t[:, k, :],
                                        own[:, bass.ds(block_of[k], 1), :].rearrange("p b f -> p (b f)"),
                                        start=False, stop=(half > 0))
                            last.then_inc(joined, 1)

                    steps(pe, BATCHES, RING, 2, step)

                @block.scalar
                def _(act):
                    def step(s, r4):
                        r = r4 % 2
                        if within(s, BATCHES):
                            act.wait_ge(turned, s + 1)
                            if past(s, 1):
                                act.wait_ge(joined, s)
                            act.activation(hot_t, tp[0][:], ACT.Copy)
                            act.activation(edge_t, tp[1][:], ACT.Copy).then_inc(copied, 1)
                        if past(s, 2) and within(s, BATCHES + 2):
                            q = s - 2
                            act.wait_ge(split, q + 1)
                            act.activation(gate[r], gate[r], ACT.Exp).then_inc(gate_ready, 1)
                        if past(s, 1) and within(s, BATCHES + 1):
                            q, c = s - 1, 1 - r
                            act.wait_ge(joined, q + 1)
                            if past(s, 3):
                                act.wait_ge(mixed, q - 1)
                            act.activation(soft[c], zp[c][:], ACT.Abs).then_inc(chain, 1)
                            act.wait_ge(chain, q * 2 + 1)
                            act.activation(soft[c], soft[c], ACT.Exp, scale=-1.0).then_inc(chain, 1)
                            act.wait_ge(chain, q * 2 + 2)
                            act.activation(soft[c], soft[c], ACT.Ln, bias=1.0).then_inc(logged, 1)

                    steps(act, BATCHES, RING, 2, step)

        def by_node(tag, program, pool_program=None, act_program=None):
            chain = sem(f"{tag}_chain")
            with nc.Block() as block:
                @block.vector
                def _(dve):
                    count = [0]

                    def link(ins):
                        count[0] += 1
                        ins.then_inc(chain, 1)
                        dve.wait_ge(chain, count[0])

                    program(dve, link)
                if pool_program:
                    block.gpsimd(pool_program)
                if act_program:
                    block.scalar(act_program)

        live = lambda v: v[:, 0:BLKS, :]
        sums1 = slab_acc[:, 0:BLKS * (D + 1)].rearrange("p (b f) -> p b f", f=D + 1)
        message, weight = sums1[:, :, 0:D], sums1[:, :, D]
        own = sb("own", [P, BLKS])
        maxima = sb("maxima", [P, BLKS])
        node = sb("node", [P, 4, BLKS])
        spread_out = lambda a: a.unsqueeze(2).to_broadcast([P, BLKS, D])

        def own_scores(tag, table_sb):
            by_node(tag, lambda dve, link: link(dve.tensor_copy(own[:], table_sb[:, 0:BLKS, D + 2])))

        constants()
        place_edges("ps", io["src"], io["dst"], slab_acc, sorted_src, by_src, False)
        place_edges("pd", io["dst"], io["src"], slab_a, sorted_dst, by_dst, True,
                    scatter_of=("ss", slab_acc, sorted_src))
        load_sorted("ls", sorted_src, by_src, extra=lambda block: block.gpsimd(
            lambda pool: scatter(pool, "sd", slab_a, sorted_dst)))
        load_sorted("ld", sorted_dst, by_dst, with_loops=True)
        load_weights()

        release()

        att = blocks(slab_a, W_ATT)
        norm("n0")
        dense("d0", [h_v], [weights["l0"]], biases["l0"], W_ATT, target=att, table=tab0)
        own_scores("o0", att)
        attention("a0", tab0, by_src, own, sums1, True)

        def finish0(dve, link):
            link(dve.tensor_scalar(node[:, 0, :], weight, 0.0, None, ALU.is_equal))
            link(dve.tensor_tensor(node[:, 1, :], weight, node[:, 0, :], ALU.add))
            link(dve.reciprocal(node[:, 2, :], node[:, 1, :]))
            link(dve.tensor_tensor(message, message, spread_out(node[:, 2, :]), ALU.mult))
            link(dve.tensor_tensor(live(x_v), live(x_v), message, ALU.add))

        by_node("f0", finish0)

        release()

        norm("n1")
        dense("d1", [h_v], [weights["l1"]], biases["l1"], W_ATT, target=att, table=tab1)
        own_scores("o1", att)
        attention("a1", tab1, by_dst, own, sums1, False, maxima=maxima[:, :])

        topped, overall, scaled = sem("topped"), sem("overall"), sem("scaled")
        prod = blocks(slab_a)

        def finish1(dve, link):
            dve.tensor_reduce(node[:, 0, 0:1], maxima[:], AX.X, ALU.max).then_inc(topped, 1)
            dve.wait_ge(overall, 1)
            link(dve.tensor_scalar(node[:, 1, :], maxima[:], node[:, 0, 1:2], None, ALU.subtract))
            dve.wait_ge(scaled, 1)
            link(dve.tensor_tensor(node[:, 3, :], weight, node[:, 2, :], ALU.mult))
            link(dve.tensor_scalar(node[:, 3, :], node[:, 3, :], 1e-9, None, ALU.add))
            link(dve.reciprocal(node[:, 3, :], node[:, 3, :]))
            link(dve.tensor_tensor(node[:, 3, :], node[:, 3, :], node[:, 2, :], ALU.mult))
            link(dve.tensor_tensor(message, message, spread_out(node[:, 3, :]), ALU.mult))
            link(dve.memset(prod, 0.0))
            link(dve.tensor_tensor(live(prod), live(h_v), message, ALU.mult))

        def overall_max(pool):
            pool.wait_ge(topped, 1)
            pool.partition_all_reduce(node[:, 0, 1:2], node[:, 0, 0:1], P, RMAX).then_inc(overall, 1)

        def exp_scale(act):
            act.wait_ge(overall, 1)
            act.wait_ge(chain_of_f1[0], 1)
            act.activation(node[:, 2, :], node[:, 1, :], ACT.Exp, scale=1.0 - SLOPE).then_inc(scaled, 1)

        chain_of_f1 = [None]
        diff = sem("diff")

        def finish1_wrapped(dve, link):
            first = [True]

            def link1(ins):
                if first[0]:
                    first[0] = False
                    ins.then_inc(diff, 1)
                    return
                link(ins)

            finish1(dve, link1)

        chain_of_f1[0] = diff
        by_node("f1", finish1_wrapped, pool_program=overall_max, act_program=exp_scale)
        prod_w = blocks(slab_b)
        dense("d1b", [prod], [weights["l1w2"]], biases["l1w2"], D, target=prod_w)

        def finish1b(dve, link):
            link(dve.tensor_tensor(message, message, live(h_v), ALU.add))
            link(dve.tensor_tensor(message, message, live(prod_w), ALU.add))
            link(dve.scalar_tensor_tensor(message, message, SLOPE, message, ALU.mult, ALU.max))
            link(dve.tensor_tensor(live(x_v), live(x_v), message, ALU.add))

        by_node("f1b", finish1b)

        release()

        norm("n2")
        state = blocks(slab_a)
        sums2 = blocks(slab_acc)
        dense("d2", [h_v], [weights["pre"]], biases["pre"], D, target=state, table=tab2[0])
        for n in range(3):
            spread(f"r{n}", tab2[n], sums2)
            dense(f"u{n}", [sums2, state], [weights[f"agg{n}"], weights[f"own{n}"]], biases[f"u{n}"], D,
                  target=state, table=tab2[n + 1] if n < 2 else None, relu=True)
        by_node("f2", lambda dve, link: link(dve.tensor_tensor(x_v, x_v, state, ALU.add)))

        release()

        norm("n3")
        dense("d3s", [h_v], [weights["ts"]], None, 2 * D, table=tab3)
        own_gate, own_core = blocks(slab_a), blocks(slab_b)
        dense("d3d", [h_v], [weights["td"]], biases["td"], 2 * D, target=own_gate, target2=own_core)
        by_node("f3", lambda dve, link: link(dve.tensor_tensor(x_v, x_v, h_v, ALU.add)))
        gated("g3", tab3, io["edge"], own_gate, own_core, sums2)

        written, summed3 = sem("written"), sem("summed3")
        with nc.Block() as block:
            @block.vector
            def _(dve):
                dve.tensor_tensor(x_v, x_v, sums2, ALU.add).then_inc(summed3, 1)

            @block.sync
            def _(sp):
                sp.wait_ge(summed3, 1)
                sp.dma_start(out[0:(BLKS - 1) * P, :].rearrange("(b p) f -> p b f", p=P),
                             x_v[:, 0:BLKS - 1, :]).then_inc(written, 16)
                sp.dma_start(out[(BLKS - 1) * P:N, :], x_v[0:TAIL, BLKS - 1, :]).then_inc(written, 16)
                sp.wait_ge(written, 32)


def lay_out(inputs):
    import numpy as np
    c = np.ascontiguousarray
    i = {k: np.asarray(v) for k, v in inputs.items()}
    return {
        "x": c(i["x"]), "src": c(i["src"]), "dst": c(i["dst"]), "edge": c(i["edge_attr_128"]),
        "w0": c(i["L0_gnn_W"]), "w0_t": c(i["L0_gnn_W"].T),
        "a0": c(i["L0_gnn_a"].reshape(2, D)[::-1].T), "a1": c(i["L1_gnn_a"].reshape(2, D).T),
        "watt_t": c(i["L1_gnn_Watt_w"].T), "batt": c(i["L1_gnn_Watt_b"].reshape(D, 1)),
        "w1": c(i["L1_gnn_W1_w"]), "b1": c(i["L1_gnn_W1_b"].reshape(1, D)),
        "w2": c(i["L1_gnn_W2_w"]), "b2": c(i["L1_gnn_W2_b"].reshape(1, D)),
        "wpre": c(i["L2_gnn_W_pre"]), "bpre": c(i["L2_gnn_b_pre"].reshape(1, D)),
        "wconv_t": c(i["L2_gnn_W_conv"].transpose(0, 2, 1)), "bconv_t": c(i["L2_gnn_b_conv"].T),
        "wupd": c(i["L2_gnn_W_upd"]), "bupd": c(i["L2_gnn_b_upd"]),
        "wf": c(i["L3_gnn_W_f"]), "bf": c(i["L3_gnn_b_f"].reshape(1, D)),
        "ws": c(i["L3_gnn_W_s"]), "bs": c(i["L3_gnn_b_s"].reshape(1, D)),
    }


def kernel(**inputs):
    import concourse.bacc as bacc
    from concourse.bass_utils import run_bass_kernel_spmd

    nc = bacc.Bacc("TRN2", target_bir_lowering=False, num_devices=1)
    arrays, io = {}, {}
    for name, a in lay_out(inputs).items():
        arrays[f"in_{name}"] = a
        io[name] = nc.dram_tensor(f"in_{name}", a.shape, mybir.dt.from_np(a.dtype), kind="ExternalInput").ap()
    out = nc.dram_tensor("out", (N, D), F32, kind="ExternalOutput").ap()
    gnn(nc, io, out)
    r = run_bass_kernel_spmd(nc, [arrays], core_ids=[0])
    return r.results[0]["out"]
```

```python
from contextlib import ExitStack

import concourse.bass as bass
from concourse import mybir

F32 = mybir.dt.float32
BF16 = mybir.dt.bfloat16
I32 = mybir.dt.int32
ALU = mybir.AluOpType
ACT = mybir.ActivationFunctionType
AX = mybir.AxisListType
RMAX = bass.bass_isa.ReduceOp.max

P = 128
N = 6250
E = 106250
D = 128
BLKS = -(-N // P)
TAIL = N - (BLKS - 1) * P
NB = BLKS + 3
BUCKETS = BLKS + 1
COLS = 832
LASTROW = E - (P - 1) * COLS
PADS = P * COLS - E
PADKEY = BLKS * P
U = 4
RING = 4
ARING = 10
TILES = 880
BATCHES = TILES // U
assert (E + BLKS * (P - 1)) // P + -(-PADS // P) <= TILES and BATCHES % RING == BATCHES % ARING == 0
REC = 4
FAR = -1.0e30
FLOOR = -1.0e28
SLOPE = 0.2
SU = 8
SR = 4
SLAB = NB * 131 + 36
W_ATT = 131
DB = 2
DBATCHES = NB // DB


def steps(eng, count, ring, lag, step, load=None):
    def peeled(s):
        if load is None:
            step(s, s % ring)
        else:
            step(s, s % ring, load.words(s, 1)[0] if load.lag <= s < count + load.lag else None)

    for s in range(ring):
        peeled(s)
    with eng.Fori(1, count // ring) as i:
        words = load.words(i * ring, ring) if load else None
        for r in range(ring):
            step(i * ring + r, r, *([words[r]] if load else []))
    for s in range(count, count + lag):
        peeled(s)


class BlockWords:

    def __init__(self, nc, eng, table, lag):
        self.nc, self.eng, self.table, self.lag = nc, eng, table, lag

    def words(self, s, n):
        return self.nc.values_load_multi_w_load_instructions(
            self.table[0:1, bass.ds(s - self.lag, n)], engines=[self.eng.engine], min_val=0, max_val=0x3F3F3F3F,
            skip_runtime_bounds_check_because="a word holds four numbers below 64")[1]

    def blocks(self, word):
        return [self.nc.s_assert_within(
            self.eng.snap((word >> (8 * k)) & 63), 0, BLKS - 1,
            skip_runtime_bounds_check_because="a tile's block is counted over BLKS - 1 blocks") for k in range(U)]


def past(s, lag):
    return not isinstance(s, int) or s >= lag


def within(s, count):
    return not isinstance(s, int) or s < count


def hold_wait(eng, passed):
    eng.sem_inc(passed, 1)


def gnn(nc, io, out):
    with ExitStack() as ctx:
        def sb(name, shape, dt=F32):
            return ctx.enter_context(nc.sbuf_tensor(name, shape, dt))

        def dram(name, shape, dt=F32):
            return nc.dram_tensor(name, shape, dt, kind="Internal").ap()

        in_use = []

        def sem(name):
            in_use.append(nc.alloc_semaphore(name=name))
            return in_use[-1]

        def release():
            nc.clear_and_free_semaphores(list(in_use))
            in_use.clear()
            nc.all_engine_barrier()

        slab_x = sb("slab_x", [P, SLAB])
        slab_h = sb("slab_h", [P, SLAB])
        slab_acc = sb("slab_acc", [P, SLAB])
        slab_a = sb("slab_a", [P, SLAB])
        slab_b = sb("slab_b", [P, SLAB])
        rings = sb("rings", [P, RING * U * 3 * D])
        rows, rows2 = rings[:, 0:RING * U * 2 * D], rings[:, RING * U * 2 * D:]

        def blocks(slab, width=D, n=NB):
            return slab[:, 0:n * width].rearrange("p (b f) -> p b f", f=width)

        x_v, h_v = blocks(slab_x), blocks(slab_h)

        ident = sb("ident", [P, P])
        quarter = sb("quarter", [P, P])
        far_bf = sb("far_bf", [P, P], BF16)
        tri = sb("tri", [P, P])
        lane = sb("lane", [P, P])
        lane_bf = sb("lane_bf", [P, P], BF16)
        ones = sb("ones", [P, P])
        stats = sb("stats", [P, 4, NB])

        by_src = {"idx": sb("src_idx", [P, TILES], I32), "lo": sb("src_lo", [P, TILES]),
                  "words": sb("src_words", [1, BATCHES], I32), "same": sb("src_same", [P, TILES])}
        by_dst = {"idx": sb("dst_idx", [P, TILES], I32), "lo": sb("dst_lo", [P, TILES]),
                  "words": sb("dst_words", [1, BATCHES], I32), "same": sb("dst_same", [P, TILES]),
                  "noloop": sb("dst_noloop", [P, TILES]), "edge": sb("dst_edge", [P, TILES], I32)}
        stage_idx = sb("stage_idx", [P, ARING, U], I32)
        stage_edge = sb("stage_edge", [P, RING, U], I32)

        sorted_src = dram("sorted_src", [P, TILES * REC])
        sorted_dst = dram("sorted_dst", [P, TILES * REC])
        tab0 = dram("tab0", [NB * P, W_ATT])
        tab1 = dram("tab1", [NB * P, W_ATT])
        tab2 = [dram(f"tab2_{n}", [NB * P, D]) for n in range(3)]
        tab3 = dram("tab3", [NB * P, 2 * D])

        weights, biases = {}, {}
        for name, width in (("l0", W_ATT), ("l1", W_ATT), ("l1w2", D), ("pre", D), ("td", 2 * D), ("ts", 2 * D),
                            ("edge", 2 * D)) + tuple((f"{k}{n}", D) for n in range(3) for k in ("agg", "own")):
            weights[name] = sb(f"w_{name}", [P, width])
        for name, width in (("l0", W_ATT), ("l1", W_ATT), ("l1w2", D), ("pre", D), ("td", 2 * D),
                            ("u0", D), ("u1", D), ("u2", D)):
            biases[name] = sb(f"b_{name}", [P, width])

        def constants():
            loaded, made, filled = sem("c_loaded"), sem("c_made"), sem("c_filled")
            with nc.Block() as block:
                @block.gpsimd
                def _(pool):
                    pool.memset(ident[:], 0.0).then_inc(made, 1)
                    pool.memset(tri[:], 1.0).then_inc(made, 1)
                    pool.iota(lane[:], pattern=[[1, P]], base=0, channel_multiplier=0,
                              allow_small_or_imprecise_dtypes=True).then_inc(made, 1)
                    pool.iota(lane_bf[:], pattern=[[1, P]], base=0, channel_multiplier=0,
                              allow_small_or_imprecise_dtypes=True).then_inc(made, 1)
                    pool.wait_ge(made, 4)
                    pool.affine_select(out=ident[:], in_=ident[:], compare_op=ALU.not_equal, fill=1.0, base=0,
                                       pattern=[[-1, P]], channel_multiplier=1).then_inc(made, 1)
                    pool.affine_select(out=tri[:], in_=tri[:], compare_op=ALU.is_gt, fill=0.0, base=0,
                                       pattern=[[1, P]], channel_multiplier=-1).then_inc(made, 1)

                @block.vector
                def _(dve):
                    dve.memset(ones[:], 1.0)
                    dve.memset(slab_x[:], 0.0).then_inc(filled, 1)
                    dve.wait_ge(made, 5)
                    dve.tensor_scalar(quarter[:], ident[:], 0.25, None, ALU.mult)
                    dve.tensor_scalar(far_bf[:], ident[:], 0.25 * FAR, None, ALU.mult)

                @block.sync
                def _(sp):
                    sp.wait_ge(filled, 1)
                    sp.dma_start(x_v[:, 0:BLKS - 1, :],
                                 io["x"][0:(BLKS - 1) * P, :].rearrange("(b p) f -> p b f", p=P)).then_inc(loaded, 16)
                    sp.dma_start(x_v[0:TAIL, BLKS - 1, :], io["x"][(BLKS - 1) * P:N, :]).then_inc(loaded, 16)
                    sp.wait_ge(loaded, 32)

        def sort_views(home):
            work = slab_b
            col = lambda n: work[:, n * COLS:(n + 1) * COLS]
            return {"record": home[:, 0:COLS * REC].rearrange("p (c w) -> p c w", w=REC),
                    "slot": home[:, COLS * REC:COLS * (REC + 1)].bitcast(I32),
                    "key": col(0).bitcast(I32), "nbr": col(1).bitcast(I32), "blk": col(2), "mask": col(3),
                    "scan": col(4), "pos": col(5), "int": col(6).bitcast(I32), "int2": col(7).bitcast(I32)}

        cnt = sb("cnt", [P, 64])
        base = sb("base", [P, 64])
        start = sb("start", [P, 4])
        start_i = sb("start_i", [P, 1], I32)
        pick = sb("pick", [P, P])

        def place_edges(tag, key_in, nbr_in, home, table, order, with_loops, scatter_of=None):
            v = sort_views(home)
            loaded, ready, chain = sem(f"{tag}_loaded"), sem(f"{tag}_ready"), sem(f"{tag}_chain")
            counted, placed, summed = sem(f"{tag}_counted"), sem(f"{tag}_placed"), sem(f"{tag}_summed")
            picked = sem(f"{tag}_picked")
            cleared, masked, passed = sem(f"{tag}_cleared"), sem(f"{tag}_masked"), sem(f"{tag}_passed")
            fill = rows[:, 0:TILES * REC]
            with ExitStack() as local, nc.Block() as block:
                tot = local.enter_context(nc.psum_tensor(f"{tag}_tot", [P, 512], F32))
                bas = local.enter_context(nc.psum_tensor(f"{tag}_bas", [P, 512], F32))
                til = local.enter_context(nc.psum_tensor(f"{tag}_til", [P, 2, 512], F32))

                @block.sync
                def _(sp):
                    sp.wait_ge(ready, 1)
                    for dst, src in ((v["key"], key_in), (v["nbr"], nbr_in)):
                        sp.dma_start(dst[0:P - 1, :], src[0:(P - 1) * COLS].rearrange("(p c) -> p c", c=COLS)
                                     ).then_inc(loaded, 16)
                        sp.dma_start(dst[P - 1:P, 0:LASTROW],
                                     src[(P - 1) * COLS:E].rearrange("(p c) -> p c", p=1)).then_inc(loaded, 16)
                    sp.wait_ge(ready, 2)
                    sp.dma_start(table[:, :], fill).then_inc(cleared, 16)
                    sp.wait_ge(cleared, 16)

                @block.vector
                def _(dve):
                    count = [0]

                    def link(ins):
                        count[0] += 1
                        ins.then_inc(chain, 1)
                        dve.wait_ge(chain, count[0])

                    dve.memset(v["key"], PADKEY)
                    dve.memset(v["nbr"], PADKEY).then_inc(ready, 1)
                    f = fill.rearrange("p (t w) -> p t w", w=REC)
                    link(dve.memset(f, 0.0))
                    dve.memset(f[:, :, 1:3], -1.0).then_inc(ready, 1)
                    dve.wait_ge(loaded, 64)
                    rec = v["record"]
                    link(dve.tensor_single_scalar(v["int"], v["key"], 7, ALU.logical_shift_right))
                    link(dve.tensor_copy(v["blk"], v["int"]))
                    link(dve.tensor_single_scalar(v["int2"], v["key"], P - 1, ALU.bitwise_and))
                    link(dve.tensor_scalar(v["scan"], v["blk"], float(BLKS), -1000.0, ALU.is_equal, ALU.mult))
                    link(dve.tensor_tensor(rec[:, :, 1], v["int2"], v["scan"], ALU.add))
                    link(dve.tensor_copy(rec[:, :, 0], v["nbr"]))
                    if with_loops:
                        link(dve.tensor_tensor(v["mask"], v["key"], v["nbr"], ALU.is_equal))
                        link(dve.scalar_tensor_tensor(rec[:, :, 2], v["mask"], -1000.0, rec[:, :, 1],
                                                      ALU.mult, ALU.add))
                        dve.wait_ge(placed, 1)
                        link(dve.tensor_scalar(rec[:, :, 3], v["int"], float(E - 1), None, ALU.min))
                    else:
                        link(dve.memset(rec[:, :, 2:4], 0.0))

                    with dve.Fori(0, BUCKETS) as b:
                        dve.tensor_scalar(v["mask"], v["blk"], lane[:, bass.ds(b, 1)], 0.0, ALU.is_equal, ALU.add,
                                          accum_out=cnt[:, bass.ds(b, 1)]).then_inc(masked, 1)
                        dve.wait_ge(masked, b + 1)
                    link(dve.tensor_copy(cnt[:, BUCKETS:BUCKETS + 1], ones[:, 0:1]))
                    dve.tensor_copy(start[:, 3:4], ones[:, 0:1]).then_inc(counted, 1)
                    dve.wait_ge(summed, 1)
                    link(dve.tensor_scalar(start_i[0:BUCKETS, :], tot[0:BUCKETS, 0:1], float(P - 1), None, ALU.add))
                    link(dve.tensor_single_scalar(start_i[0:BUCKETS, :], start_i[0:BUCKETS, :], 7,
                                                  ALU.logical_shift_right))
                    dve.tensor_copy(start[0:BUCKETS, 0:1], start_i[0:BUCKETS, :]).then_inc(counted, 1)
                    dve.wait_ge(summed, 2)
                    link(dve.tensor_copy(start[0:BUCKETS, 1:2], tot[0:BUCKETS, 1:2]))
                    link(dve.tensor_scalar(start[0:BUCKETS, 2:3], start[0:BUCKETS, 1:2], float(P), None, ALU.mult))
                    dve.wait_ge(placed, 2)
                    dve.tensor_scalar(v["pos"][0:BUCKETS, 0:COLS], v["scan"][0:BUCKETS, 0:COLS],
                                      start[0:BUCKETS, 1:2], None, ALU.is_ge)
                    dve.tensor_scalar(v["mask"][0:BUCKETS, 0:TILES - COLS], v["scan"][0:BUCKETS, 0:TILES - COLS],
                                      float(COLS), start[0:BUCKETS, 1:2], ALU.add, ALU.is_ge).then_inc(counted, 1)
                    dve.wait_ge(summed, 3)
                    link(dve.tensor_copy(base[:, 0:BUCKETS], bas[:, 0:BUCKETS]))
                    tb = rows2[:, 0:TILES]
                    dve.tensor_copy(tb[:, 0:512], til[:, 0, :])
                    link(dve.tensor_copy(tb[:, 512:TILES], til[:, 1, 0:TILES - 512]))
                    dve.memset(order["same"][:, 0:1], 0.0)
                    link(dve.tensor_tensor(order["same"][:, 1:TILES], tb[:, 1:TILES], tb[:, 0:TILES - 1],
                                           ALU.is_equal))
                    if with_loops:
                        link(dve.tensor_scalar(order["same"][:, :], order["same"][:, :], 1.0, -FAR,
                                               ALU.subtract, ALU.mult))
                    tbi = rows2[0:1, TILES:2 * TILES].bitcast(I32)
                    link(dve.tensor_copy(tbi, tb[0:1, :]))
                    quad = tbi.rearrange("p (b k) -> p b k", k=U)
                    link(dve.tensor_copy(order["words"][:, :], quad[:, :, 0]))
                    for k in range(1, U):
                        link(dve.tensor_single_scalar(quad[:, :, k], quad[:, :, k], 8 * k, ALU.logical_shift_left))
                        link(dve.tensor_tensor(order["words"][:, :], order["words"][:, :], quad[:, :, k],
                                               ALU.bitwise_or))
                    with dve.Fori(0, BUCKETS) as b:
                        dve.tensor_scalar(v["mask"], v["blk"], lane[:, bass.ds(b, 1)], None, ALU.is_equal
                                          ).then_inc(masked, 1)
                        dve.wait_ge(masked, b * 3 + BUCKETS + 1)
                        dve.tensor_tensor_scan(v["scan"], v["mask"], v["mask"], base[:, bass.ds(b, 1)],
                                               ALU.add, ALU.max).then_inc(masked, 1)
                        dve.wait_ge(masked, b * 3 + BUCKETS + 2)
                        hold_wait(dve, passed)
                        dve.copy_predicated(v["pos"], v["mask"].bitcast(I32), v["scan"]).then_inc(masked, 1)
                        dve.wait_ge(masked, b * 3 + BUCKETS + 3)
                    link(dve.tensor_scalar(v["int"], v["pos"], -1.0, None, ALU.add))
                    link(dve.tensor_single_scalar(v["int2"], v["int"], P - 1, ALU.bitwise_and))
                    link(dve.tensor_single_scalar(v["int"], v["int"], 7, ALU.logical_shift_right))
                    link(dve.scalar_tensor_tensor(v["slot"], v["int2"], float(TILES), v["int"], ALU.mult, ALU.add))

                @block.tensor
                def _(pe):
                    pe.wait_ge(counted, 1)
                    pe.matmul(tot[0:BUCKETS, 0:1], cnt[:, 0:BUCKETS], start[:, 3:4], start=True, stop=True
                              ).then_inc(summed, 1)
                    pe.wait_ge(counted, 2)
                    pe.matmul(tot[0:BUCKETS, 1:2], tri[0:BUCKETS, 0:BUCKETS], start[0:BUCKETS, 0:1],
                              start=True, stop=True).then_inc(summed, 1)
                    pe.wait_ge(counted, 3)
                    pe.matmul(bas[:, 0:BUCKETS], tri[:, :], cnt[:, 0:BUCKETS], start=True, stop=False)
                    pe.matmul(bas[:, 0:BUCKETS], start[0:BUCKETS, 2:3].to_broadcast([BUCKETS, P]),
                              ident[0:BUCKETS, 0:BUCKETS], start=False, stop=True)
                    pk = pick[0:BUCKETS, :]
                    pe.matmul(til[:, 0, :], pk, v["pos"][0:BUCKETS, 0:512], start=True, stop=True)
                    pe.matmul(til[:, 1, 0:COLS - 512], pk, v["pos"][0:BUCKETS, 512:COLS], start=True, stop=True)
                    pe.matmul(til[:, 1, COLS - 512:TILES - 512], pk, v["mask"][0:BUCKETS, 0:TILES - COLS],
                              start=True, stop=True).then_inc(summed, 1)

                @block.gpsimd
                def _(pool):
                    if with_loops:
                        pool.wait_ge(chain, 3)
                        pool.iota(v["int"], pattern=[[1, COLS]], base=0, channel_multiplier=COLS).then_inc(placed, 1)
                    else:
                        pool.memset(pick[:], 1.0).then_inc(placed, 1)
                        pool.wait_ge(placed, 1)
                        pool.affine_select(out=pick[:], in_=pick[:], compare_op=ALU.not_equal, fill=0.0, base=0,
                                           pattern=[[0, P]], channel_multiplier=1).then_inc(picked, 1)
                        pool.wait_ge(picked, 1)
                        pool.affine_select(out=pick[:], in_=pick[:], compare_op=ALU.not_equal, fill=0.0, base=-BLKS,
                                           pattern=[[0, P]], channel_multiplier=1).then_inc(picked, 1)
                        pool.wait_ge(picked, 2)
                    pool.wait_ge(summed, 1)
                    pool.iota(v["scan"], pattern=[[1, COLS]], base=0, channel_multiplier=0,
                              allow_small_or_imprecise_dtypes=True).then_inc(placed, 1)
                    if scatter_of:
                        scatter(pool, *scatter_of)

        scatter_rec = sb("scatter_rec", [P, SR, SU * REC])
        scatter_slot = sb("scatter_slot", [P, SR, SU], I32)

        def scatter(pool, tag, home, table):
            v = sort_views(home)
            staged, passed = sem(f"{tag}_staged"), sem(f"{tag}_passed")
            sent = [sem(f"{tag}_sent{r}") for r in range(SR)]
            record = home[:, 0:COLS * REC]
            target = table[:, :].rearrange("p (t w) -> (p t) w", w=REC)

            def step(s, r):
                if past(s, SR):
                    pool.wait_ge(sent[r], ((s - r) // SR) * (16 * SU) if isinstance(s, int)
                                 else (s - r) * (16 * SU // SR))
                pool.tensor_copy(scatter_rec[:, r, :], record[:, bass.ds(s * (SU * REC), SU * REC)])
                pool.tensor_copy(scatter_slot[:, r, :], v["slot"][:, bass.ds(s * SU, SU)]).then_inc(staged, 1)
                pool.wait_ge(staged, s + 1)
                hold_wait(pool, passed)
                for k in range(SU):
                    pool.indirect_dma_start(
                        out=target, out_offset=bass.IndirectOffsetOnAxis(ap=scatter_slot[:, r, k:k + 1], axis=0),
                        in_=scatter_rec[:, r, k * REC:(k + 1) * REC], in_offset=None).then_inc(sent[r], 16)

            steps(pool, COLS // SU, SR, 0, step)
            for r in range(SR):
                pool.wait_ge(sent[r], 16 * SU * (COLS // SU // SR))

        def load_sorted(tag, table, order, extra=None, with_loops=False):
            got, split = sem(f"{tag}_got"), sem(f"{tag}_split")
            raw = slab_b[:, 0:TILES * REC]
            words = raw.rearrange("p (t w) -> p t w", w=REC)
            with nc.Block() as block:
                @block.sync
                def _(sp):
                    sp.dma_start(raw, table[:, :]).then_inc(got, 16)

                @block.vector
                def _(dve):
                    dve.wait_ge(got, 16)
                    dve.tensor_copy(order["idx"][:, :], words[:, :, 0])
                    dve.tensor_copy(order["lo"][:, :], words[:, :, 1])
                    if with_loops:
                        dve.tensor_copy(order["noloop"][:, :], words[:, :, 2])
                        dve.tensor_copy(order["edge"][:, :], words[:, :, 3])

                if extra:
                    extra(block)

        def load_weights():
            got, multiplied = sem("w_got"), sem("w_multiplied")
            w0 = slab_a[:, 0:128]
            w1t = slab_a[:, 128:256]
            a01 = slab_a[:, 256:260]
            cols = slab_a[:, 260:264]
            wct = slab_a[:, 512:896].rearrange("p (n f) -> p n f", f=D)
            top = slab_a[:, 896:1280].rearrange("p (n f) -> p n f", f=D)
            filled = sem("w_filled")
            with ExitStack() as local, nc.Block() as block:
                ps = [local.enter_context(nc.psum_tensor(f"w_ps{i}", [P, 512], F32)) for i in range(5)]
                loads = [(w0, io["w0"]), (w1t, io["watt_t"]), (a01[:, 0:2], io["a0"]), (a01[:, 2:4], io["a1"]),
                         (weights["l0"][:, 0:D], io["w0_t"]), (weights["l1"][:, 0:D], io["w1"]),
                         (weights["l1w2"][:, :], io["w2"]), (weights["pre"][:, :], io["wpre"]),
                         (cols[:, 0:1], io["batt"]), (cols[:, 1:4], io["bconv_t"])]
                for n in range(3):
                    loads += [(wct[:, n, :], io["wconv_t"][n]), (top[:, n, :], io["wupd"][n, 0:D, :]),
                              (weights[f"own{n}"][:, :], io["wupd"][n, D:2 * D, :]),
                              (biases[f"u{n}"][:, :], io["bupd"][n:n + 1, :].to_broadcast([P, D]))]
                for i, name in enumerate(("td", "ts", "edge")):
                    loads += [(weights[name][:, 0:D], io["wf"][i * D:(i + 1) * D, :]),
                              (weights[name][:, D:2 * D], io["ws"][i * D:(i + 1) * D, :])]
                loads += [(biases["l1"][:, 0:D], io["b1"].to_broadcast([P, D])),
                          (biases["l1w2"][:, :], io["b2"].to_broadcast([P, D])),
                          (biases["pre"][:, :], io["bpre"].to_broadcast([P, D])),
                          (biases["td"][:, 0:D], io["bf"].to_broadcast([P, D])),
                          (biases["td"][:, D:2 * D], io["bs"].to_broadcast([P, D]))]

                @block.sync
                def _(sp):
                    for dst, src in loads:
                        sp.dma_start(dst, src).then_inc(got, 16)

                @block.tensor
                def _(pe):
                    pe.wait_ge(got, 16 * len(loads))
                    pe.matmul(ps[0][:, 0:2], w0, a01[:, 0:2], start=True, stop=True)
                    pe.matmul(ps[1][:, 0:2], w1t, a01[:, 2:4], start=True, stop=True)
                    pe.matmul(ps[1][:, 2:4], cols[:, 0:1].to_broadcast([P, P]), a01[:, 2:4], start=True, stop=True)
                    for n in range(3):
                        pe.matmul(ps[2 + n][:, 0:D], wct[:, n, :], top[:, n, :], start=True, stop=True)
                        last = pe.matmul(ps[2 + n][:, D:2 * D], cols[:, 1 + n:2 + n].to_broadcast([P, P]),
                                         top[:, n, :], start=True, stop=True)
                    last.then_inc(multiplied, 1)

                @block.vector
                def _(dve):
                    dve.memset(biases["l0"][:, :], 0.0).then_inc(filled, 1)
                    dve.memset(weights["l0"][:, D:D + 1], 0.0)
                    dve.memset(weights["l1"][:, D:D + 1], 0.0)
                    dve.memset(biases["l1"][:, D:D + 1], 1.0)
                    dve.wait_ge(filled, 1)
                    dve.memset(biases["l0"][:, D:D + 1], 1.0)
                    dve.wait_ge(multiplied, 1)
                    dve.tensor_copy(weights["l0"][:, D + 1:W_ATT], ps[0][:, 0:2])
                    dve.tensor_copy(weights["l1"][:, D + 1:W_ATT], ps[1][:, 0:2])
                    dve.tensor_copy(biases["l1"][:, D + 1:W_ATT], ps[1][:, 2:4])
                    for n in range(3):
                        dve.tensor_copy(weights[f"agg{n}"][:, :], ps[2 + n][:, 0:D])
                        dve.tensor_tensor(biases[f"u{n}"][:, :], ps[2 + n][:, D:2 * D], biases[f"u{n}"][:, :],
                                          ALU.add)

        def norm(tag):
            chain, rooted = sem(f"{tag}_chain"), sem(f"{tag}_rooted")
            sq = blocks(slab_b)
            mean, var, std, inv = (stats[:, i, :] for i in range(4))
            wide = lambda a: a.unsqueeze(2).to_broadcast([P, NB, D])
            with nc.Block() as block:
                @block.vector
                def _(dve):
                    count = [0]

                    def link(ins):
                        count[0] += 1
                        ins.then_inc(chain, 1)
                        dve.wait_ge(chain, count[0])

                    link(dve.tensor_reduce(mean, x_v, AX.X, ALU.add))
                    link(dve.tensor_scalar(mean, mean, 1.0 / D, None, ALU.mult))
                    link(dve.tensor_tensor(h_v, x_v, wide(mean), ALU.subtract))
                    link(dve.tensor_tensor(sq, h_v, h_v, ALU.mult))
                    link(dve.tensor_reduce(var, sq, AX.X, ALU.add))
                    link(dve.tensor_scalar(var, var, 1.0 / D, 1e-5, ALU.mult, ALU.add))
                    dve.wait_ge(rooted, 1)
                    link(dve.reciprocal(inv, std))
                    link(dve.tensor_tensor(h_v, h_v, wide(inv), ALU.mult))
                    link(dve.tensor_scalar(h_v, h_v, 0.0, None, ALU.max))

                @block.scalar
                def _(act):
                    act.wait_ge(chain, 6)
                    act.activation(std, var, ACT.Sqrt).then_inc(rooted, 1)

        def dense(tag, sources, mats, bias, width, target=None, target2=None, table=None, relu=False):
            staged, turned, copied = sem(f"{tag}_staged"), sem(f"{tag}_turned"), sem(f"{tag}_copied")
            produced, evacuated, added = sem(f"{tag}_produced"), sem(f"{tag}_evacuated"), sem(f"{tag}_added")
            stored = [sem(f"{tag}_stored{r}") for r in range(2)]
            ns = len(sources)
            stage = [rows[:, r * 512:r * 512 + ns * DB * D].rearrange("p (i u f) -> p i u f", i=ns, u=DB)
                     for r in range(2)]
            tsb = [rows[:, 1024 + r * 512:1024 + r * 512 + ns * DB * D].rearrange("p (i f) -> p i f", f=P)
                   for r in range(2)]
            oring = [rows[:, 2048 + r * 512:2048 + r * 512 + DB * width].rearrange("p (u f) -> p u f", u=DB)
                     for r in range(2)]
            with ExitStack() as local, nc.Block() as block:
                tp = [local.enter_context(nc.psum_tensor(f"{tag}_tp{r}", [P, 4, P], F32)) for r in range(2)]
                op = [local.enter_context(nc.psum_tensor(f"{tag}_op{r}", [P, DB, 256], F32)) for r in range(2)]

                @block.scalar
                def _(act):
                    def step(s, r):
                        if within(s, DBATCHES):
                            if past(s, 2):
                                act.wait_ge(turned, s - 1)
                            for i, src in enumerate(sources):
                                last = act.activation(stage[r][:, i, :, :], src[:, bass.ds(s * DB, DB), :], ACT.Copy)
                            last.then_inc(staged, 1)
                        if past(s, 1):
                            q = s - 1
                            act.wait_ge(turned, q + 1)
                            if past(s, 3):
                                act.wait_ge(produced, q - 1)
                            act.activation(tsb[1 - r], tp[1 - r][:, 0:ns * DB, :], ACT.Copy).then_inc(copied, 1)

                    steps(act, DBATCHES, 2, 1, step)

                @block.tensor
                def _(pe):
                    def step(s, r):
                        if within(s, DBATCHES):
                            pe.wait_ge(staged, s + 1)
                            if past(s, 2):
                                pe.wait_ge(copied, s - 1)
                            for i in range(ns):
                                for u in range(DB):
                                    last = pe.transpose(tp[r][:, i * DB + u, :], stage[r][:, i, u, :], ident[:])
                            last.then_inc(turned, 1)
                        if past(s, 1):
                            q = s - 1
                            pe.wait_ge(copied, q + 1)
                            if past(s, 3):
                                pe.wait_ge(evacuated, q - 1)
                            for u in range(DB):
                                for i in range(ns):
                                    last = pe.matmul(op[1 - r][:, u, 0:width], tsb[1 - r][:, i * DB + u, :],
                                                     mats[i][:, :], start=(i == 0), stop=(i == ns - 1))
                            last.then_inc(produced, 1)

                    steps(pe, DBATCHES, 2, 1, step)

                @block.vector
                def _(dve):
                    def step(q, r):
                        dve.wait_ge(produced, q + 1)
                        if target is None and past(q, 2):
                            dve.wait_ge(stored[r], (q - r) * 8)
                        halves = ([(oring[r], 0, width)] if target is None else
                                  [(target[:, bass.ds(q * DB, DB), :], 0, width)] if target2 is None else
                                  [(t[:, bass.ds(q * DB, DB), :], i * D, D) for i, t in enumerate((target, target2))])
                        for dst, at, w in halves:
                            if bias is None:
                                last = dve.tensor_copy(dst, op[r][:, :, at:at + w])
                            else:
                                last = dve.tensor_tensor(dst, op[r][:, :, at:at + w],
                                                         bias[:, at:at + w].unsqueeze(1).to_broadcast([P, DB, w]),
                                                         ALU.add)
                        if relu:
                            last.then_inc(added, 1)
                            dve.wait_ge(added, q + 1)
                            last = dve.tensor_scalar(halves[0][0], halves[0][0], 0.0, None, ALU.max)
                        last.then_inc(evacuated, 1)

                    steps(dve, DBATCHES, 2, 0, step)

                if table is not None:
                    trows = table.rearrange("(b p) f -> p b f", p=P)

                    @block.sync
                    def _(sp):
                        def step(q, r):
                            sp.wait_ge(evacuated, q + 1)
                            src = oring[r] if target is None else target[:, bass.ds(q * DB, DB), :]
                            sp.dma_start(trows[:, bass.ds(q * DB, DB), :], src).then_inc(stored[r], 16)

                        steps(sp, DBATCHES, 2, 0, step)
                        for r in range(2):
                            sp.wait_ge(stored[r], 16 * (DBATCHES // 2))

        def gathers(pool, tag, sources, freed, ring=RING):
            staged, passed = sem(f"{tag}_staged"), sem(f"{tag}_passed")
            got = [sem(f"{tag}_got{r}") for r in range(ring)]

            def step(s, r):
                if past(s, ring):
                    pool.wait_ge(freed, s - (ring - 1))
                for table, idx, stage, place in sources:
                    last = pool.tensor_copy(stage[:, r, :], idx[:, bass.ds(s * U, U)])
                last.then_inc(staged, 1)
                pool.wait_ge(staged, s + 1)
                hold_wait(pool, passed)
                for k in range(U):
                    for table, idx, stage, place in sources:
                        pool.indirect_dma_start(
                            out=place[:, r, k, :], out_offset=None, in_=table,
                            in_offset=bass.IndirectOffsetOnAxis(ap=stage[:, r, k:k + 1], axis=0)).then_inc(got[r], 16)

            return got, lambda: steps(pool, BATCHES, ring, 0, step)

        def arrived(eng, got, s, r, per):
            ring = len(got)
            eng.wait_ge(got[r], (s // ring + 1) * per if isinstance(s, int) else (s - r) // ring * per + per)

        def attention(tag, table, order, own, sums, floor_at_zero, maxima=None):
            mask_ready, scored, leaky = sem(f"{tag}_mask"), sem(f"{tag}_scored"), sem(f"{tag}_leaky")
            positive, passed = sem(f"{tag}_positive"), sem(f"{tag}_dve_passed")
            shift, chain, probs = sem(f"{tag}_shift"), sem(f"{tag}_chain"), sem(f"{tag}_probs")
            turned, copied, mixed = sem(f"{tag}_turned"), sem(f"{tag}_copied"), sem(f"{tag}_mixed")
            merged, cleared = sem(f"{tag}_merged"), sem(f"{tag}_cleared")
            ring = rings[:, 0:ARING * U * W_ATT].rearrange("p (r k f) -> p r k f", r=ARING, k=U)
            at = [0]

            def work(n):
                at[0] += n
                return slab_b[:, at[0] - n:at[0]]

            tiles4 = lambda a: a.rearrange("p (k e) -> p k e", k=U)
            mask = [tiles4(work(U * P // 2).bitcast(BF16)) for _ in range(2)]
            score = [tiles4(work(U * P)) for _ in range(2)]
            prob = [tiles4(work(U * P)) for _ in range(2)]
            prob_t = [tiles4(work(U * P)) for _ in range(2)]
            top = [work(U) for _ in range(2)]
            run = [work(U + 1) for _ in range(5)]
            drop = [work(U) for _ in range(2)]
            minus = [work(U) for _ in range(2)]
            decay = [work(U) for _ in range(5)]
            op0 = ALU.mult if floor_at_zero else ALU.add
            lanes_bf = lane_bf[:].unsqueeze(1).to_broadcast([P, U, P])
            K = 4
            with ExitStack() as local, nc.Block() as block:
                xp = [local.enter_context(nc.psum_tensor(f"{tag}_x{r}", [P, U, P], F32)) for r in range(2)]
                tp = local.enter_context(nc.psum_tensor(f"{tag}_t", [P, U, P], F32))
                op = [local.enter_context(nc.psum_tensor(f"{tag}_o{r}", [P, U, 256], F32)) for r in range(2)]
                got = [None]

                @block.gpsimd
                def _(pool):
                    got[0], run_gathers = gathers(pool, tag, [(table, order["idx"], stage_idx, ring)], mixed, ARING)
                    run_gathers()

                @block.vector
                def _(dve):
                    dve.memset(sums, 0.0)
                    if maxima is not None:
                        dve.memset(maxima, FAR)
                    dve.memset(run[4], 0.0).then_inc(cleared, 1)
                    dve.wait_ge(cleared, 1)
                    load = BlockWords(nc, dve, order["words"], 4)

                    def step(s, rr, word):
                        r = rr % 2
                        block_of = load.blocks(word) if past(s, 4) else None
                        if within(s, BATCHES):
                            lo = order["lo"][:, bass.ds(s * U, U)].unsqueeze(2).to_broadcast([P, U, P])
                            if past(s, 2):
                                dve.wait_ge(scored, s - 1)
                            dve.tensor_tensor(mask[r], lanes_bf, lo, ALU.not_equal).then_inc(mask_ready, 1)
                        if past(s, 4):
                            dve.wait_ge(mixed, s - 3)

                        def merge(k):
                            if not past(s, 4):
                                return
                            q = s - 4
                            acc = sums[:, bass.ds(block_of[k], 1), :].rearrange("p b f -> p (b f)")
                            dve.wait_ge(merged, q * U + k)
                            if maxima is not None:
                                dve.tensor_copy(maxima[:, bass.ds(block_of[k], 1)],
                                                run[(rr - 4) % 5][:, k + 1:k + 2])
                            dve.scalar_tensor_tensor(acc, acc, decay[(rr - 4) % 5][:, k:k + 1],
                                                     op[r][:, k, 0:D + 1], ALU.mult, ALU.add).then_inc(merged, 1)

                        if not (past(s, 1) and within(s, BATCHES + 1)):
                            for k in range(U):
                                merge(k)
                            return
                        merge(0)
                        q, c, now, before = s - 1, 1 - r, (rr - 1) % 5, (rr - 2) % 5
                        same = order["same"][:, bass.ds(q * U, U)]

                        def link(ins, n):
                            ins.then_inc(chain, 1)
                            return q * K + n

                        dve.wait_ge(positive, q + 1)
                        hold_wait(dve, passed)
                        for k in range(U):
                            last = dve.tensor_tensor_reduce(
                                out=score[c][:, k, :], in0=xp[c][:, k, :], in1=score[c][:, k, :], scale=1.0,
                                scalar=FLOOR, op0=ALU.add, op1=ALU.max, accum_out=top[c][:, k:k + 1])
                        last.then_inc(leaky, 1)
                        carried = link(dve.tensor_copy(run[now][:, 0:1], run[before][:, U:U + 1]), 1)
                        merge(1)
                        dve.wait_ge(leaky, q + 1)
                        dve.wait_ge(chain, carried)
                        scanned = link(dve.tensor_tensor_scan(run[now][:, 1:U + 1], same, top[c], run[now][:, 0:1],
                                                              op0, ALU.max), 2)
                        merge(2)
                        dve.wait_ge(chain, scanned)
                        if past(s, 3):
                            dve.wait_ge(probs, q - 1)
                        kept = link(dve.tensor_tensor(drop[c], run[now][:, 0:U], same, op0), 3)
                        dve.tensor_scalar(minus[c], run[now][:, 1:U + 1], -(1.0 - SLOPE), None, ALU.mult
                                          ).then_inc(shift, 1)
                        merge(3)
                        dve.wait_ge(chain, kept)
                        link(dve.tensor_tensor(drop[c], drop[c], run[now][:, 1:U + 1], ALU.subtract), 4)

                    steps(dve, BATCHES, ARING, 4, step, load)

                @block.tensor
                def _(pe):
                    load = BlockWords(nc, pe, order["words"], 0)

                    def step(s, rr, word):
                        r = rr % 2
                        if within(s, BATCHES):
                            block_of = load.blocks(word)
                            pe.wait_ge(mask_ready, s + 1)
                            arrived(pe, got[0], s, rr, 16 * U)
                            if past(s, 2):
                                pe.wait_ge(leaky, s - 1)
                            for k in range(U):
                                pe.matmul(xp[r][:, k, :], mask[r][:, k, :], far_bf[:], start=True, stop=False)
                                pe.matmul(xp[r][:, k, :], ring[:, rr, k, D + 1:D + 2].to_broadcast([P, P]),
                                          quarter[:], start=False, stop=False)
                                last = pe.matmul(xp[r][:, k, :], quarter[:],
                                                 own[:, bass.ds(block_of[k], 1)].to_broadcast([P, P]),
                                                 start=False, stop=True)
                            last.then_inc(scored, 1)
                        if past(s, 2) and within(s, BATCHES + 2):
                            q = s - 2
                            pe.wait_ge(probs, q + 1)
                            if past(s, 3):
                                pe.wait_ge(copied, q)
                            for k in range(U):
                                last = pe.transpose(tp[:, k, :], prob[r][:, k, :], ident[:])
                            last.then_inc(turned, 1)
                        if past(s, 3):
                            q, c = s - 3, 1 - r
                            pe.wait_ge(copied, q + 1)
                            if past(s, 5):
                                pe.wait_ge(merged, (q - 1) * U)
                            for k in range(U):
                                last = pe.matmul(op[c][:, k, 0:D + 1], prob_t[c][:, k, :],
                                                 ring[:, (rr - 3) % ARING, k, 0:D + 1], start=True, stop=True)
                            last.then_inc(mixed, 1)

                    steps(pe, BATCHES, ARING, 3, step, load)

                @block.scalar
                def _(act):
                    def step(s, rr):
                        r = rr % 2
                        if within(s, BATCHES):
                            act.wait_ge(scored, s + 1)
                            if past(s, 2):
                                act.wait_ge(probs, s - 1)
                            act.activation(score[r], xp[r][:], ACT.Relu, scale=4.0).then_inc(positive, 1)
                        if past(s, 1) and within(s, BATCHES + 1):
                            q, c = s - 1, 1 - r
                            act.wait_ge(shift, q + 1)
                            if past(s, 3):
                                act.wait_ge(turned, q - 1)
                            if past(s, 6):
                                act.wait_ge(merged, (q - 4) * U)
                            for k in range(U):
                                act.activation(prob[c][:, k, :], score[c][:, k, :], ACT.Exp,
                                               bias=minus[c][:, k:k + 1], scale=1.0 - SLOPE)
                            act.wait_ge(chain, (q + 1) * K)
                            act.activation(decay[(rr - 1) % 5], drop[c], ACT.Exp, scale=1.0 - SLOPE
                                           ).then_inc(probs, 1)
                        if past(s, 2):
                            q = s - 2
                            act.wait_ge(turned, q + 1)
                            if past(s, 4):
                                act.wait_ge(mixed, q - 1)
                            act.activation(prob_t[r], tp[:], ACT.Copy).then_inc(copied, 1)

                    steps(act, BATCHES, ARING, 2, step)

        def spread(tag, table, sums):
            hot_ready, mixed, merged, cleared = (sem(f"{tag}_{n}") for n in ("hot", "mixed", "merged", "cleared"))
            ring = rows[:, 0:RING * U * D].rearrange("p (r k f) -> p r k f", r=RING, k=U)
            hot = [rows2[:, r * U * P:(r + 1) * U * P].rearrange("p (k e) -> p k e", k=U) for r in range(2)]
            with ExitStack() as local, nc.Block() as block:
                op = [local.enter_context(nc.psum_tensor(f"{tag}_o{r}", [P, U, D], F32)) for r in range(2)]
                got = [None]

                @block.gpsimd
                def _(pool):
                    got[0], run_gathers = gathers(pool, tag, [(table, by_dst["idx"], stage_idx, ring)], mixed)
                    run_gathers()

                @block.vector
                def _(dve):
                    dve.memset(sums, 0.0).then_inc(cleared, 1)
                    dve.wait_ge(cleared, 1)
                    load = BlockWords(nc, dve, by_dst["words"], 2)

                    def step(s, r, word):
                        r = r % 2
                        if past(s, 2):
                            dve.wait_ge(mixed, s - 1)
                        block_of = load.blocks(word) if past(s, 2) else None
                        for k in range(U):
                            if within(s, BATCHES):
                                last = dve.tensor_scalar(hot[r][:, k, :], lane[:],
                                                         by_dst["noloop"][:, bass.ds(s * U + k, 1)], None,
                                                         ALU.is_equal)
                                if k == U - 1:
                                    last.then_inc(hot_ready, 1)
                            if past(s, 2):
                                q = s - 2
                                acc = sums[:, bass.ds(block_of[k], 1), :].rearrange("p b f -> p (b f)")
                                dve.wait_ge(merged, q * U + k)
                                dve.tensor_tensor(acc, acc, op[r][:, k, :], ALU.add).then_inc(merged, 1)

                    steps(dve, BATCHES, RING, 2, step, load)

                @block.tensor
                def _(pe):
                    def step(s, r4):
                        r = r4 % 2
                        pe.wait_ge(hot_ready, s + 1)
                        arrived(pe, got[0], s, r4, 16 * U)
                        if past(s, 2):
                            pe.wait_ge(merged, (s - 1) * U)
                        for k in range(U):
                            last = pe.matmul(op[r][:, k, :], hot[r][:, k, :], ring[:, r4, k, :], start=True, stop=True)
                        last.then_inc(mixed, 1)

                    steps(pe, BATCHES, RING, 0, step)

        def gated(tag, table, edge_rows, own_gate, own_core, sums):
            hot_ready, turned, copied, joined = (sem(f"{tag}_{n}") for n in ("hot", "turned", "copied", "joined"))
            projected = sem(f"{tag}_projected")
            logged, split, gate_ready, sent = (sem(f"{tag}_{n}") for n in ("logged", "split", "gate", "sent"))
            mixed, merged, cleared, chain = (sem(f"{tag}_{n}") for n in ("mixed", "merged", "cleared", "chain"))
            ring = rows[:, :].rearrange("p (r k f) -> p r k f", r=RING, k=U)
            ering = rows2[:, :].rearrange("p (r k f) -> p r k f", r=RING, k=U)
            home = slab_h
            pos = [0]

            def work(n):
                pos[0] += n
                assert pos[0] <= SLAB
                return home[:, pos[0] - n:pos[0]]

            tiles4 = lambda a: a.rearrange("p (k e) -> p k e", k=U)
            hot = [tiles4(work(512)) for _ in range(4)]
            hot_t = [tiles4(work(512)) for _ in range(2)]
            edge_t = [tiles4(work(512)) for _ in range(2)]
            soft = [tiles4(work(1024)) for _ in range(2)]
            gate = [a[:, :, 0:D] for a in soft]
            core = [a[:, :, D:2 * D] for a in soft]
            with ExitStack() as local, nc.Block() as block:
                tp = [local.enter_context(nc.psum_tensor(f"{tag}_t{r}", [P, U, P], F32)) for r in range(2)]
                zp = [local.enter_context(nc.psum_tensor(f"{tag}_z{r}", [P, U, 2 * D], F32)) for r in range(2)]
                op = [local.enter_context(nc.psum_tensor(f"{tag}_o{r}", [P, U, D], F32)) for r in range(2)]
                got = [None]

                @block.gpsimd
                def _(pool):
                    got[0], run_gathers = gathers(
                        pool, tag, [(table, by_dst["idx"], stage_idx, ring),
                                    (edge_rows, by_dst["edge"], stage_edge, ering)], joined)
                    run_gathers()

                @block.vector
                def _(dve):
                    dve.memset(sums, 0.0).then_inc(cleared, 1)
                    dve.wait_ge(cleared, 1)
                    load = BlockWords(nc, dve, by_dst["words"], 4)

                    def step(s, r4, word):
                        r = r4 % 2
                        if past(s, 2) and within(s, BATCHES + 2):
                            q = s - 2
                            dve.wait_ge(projected, q + 1)
                            dve.tensor_tensor(zp[r][:], zp[r][:], ring[:, (r4 - 2) % RING, :, :], ALU.add
                                              ).then_inc(joined, 1)
                        if within(s, BATCHES) and past(s, 4):
                            dve.wait_ge(mixed, s - 3)
                        elif past(s, 4):
                            dve.wait_ge(mixed, s - 3)
                        block_of = load.blocks(word) if past(s, 4) else None
                        for k in range(U):
                            if within(s, BATCHES):
                                last = dve.tensor_scalar(hot[r4][:, k, :], lane[:],
                                                         by_dst["lo"][:, bass.ds(s * U + k, 1)], None, ALU.is_equal)
                                if k == U - 1:
                                    last.then_inc(hot_ready, 1)
                            if past(s, 4):
                                q = s - 4
                                acc = sums[:, bass.ds(block_of[k], 1), :].rearrange("p b f -> p (b f)")
                                dve.wait_ge(merged, q * U + k)
                                dve.tensor_tensor(acc, acc, op[r][:, k, :], ALU.add).then_inc(merged, 1)
                        if past(s, 3) and within(s, BATCHES + 3):
                            q, c = s - 3, 1 - r
                            dve.wait_ge(gate_ready, q + 1)
                            dve.wait_ge(split, q + 1)
                            dve.tensor_tensor(core[c], core[c], gate[c], ALU.mult).then_inc(sent, 1)
                        if past(s, 2) and within(s, BATCHES + 2):
                            q = s - 2
                            dve.wait_ge(logged, q + 1)
                            dve.scalar_tensor_tensor(gate[r], zp[r][:, :, 0:D], 0.0, soft[r][:, :, 0:D],
                                                     ALU.min, ALU.subtract)
                            dve.scalar_tensor_tensor(core[r], zp[r][:, :, D:2 * D], 0.0, soft[r][:, :, D:2 * D],
                                                     ALU.max, ALU.add).then_inc(split, 1)

                    steps(dve, BATCHES, RING, 4, step, load)

                @block.tensor
                def _(pe):
                    load = BlockWords(nc, pe, by_dst["words"], 1)

                    def step(s, r4, word):
                        r = r4 % 2
                        if within(s, BATCHES):
                            pe.wait_ge(hot_ready, s + 1)
                            arrived(pe, got[0], s, r4, 2 * 16 * U)
                            if past(s, 1):
                                pe.wait_ge(copied, s)
                            for k in range(U):
                                pe.transpose(tp[0][:, k, :], hot[r4][:, k, :], ident[:])
                                last = pe.transpose(tp[1][:, k, :], ering[:, r4, k, :], ident[:])
                            last.then_inc(turned, 1)
                        if past(s, 1) and within(s, BATCHES + 1):
                            q, c = s - 1, 1 - r
                            block_of = load.blocks(word)
                            pe.wait_ge(copied, q + 1)
                            if past(s, 3):
                                pe.wait_ge(split, q - 1)
                            for k in range(U):
                                pe.matmul(zp[c][:, k, :], edge_t[c][:, k, :], weights["edge"][:, :],
                                          start=True, stop=False)
                                for half, own in ((0, own_gate), (D, own_core)):
                                    last = pe.matmul(
                                        zp[c][:, k, half:half + D], hot_t[c][:, k, :],
                                        own[:, bass.ds(block_of[k], 1), :].rearrange("p b f -> p (b f)"),
                                        start=False, stop=(half > 0))
                            last.then_inc(projected, 1)
                        if past(s, 3):
                            q, c = s - 3, 1 - r
                            pe.wait_ge(sent, q + 1)
                            if past(s, 5):
                                pe.wait_ge(merged, (q - 1) * U)
                            for k in range(U):
                                last = pe.matmul(op[c][:, k, :], hot[(r4 - 3) % 4][:, k, :], core[c][:, k, :],
                                                 start=True, stop=True)
                            last.then_inc(mixed, 1)

                    steps(pe, BATCHES, RING, 3, step, load)

                @block.scalar
                def _(act):
                    act.preload_act_table_set("natural_log_exp_and_others")

                    def step(s, r4):
                        r = r4 % 2
                        if within(s, BATCHES):
                            act.wait_ge(turned, s + 1)
                            if past(s, 2):
                                act.wait_ge(projected, s - 1)
                            act.activation(hot_t[r], tp[0][:], ACT.Copy)
                            act.activation(edge_t[r], tp[1][:], ACT.Copy).then_inc(copied, 1)
                        if past(s, 3):
                            q, c = s - 3, 1 - r
                            act.wait_ge(split, q + 1)
                            act.activation(gate[c], gate[c], ACT.Exp).then_inc(gate_ready, 1)
                        if past(s, 2) and within(s, BATCHES + 2):
                            q = s - 2
                            act.wait_ge(joined, q + 1)
                            if past(s, 4):
                                act.wait_ge(mixed, q - 1)
                            act.activation(soft[r], zp[r][:], ACT.Abs).then_inc(chain, 1)
                            act.wait_ge(chain, q * 2 + 1)
                            act.activation(soft[r], soft[r], ACT.Exp, scale=-1.0).then_inc(chain, 1)
                            act.wait_ge(chain, q * 2 + 2)
                            act.activation(soft[r], soft[r], ACT.Ln, bias=1.0).then_inc(logged, 1)

                    steps(act, BATCHES, RING, 3, step)

        def by_node(tag, program, pool_program=None, act_program=None):
            chain = sem(f"{tag}_chain")
            with nc.Block() as block:
                @block.vector
                def _(dve):
                    count = [0]

                    def link(ins):
                        count[0] += 1
                        ins.then_inc(chain, 1)
                        dve.wait_ge(chain, count[0])

                    program(dve, link)
                if pool_program:
                    block.gpsimd(pool_program)
                if act_program:
                    block.scalar(act_program)

        live = lambda v: v[:, 0:BLKS, :]
        sums1 = slab_acc[:, 0:BLKS * (D + 1)].rearrange("p (b f) -> p b f", f=D + 1)
        message, weight = sums1[:, :, 0:D], sums1[:, :, D]
        own = sb("own", [P, BLKS])
        maxima = sb("maxima", [P, BLKS])
        node = sb("node", [P, 4, BLKS])
        spread_out = lambda a: a.unsqueeze(2).to_broadcast([P, BLKS, D])

        def own_scores(tag, table_sb):
            by_node(tag, lambda dve, link: link(dve.tensor_copy(own[:], table_sb[:, 0:BLKS, D + 2])))

        constants()
        place_edges("ps", io["src"], io["dst"], slab_acc, sorted_src, by_src, False)
        place_edges("pd", io["dst"], io["src"], slab_a, sorted_dst, by_dst, True,
                    scatter_of=("ss", slab_acc, sorted_src))
        load_sorted("ls", sorted_src, by_src, extra=lambda block: block.gpsimd(
            lambda pool: scatter(pool, "sd", slab_a, sorted_dst)))
        load_sorted("ld", sorted_dst, by_dst, with_loops=True)
        load_weights()

        release()

        att = blocks(slab_a, W_ATT)
        norm("n0")
        dense("d0", [h_v], [weights["l0"]], biases["l0"], W_ATT, target=att, table=tab0)
        own_scores("o0", att)
        attention("a0", tab0, by_src, own, sums1, True)

        def finish0(dve, link):
            link(dve.tensor_scalar(node[:, 0, :], weight, 0.0, None, ALU.is_equal))
            link(dve.tensor_tensor(node[:, 1, :], weight, node[:, 0, :], ALU.add))
            link(dve.reciprocal(node[:, 2, :], node[:, 1, :]))
            link(dve.tensor_tensor(message, message, spread_out(node[:, 2, :]), ALU.mult))
            link(dve.tensor_tensor(live(x_v), live(x_v), message, ALU.add))

        by_node("f0", finish0)

        release()

        norm("n1")
        dense("d1", [h_v], [weights["l1"]], biases["l1"], W_ATT, target=att, table=tab1)
        own_scores("o1", att)
        attention("a1", tab1, by_dst, own, sums1, False, maxima=maxima[:, :])

        topped, overall, scaled = sem("topped"), sem("overall"), sem("scaled")
        prod = blocks(slab_a)

        def finish1(dve, link):
            dve.tensor_reduce(node[:, 0, 0:1], maxima[:], AX.X, ALU.max).then_inc(topped, 1)
            dve.wait_ge(overall, 1)
            link(dve.tensor_scalar(node[:, 1, :], maxima[:], node[:, 0, 1:2], None, ALU.subtract))
            dve.wait_ge(scaled, 1)
            link(dve.tensor_tensor(node[:, 3, :], weight, node[:, 2, :], ALU.mult))
            link(dve.tensor_scalar(node[:, 3, :], node[:, 3, :], 1e-9, None, ALU.add))
            link(dve.reciprocal(node[:, 3, :], node[:, 3, :]))
            link(dve.tensor_tensor(node[:, 3, :], node[:, 3, :], node[:, 2, :], ALU.mult))
            link(dve.tensor_tensor(message, message, spread_out(node[:, 3, :]), ALU.mult))
            link(dve.memset(prod, 0.0))
            link(dve.tensor_tensor(live(prod), live(h_v), message, ALU.mult))

        def overall_max(pool):
            pool.wait_ge(topped, 1)
            pool.partition_all_reduce(node[:, 0, 1:2], node[:, 0, 0:1], P, RMAX).then_inc(overall, 1)

        def exp_scale(act):
            act.wait_ge(overall, 1)
            act.wait_ge(chain_of_f1[0], 1)
            act.activation(node[:, 2, :], node[:, 1, :], ACT.Exp, scale=1.0 - SLOPE).then_inc(scaled, 1)

        chain_of_f1 = [None]
        diff = sem("diff")

        def finish1_wrapped(dve, link):
            first = [True]

            def link1(ins):
                if first[0]:
                    first[0] = False
                    ins.then_inc(diff, 1)
                    return
                link(ins)

            finish1(dve, link1)

        chain_of_f1[0] = diff
        by_node("f1", finish1_wrapped, pool_program=overall_max, act_program=exp_scale)
        prod_w = blocks(slab_b)
        dense("d1b", [prod], [weights["l1w2"]], biases["l1w2"], D, target=prod_w)

        def finish1b(dve, link):
            link(dve.tensor_tensor(message, message, live(h_v), ALU.add))
            link(dve.tensor_tensor(message, message, live(prod_w), ALU.add))
            link(dve.scalar_tensor_tensor(message, message, SLOPE, message, ALU.mult, ALU.max))
            link(dve.tensor_tensor(live(x_v), live(x_v), message, ALU.add))

        by_node("f1b", finish1b)

        release()

        norm("n2")
        state = blocks(slab_a)
        sums2 = blocks(slab_acc)
        dense("d2", [h_v], [weights["pre"]], biases["pre"], D, target=state, table=tab2[0])
        for n in range(3):
            spread(f"r{n}", tab2[n], sums2)
            dense(f"u{n}", [sums2, state], [weights[f"agg{n}"], weights[f"own{n}"]], biases[f"u{n}"], D,
                  target=state, table=tab2[n + 1] if n < 2 else None, relu=True)
        by_node("f2", lambda dve, link: link(dve.tensor_tensor(x_v, x_v, state, ALU.add)))

        release()

        norm("n3")
        dense("d3s", [h_v], [weights["ts"]], None, 2 * D, table=tab3)
        own_gate, own_core = blocks(slab_a), blocks(slab_b)
        dense("d3d", [h_v], [weights["td"]], biases["td"], 2 * D, target=own_gate, target2=own_core)
        by_node("f3", lambda dve, link: link(dve.tensor_tensor(x_v, x_v, h_v, ALU.add)))
        gated("g3", tab3, io["edge"], own_gate, own_core, sums2)

        written, summed3 = sem("written"), sem("summed3")
        with nc.Block() as block:
            @block.vector
            def _(dve):
                dve.tensor_tensor(x_v, x_v, sums2, ALU.add).then_inc(summed3, 1)

            @block.sync
            def _(sp):
                sp.wait_ge(summed3, 1)
                sp.dma_start(out[0:(BLKS - 1) * P, :].rearrange("(b p) f -> p b f", p=P),
                             x_v[:, 0:BLKS - 1, :]).then_inc(written, 16)
                sp.dma_start(out[(BLKS - 1) * P:N, :], x_v[0:TAIL, BLKS - 1, :]).then_inc(written, 16)
                sp.wait_ge(written, 32)


def lay_out(inputs):
    import numpy as np
    c = np.ascontiguousarray
    i = {k: np.asarray(v) for k, v in inputs.items()}
    return {
        "x": c(i["x"]), "src": c(i["src"]), "dst": c(i["dst"]), "edge": c(i["edge_attr_128"]),
        "w0": c(i["L0_gnn_W"]), "w0_t": c(i["L0_gnn_W"].T),
        "a0": c(i["L0_gnn_a"].reshape(2, D)[::-1].T), "a1": c(i["L1_gnn_a"].reshape(2, D).T),
        "watt_t": c(i["L1_gnn_Watt_w"].T), "batt": c(i["L1_gnn_Watt_b"].reshape(D, 1)),
        "w1": c(i["L1_gnn_W1_w"]), "b1": c(i["L1_gnn_W1_b"].reshape(1, D)),
        "w2": c(i["L1_gnn_W2_w"]), "b2": c(i["L1_gnn_W2_b"].reshape(1, D)),
        "wpre": c(i["L2_gnn_W_pre"]), "bpre": c(i["L2_gnn_b_pre"].reshape(1, D)),
        "wconv_t": c(i["L2_gnn_W_conv"].transpose(0, 2, 1)), "bconv_t": c(i["L2_gnn_b_conv"].T),
        "wupd": c(i["L2_gnn_W_upd"]), "bupd": c(i["L2_gnn_b_upd"]),
        "wf": c(i["L3_gnn_W_f"]), "bf": c(i["L3_gnn_b_f"].reshape(1, D)),
        "ws": c(i["L3_gnn_W_s"]), "bs": c(i["L3_gnn_b_s"].reshape(1, D)),
    }


def kernel(**inputs):
    import concourse.bacc as bacc
    from concourse.bass_utils import run_bass_kernel_spmd

    nc = bacc.Bacc("TRN2", target_bir_lowering=False, num_devices=1)
    arrays, io = {}, {}
    for name, a in lay_out(inputs).items():
        arrays[f"in_{name}"] = a
        io[name] = nc.dram_tensor(f"in_{name}", a.shape, mybir.dt.from_np(a.dtype), kind="ExternalInput").ap()
    out = nc.dram_tensor("out", (N, D), F32, kind="ExternalOutput").ap()
    gnn(nc, io, out)
    r = run_bass_kernel_spmd(nc, [arrays], core_ids=[0])
    return r.results[0]["out"]
```

```python
from contextlib import ExitStack

import concourse.bass as bass
from concourse import mybir

F32 = mybir.dt.float32
BF16 = mybir.dt.bfloat16
I32 = mybir.dt.int32
ALU = mybir.AluOpType
ACT = mybir.ActivationFunctionType
AX = mybir.AxisListType
RMAX = bass.bass_isa.ReduceOp.max

P = 128
N = 6250
E = 106250
D = 128
BLKS = -(-N // P)
TAIL = N - (BLKS - 1) * P
NB = BLKS + 3
BUCKETS = BLKS + 1
COLS = 832
LASTROW = E - (P - 1) * COLS
PADS = P * COLS - E
PADKEY = BLKS * P
U = 4
RING = 4
ARING = 10
TILES = 880
BATCHES = TILES // U
PITCH = TILES + 1
ROWS = -(-E // P)
CHUNKS = -(-TILES // P)
ONCE = ROWS * P - E
assert ROWS + BLKS - 1 <= TILES and ROWS + BLKS + PADS // P <= PITCH and BATCHES % RING == BATCHES % ARING == BUCKETS % 2 == 0
REC = 4
FAR = -1.0e30
FLOOR = -1.0e28
SLOPE = 0.2
SU = 8
SR = 4
BESIDE = (COLS // SU - 20, 4, 8, 8)
SLAB = NB * 131 + 36
W_ATT = 131
DB = 2
DBATCHES = NB // DB


def steps(eng, count, ring, lag, step, load=None, head=None):
    def peeled(s):
        if load is None:
            step(s, s % ring)
        else:
            step(s, s % ring, load.words(s, 1)[0] if load.lag <= s < count + load.lag else None)

    head = head or -(-max(lag, 1) // ring)
    for s in range(head * ring):
        peeled(s)
    if count > head * ring:
        with eng.Fori(head, count // ring) as i:
            words = load.words(i * ring, ring) if load else None
            for r in range(ring):
                step(i * ring + r, r, *([words[r]] if load else []))
    for s in range(count, count + lag):
        peeled(s)


class BlockWords:

    def __init__(self, nc, eng, table, lag):
        self.nc, self.eng, self.table, self.lag = nc, eng, table, lag

    def words(self, s, n):
        return self.nc.values_load_multi_w_load_instructions(
            self.table[0:1, bass.ds(s - self.lag, n)], engines=[self.eng.engine], min_val=0, max_val=0x3F3F3F3F,
            skip_runtime_bounds_check_because="a word holds four numbers below 64")[1]

    def blocks(self, word):
        return [self.nc.s_assert_within(
            self.eng.snap((word >> (8 * k)) & 63), 0, BLKS - 1,
            skip_runtime_bounds_check_because="a tile's block is counted over BLKS - 1 blocks") for k in range(U)]


def past(s, lag):
    return not isinstance(s, int) or s >= lag


def within(s, count):
    return not isinstance(s, int) or s < count


def hold_wait(eng, passed):
    eng.sem_inc(passed, 1)


def gnn(nc, io, out):
    with ExitStack() as ctx:
        def sb(name, shape, dt=F32):
            return ctx.enter_context(nc.sbuf_tensor(name, shape, dt))

        def dram(name, shape, dt=F32):
            return nc.dram_tensor(name, shape, dt, kind="Internal").ap()

        in_use = []

        def sem(name):
            in_use.append(nc.alloc_semaphore(name=name))
            return in_use[-1]

        def release():
            nc.clear_and_free_semaphores(list(in_use))
            in_use.clear()
            nc.all_engine_barrier()

        slab_x = sb("slab_x", [P, SLAB])
        slab_h = sb("slab_h", [P, SLAB])
        slab_acc = sb("slab_acc", [P, SLAB])
        slab_a = sb("slab_a", [P, SLAB])
        slab_b = sb("slab_b", [P, SLAB])
        rings = sb("rings", [P, RING * U * 3 * D])
        rows, rows2 = rings[:, 0:RING * U * 2 * D], rings[:, RING * U * 2 * D:]

        def blocks(slab, width=D, n=NB):
            return slab[:, 0:n * width].rearrange("p (b f) -> p b f", f=width)

        x_v, h_v = blocks(slab_x), blocks(slab_h)

        ident = sb("ident", [P, P])
        quarter = sb("quarter", [P, P])
        ident_bf = sb("ident_bf", [P, P], BF16)
        far_bf = sb("far_bf", [P, P], BF16)
        tri = sb("tri", [P, P])
        lane = sb("lane", [P, P])
        lane_bf = sb("lane_bf", [P, P], BF16)
        ones = sb("ones", [P, P])
        stats = sb("stats", [P, 4, NB])

        by_src = {"idx": sb("src_idx", [P, TILES], I32), "lo": sb("src_lo", [P, TILES]),
                  "words": sb("src_words", [1, BATCHES], I32), "same": sb("src_same", [P, TILES])}
        by_dst = {"idx": sb("dst_idx", [P, TILES], I32), "lo": sb("dst_lo", [P, TILES]),
                  "words": sb("dst_words", [1, BATCHES], I32), "same": sb("dst_same", [P, TILES]),
                  "noloop": sb("dst_noloop", [P, TILES]), "edge": sb("dst_edge", [P, TILES], I32)}
        stage_idx = sb("stage_idx", [P, ARING, U], I32)
        stage_edge = sb("stage_edge", [P, RING, U], I32)

        sorted_src = dram("sorted_src", [P, PITCH * REC])
        sorted_dst = dram("sorted_dst", [P, PITCH * REC])
        pairs = dram("pairs", [ROWS + 1, 2 * P], I32)
        tab0 = dram("tab0", [NB * P, W_ATT])
        tab1 = dram("tab1", [NB * P, W_ATT])
        tab2 = [dram(f"tab2_{n}", [NB * P, D]) for n in range(3)]
        tab3 = dram("tab3", [NB * P, 2 * D])

        weights, biases = {}, {}
        for name, width in (("l0", W_ATT), ("l1", W_ATT), ("l1w2", D), ("pre", D), ("td", 2 * D), ("ts", 2 * D),
                            ("edge", 2 * D)) + tuple((f"{k}{n}", D) for n in range(3) for k in ("agg", "own")):
            weights[name] = sb(f"w_{name}", [P, width])
        for name, width in (("l0", W_ATT), ("l1", W_ATT), ("l1w2", D), ("pre", D), ("td", 2 * D),
                            ("u0", D), ("u1", D), ("u2", D)):
            biases[name] = sb(f"b_{name}", [P, width])

        def constants():
            made = sem("c_made")
            with nc.Block() as block:
                @block.gpsimd
                def _(pool):
                    pool.memset(ident[:], 0.0).then_inc(made, 1)
                    pool.memset(tri[:], 1.0).then_inc(made, 1)
                    pool.iota(lane[:], pattern=[[1, P]], base=0, channel_multiplier=0,
                              allow_small_or_imprecise_dtypes=True).then_inc(made, 1)
                    pool.iota(lane_bf[:], pattern=[[1, P]], base=0, channel_multiplier=0,
                              allow_small_or_imprecise_dtypes=True).then_inc(made, 1)
                    pool.iota(part[:], pattern=[[0, 1]], base=0, channel_multiplier=1,
                              allow_small_or_imprecise_dtypes=True)
                    pool.wait_ge(made, 4)
                    pool.affine_select(out=ident[:], in_=ident[:], compare_op=ALU.not_equal, fill=1.0, base=0,
                                       pattern=[[-1, P]], channel_multiplier=1).then_inc(made, 1)
                    pool.affine_select(out=tri[:], in_=tri[:], compare_op=ALU.is_gt, fill=0.0, base=0,
                                       pattern=[[1, P]], channel_multiplier=-1).then_inc(made, 1)

                @block.vector
                def _(dve):
                    dve.memset(ones[:], 1.0)
                    dve.wait_ge(made, 5)
                    dve.tensor_scalar(quarter[:], ident[:], 0.25, None, ALU.mult)
                    dve.tensor_copy(ident_bf[:], ident[:])
                    dve.tensor_scalar(far_bf[:], ident[:], 0.25 * FAR, None, ALU.mult)

        def sort_views(home):
            work = slab_b
            col = lambda n: work[:, n * COLS:(n + 1) * COLS]
            return {"record": home[:, 0:COLS * REC].rearrange("p (c w) -> p c w", w=REC),
                    "slot": home[:, COLS * REC:COLS * (REC + 1)].bitcast(I32),
                    "key": col(0).bitcast(I32), "nbr": col(1).bitcast(I32), "blk": col(2), "mask": col(3),
                    "scan": col(4), "pos": col(5), "int": col(6).bitcast(I32), "int2": col(7).bitcast(I32),
                    "mask2": col(6), "scan2": col(7)}

        cnt = sb("cnt", [P, 64])
        base = sb("base", [P, 64])
        start = sb("start", [P, 4])
        start_i = sb("start_i", [P, 2], I32)
        bucket = sb("bucket", [P, 8])
        part = sb("part", [P, 1])
        row_of = sb("row_of", [P, 8])
        row_idx = sb("row_idx", [P, 8], I32)
        in_order = sb("in_order", [P, 1], I32)
        pick = sb("pick", [P, P])

        def place_edges(tag, key_in, nbr_in, home, table, order, with_loops, scatter_of=None):
            v = sort_views(home)
            loaded, ready, chain = sem(f"{tag}_loaded"), sem(f"{tag}_ready"), sem(f"{tag}_chain")
            counted, placed, summed = sem(f"{tag}_counted"), sem(f"{tag}_placed"), sem(f"{tag}_summed")
            picked = sem(f"{tag}_picked")
            cleared, masked, passed = sem(f"{tag}_cleared"), sem(f"{tag}_masked"), sem(f"{tag}_passed")
            listed, numbered = sem(f"{tag}_listed"), sem(f"{tag}_numbered")
            fill = rows[:, 0:TILES * REC]
            past_end, tile_no = slab_h[:, 0:CHUNKS * P], slab_h[:, 1024:1024 + CHUNKS * P]
            row_no = slab_h[0:1, 2048:2048 + TILES]
            nowhere = slab_h[0:1, 3072:3072 + P].bitcast(I32)
            last_i, last_f = slab_h[:, 3300:3301].bitcast(I32), slab_h[:, 3301:3302]
            with ExitStack() as local, nc.Block() as block:
                tot = local.enter_context(nc.psum_tensor(f"{tag}_tot", [P, 512], F32))
                bas = local.enter_context(nc.psum_tensor(f"{tag}_bas", [P, 512], F32))
                til = local.enter_context(nc.psum_tensor(f"{tag}_til", [P, 2, 512], F32))
                rno = local.enter_context(nc.psum_tensor(f"{tag}_rno", [P, 2, 512], F32))

                @block.sync
                def _(sp):
                    sp.wait_ge(ready, 1)
                    for dst, src in ((v["key"], key_in), (v["nbr"], nbr_in)):
                        sp.dma_start(dst[0:P - 1, :], src[0:(P - 1) * COLS].rearrange("(p c) -> p c", c=COLS)
                                     ).then_inc(loaded, 16)
                        sp.dma_start(dst[P - 1:P, 0:LASTROW],
                                     src[(P - 1) * COLS:E].rearrange("(p c) -> p c", p=1)).then_inc(loaded, 16)
                    if with_loops:
                        sp.dma_start(last_i[1:P, :], key_in[0:(P - 1) * COLS].rearrange("(p c) -> p c", c=COLS)
                                     [:, COLS - 1:COLS], allow_slow_non_contiguous=True).then_inc(loaded, 16)
                        whole = (ROWS - 1) * P
                        for half, ends in ((0, key_in), (P, nbr_in)):
                            sp.dma_start(pairs[0:ROWS - 1, half:half + P],
                                         ends[0:whole].rearrange("(r c) -> r c", c=P)).then_inc(listed, 16)
                        sp.dma_start(pairs[ROWS - 1:ROWS, ONCE:P], key_in[whole:E].rearrange("(p c) -> p c", p=1)
                                     ).then_inc(listed, 16)
                        sp.dma_start(pairs[ROWS - 1:ROWS, 0:ONCE], nowhere[:, 0:ONCE]).then_inc(listed, 16)
                        sp.dma_start(pairs[ROWS - 1:ROWS, P:2 * P], nbr_in[E - P:E].rearrange("(p c) -> p c", p=1)
                                     ).then_inc(listed, 16)
                        sp.dma_start(pairs[ROWS:ROWS + 1, 0:P], nowhere).then_inc(listed, 16)
                        sp.dma_start(pairs[ROWS:ROWS + 1, P:2 * P], nbr_in[0:P].rearrange("(p c) -> p c", p=1)
                                     ).then_inc(listed, 16)
                        sp.wait_ge(listed, 7 * 16)
                        sp.wait_ge(ready, 3)
                        sp.dma_start(x_v[:, 0:BLKS - 1, :],
                                     io["x"][0:(BLKS - 1) * P, :].rearrange("(b p) f -> p b f", p=P)
                                     ).then_inc(listed, 16)
                        sp.dma_start(x_v[0:TAIL, BLKS - 1, :], io["x"][(BLKS - 1) * P:N, :]).then_inc(listed, 16)
                        sp.wait_ge(listed, 9 * 16)
                    sp.wait_ge(ready, 2)
                    sp.dma_start(table[:, 0:TILES * REC], fill).then_inc(cleared, 16)
                    sp.wait_ge(cleared, 16)

                @block.vector
                def _(dve):
                    count = [0]

                    def link(ins):
                        count[0] += 1
                        ins.then_inc(chain, 1)
                        dve.wait_ge(chain, count[0])

                    if with_loops:
                        dve.memset(last_i, 0)
                        dve.memset(nowhere, PADKEY)
                    dve.memset(v["key"], PADKEY)
                    dve.memset(v["nbr"], PADKEY).then_inc(ready, 1)
                    f = fill.rearrange("p (t w) -> p t w", w=REC)
                    link(dve.memset(f, 0.0))
                    dve.memset(f[:, :, 1:3], -1.0).then_inc(ready, 1)
                    if with_loops:
                        dve.memset(slab_x[:], 0.0).then_inc(ready, 1)
                    dve.wait_ge(loaded, 80 if with_loops else 64)
                    rec = v["record"]
                    link(dve.tensor_single_scalar(v["int"], v["key"], 7, ALU.logical_shift_right))
                    link(dve.tensor_copy(v["blk"], v["int"]))
                    link(dve.tensor_single_scalar(v["int2"], v["key"], P - 1, ALU.bitwise_and))
                    link(dve.tensor_scalar(v["scan"], v["blk"], float(BLKS), -1000.0, ALU.is_equal, ALU.mult))
                    link(dve.tensor_tensor(rec[:, :, 1], v["int2"], v["scan"], ALU.add))
                    link(dve.tensor_copy(rec[:, :, 0], v["nbr"]))
                    if with_loops:
                        link(dve.tensor_tensor(v["mask"], v["key"], v["nbr"], ALU.is_equal))
                        link(dve.scalar_tensor_tensor(rec[:, :, 2], v["mask"], -1000.0, rec[:, :, 1],
                                                      ALU.mult, ALU.add))
                        dve.wait_ge(placed, 1)
                        link(dve.tensor_scalar(rec[:, :, 3], v["int"], float(E - 1), None, ALU.min))
                    else:
                        link(dve.memset(rec[:, :, 2:4], 0.0))

                    if with_loops:
                        link(dve.tensor_tensor(v["scan"][:, 1:COLS], v["blk"][:, 0:COLS - 1], v["blk"][:, 1:COLS],
                                               ALU.is_gt))
                        link(dve.tensor_single_scalar(last_i, last_i, 7, ALU.logical_shift_right))
                        link(dve.tensor_copy(last_f, last_i))
                        link(dve.tensor_tensor(v["scan"][:, 0:1], last_f, v["blk"][:, 0:1], ALU.is_gt))
                        link(dve.tensor_reduce(bucket[:, 0:1], v["scan"], AX.X, ALU.add))
                    def count_step(s, r):
                        if past(s, 2):
                            dve.wait_ge(masked, s - 1)
                        dve.tensor_scalar(v[("mask", "pos")[r]], v["blk"], lane[:, bass.ds(s, 1)], 0.0,
                                          ALU.is_equal, ALU.add, accum_out=cnt[:, bass.ds(s, 1)]).then_inc(masked, 1)

                    steps(dve, BUCKETS, 2, 0, count_step)
                    dve.wait_ge(masked, BUCKETS)
                    link(dve.tensor_copy(cnt[:, BUCKETS:BUCKETS + 1], ones[:, 0:1]))
                    dve.tensor_copy(start[:, 3:4], ones[:, 0:1]).then_inc(counted, 1)
                    dve.wait_ge(summed, 1)
                    if with_loops:
                        link(dve.tensor_scalar(in_order[:, :], tot[:, 3:4], 0.0, None, ALU.is_equal))
                    number = lambda i: bucket[0:BUCKETS, i:i + 1]
                    dve.tensor_copy(number(1), tot[0:BUCKETS, 0:1]).then_inc(counted, 1)
                    dve.wait_ge(summed, 2)
                    link(dve.tensor_copy(number(2), tot[0:BUCKETS, 2:3]))
                    link(dve.tensor_tensor(number(3), number(2), number(1), ALU.add))
                    dve.tensor_copy(start_i[0:BUCKETS, 0:1], number(2))
                    link(dve.tensor_scalar(start_i[0:BUCKETS, 1:2], number(3), float(P - 1), None, ALU.add))
                    link(dve.tensor_single_scalar(start_i[0:BUCKETS, :], start_i[0:BUCKETS, :], 7,
                                                  ALU.logical_shift_right))
                    link(dve.tensor_copy(bucket[0:BUCKETS, 4:6], start_i[0:BUCKETS, :]))
                    link(dve.tensor_tensor(number(4), number(5), number(4), ALU.subtract))
                    link(dve.tensor_single_scalar(number(1), number(1), 0.0, ALU.is_gt))
                    if with_loops:
                        link(dve.tensor_scalar(number(5), number(5), float(P), None, ALU.mult))
                        link(dve.tensor_tensor(number(5), number(5), number(3), ALU.not_equal))
                        link(dve.tensor_tensor(number(5), number(5), number(1), ALU.mult))
                        link(dve.tensor_scalar(number(6), part[0:BUCKETS, :], float(BLKS - 1), float(2 * ROWS),
                                               ALU.is_equal, ALU.mult))
                        link(dve.tensor_tensor(number(6), number(6), number(5), ALU.subtract))
                    dve.tensor_tensor(start[0:BUCKETS, 0:1], number(4), number(1), ALU.mult).then_inc(counted, 1)
                    dve.wait_ge(summed, 3)
                    link(dve.tensor_copy(start[0:BUCKETS, 1:2], tot[0:BUCKETS, 1:2]))
                    link(dve.tensor_scalar(start[0:BUCKETS, 2:3], start[0:BUCKETS, 1:2], float(P), None, ALU.mult))
                    if with_loops:
                        link(dve.tensor_tensor(number(7), start[0:BUCKETS, 1:2], start[0:BUCKETS, 0:1], ALU.add))
                        dve.wait_ge(numbered, 2)
                        dve.tensor_scalar(past_end[0:BUCKETS, :], tile_no[0:BUCKETS, :], number(7), None, ALU.is_ge
                                          ).then_inc(counted, 1)
                        dve.wait_ge(summed, 4)
                        link(dve.tensor_tensor(row_of[:, 0:CHUNKS], row_of[:, 0:CHUNKS], tot[:, 8:8 + CHUNKS], ALU.add))
                        link(dve.tensor_scalar(row_idx[:, 0:CHUNKS], row_of[:, 0:CHUNKS], float(ROWS), None, ALU.min))
                        dve.tensor_tensor(row_no[:, 0:512], tile_no[0:1, 0:512], rno[0:1, 0, :], ALU.add)
                        link(dve.tensor_tensor(row_no[:, 512:TILES], tile_no[0:1, 512:TILES],
                                               rno[0:1, 1, 0:TILES - 512], ALU.add))
                        link(dve.tensor_scalar(order["edge"][0:1, :], row_no, float(P), float(E - P),
                                               ALU.mult, ALU.min))
                    dve.wait_ge(numbered, 2)
                    dve.tensor_scalar(v["pos"][0:BUCKETS, 0:COLS], tile_no[0:BUCKETS, 0:COLS],
                                      start[0:BUCKETS, 1:2], None, ALU.is_ge)
                    dve.tensor_scalar(v["mask"][0:BUCKETS, 0:TILES - COLS], tile_no[0:BUCKETS, COLS:TILES],
                                      start[0:BUCKETS, 1:2], None, ALU.is_ge).then_inc(counted, 1)
                    dve.wait_ge(summed, 5 if with_loops else 4)
                    link(dve.tensor_copy(base[:, 0:BUCKETS], bas[:, 0:BUCKETS]))
                    tb = rows2[:, 0:TILES]
                    dve.tensor_copy(tb[:, 0:512], til[:, 0, :])
                    link(dve.tensor_copy(tb[:, 512:TILES], til[:, 1, 0:TILES - 512]))
                    dve.memset(order["same"][:, 0:1], 0.0)
                    link(dve.tensor_tensor(order["same"][:, 1:TILES], tb[:, 1:TILES], tb[:, 0:TILES - 1],
                                           ALU.is_equal))
                    if with_loops:
                        link(dve.tensor_scalar(order["same"][:, :], order["same"][:, :], 1.0, -FAR,
                                               ALU.subtract, ALU.mult))
                    tbi = rows2[0:1, TILES:2 * TILES].bitcast(I32)
                    link(dve.tensor_copy(tbi, tb[0:1, :]))
                    quad = tbi.rearrange("p (b k) -> p b k", k=U)
                    link(dve.tensor_copy(order["words"][:, :], quad[:, :, 0]))
                    for k in range(1, U):
                        link(dve.tensor_single_scalar(quad[:, :, k], quad[:, :, k], 8 * k, ALU.logical_shift_left))
                        link(dve.tensor_tensor(order["words"][:, :], order["words"][:, :], quad[:, :, k],
                                               ALU.bitwise_or))
                    def place_pair(i):
                        done = i * 6 + BUCKETS
                        pair = [(i * 2 + u, v[("mask", "mask2")[u]], v[("scan", "scan2")[u]]) for u in range(2)]
                        for u, (b, mask, scan) in enumerate(pair):
                            if past(i, 1):
                                dve.wait_ge(masked, done - 1 + u)
                            dve.tensor_scalar(mask, v["blk"], lane[:, bass.ds(b, 1)], None, ALU.is_equal
                                              ).then_inc(masked, 1)
                        for u, (b, mask, scan) in enumerate(pair):
                            dve.wait_ge(masked, done + 1 + u)
                            dve.tensor_tensor_scan(scan, mask, mask, base[:, bass.ds(b, 1)],
                                                   ALU.add, ALU.max).then_inc(masked, 1)
                        for u, (b, mask, scan) in enumerate(pair):
                            dve.wait_ge(masked, done + 3 + 2 * u)
                            hold_wait(dve, passed)
                            dve.copy_predicated(v["pos"], mask.bitcast(I32), scan).then_inc(masked, 1)

                    place_pair(0)
                    with dve.Fori(1, BUCKETS // 2) as i:
                        place_pair(i)
                    dve.wait_ge(masked, 4 * BUCKETS)
                    link(dve.tensor_scalar(v["int"], v["pos"], -1.0, None, ALU.add))
                    link(dve.tensor_single_scalar(v["int2"], v["int"], P - 1, ALU.bitwise_and))
                    link(dve.tensor_single_scalar(v["int"], v["int"], 7, ALU.logical_shift_right))
                    link(dve.scalar_tensor_tensor(v["slot"], v["int2"], float(PITCH), v["int"], ALU.mult, ALU.add))

                @block.tensor
                def _(pe):
                    pe.wait_ge(counted, 1)
                    if with_loops:
                        pe.matmul(tot[:, 3:4], ones[:, :], bucket[:, 0:1], start=True, stop=True)
                    pe.matmul(tot[0:BUCKETS, 0:1], cnt[:, 0:BUCKETS], start[:, 3:4], start=True, stop=True
                              ).then_inc(summed, 1)
                    pe.wait_ge(counted, 2)
                    pe.matmul(tot[0:BUCKETS, 2:3], tri[0:BUCKETS, 0:BUCKETS], bucket[0:BUCKETS, 1:2],
                              start=True, stop=True).then_inc(summed, 1)
                    pe.wait_ge(counted, 3)
                    pe.matmul(tot[0:BUCKETS, 1:2], tri[0:BUCKETS, 0:BUCKETS], start[0:BUCKETS, 0:1],
                              start=True, stop=True).then_inc(summed, 1)
                    if with_loops:
                        pe.wait_ge(counted, 4)
                        for c in range(CHUNKS):
                            pe.matmul(tot[:, 8 + c:9 + c], past_end[0:BUCKETS, c * P:(c + 1) * P],
                                      bucket[0:BUCKETS, 6:7], start=True, stop=True)
                        weight_of = bucket[0:BUCKETS, 6:7].to_broadcast([BUCKETS, P])
                        pe.matmul(rno[:, 0, :], weight_of, past_end[0:BUCKETS, 0:512], start=True, stop=True)
                        pe.matmul(rno[:, 1, 0:TILES - 512], weight_of, past_end[0:BUCKETS, 512:TILES],
                                  start=True, stop=True).then_inc(summed, 1)
                    pe.wait_ge(counted, 5 if with_loops else 4)
                    pe.matmul(bas[:, 0:BUCKETS], tri[:, :], cnt[:, 0:BUCKETS], start=True, stop=False)
                    pe.matmul(bas[:, 0:BUCKETS], start[0:BUCKETS, 2:3].to_broadcast([BUCKETS, P]),
                              ident[0:BUCKETS, 0:BUCKETS], start=False, stop=True)
                    if not with_loops:
                        pe.wait_ge(picked, 2)
                    pk = pick[0:BUCKETS, :]
                    pe.matmul(til[:, 0, :], pk, v["pos"][0:BUCKETS, 0:512], start=True, stop=True)
                    pe.matmul(til[:, 1, 0:COLS - 512], pk, v["pos"][0:BUCKETS, 512:COLS], start=True, stop=True)
                    pe.matmul(til[:, 1, COLS - 512:TILES - 512], pk, v["mask"][0:BUCKETS, 0:TILES - COLS],
                              start=True, stop=True).then_inc(summed, 1)

                @block.gpsimd
                def _(pool):
                    pool.iota(row_of[:, :], pattern=[[P, 8]], base=0, channel_multiplier=1,
                              allow_small_or_imprecise_dtypes=True).then_inc(numbered, 1)
                    pool.iota(tile_no, pattern=[[1, CHUNKS * P]], base=0, channel_multiplier=0,
                              allow_small_or_imprecise_dtypes=True).then_inc(numbered, 1)
                    if with_loops:
                        pool.wait_ge(chain, 3)
                        pool.iota(v["int"], pattern=[[1, COLS]], base=0, channel_multiplier=COLS).then_inc(placed, 1)
                    else:
                        pool.memset(pick[:], 1.0).then_inc(placed, 1)
                        pool.wait_ge(placed, 1)
                        pool.affine_select(out=pick[:], in_=pick[:], compare_op=ALU.not_equal, fill=0.0, base=0,
                                           pattern=[[0, P]], channel_multiplier=1).then_inc(picked, 1)
                        pool.wait_ge(picked, 1)
                        pool.affine_select(out=pick[:], in_=pick[:], compare_op=ALU.not_equal, fill=0.0, base=-BLKS,
                                           pattern=[[0, P]], channel_multiplier=1).then_inc(picked, 1)
                    if scatter_of:
                        scatter(pool, *scatter_of)

        scatter_rec = sb("scatter_rec", [P, SR, SU * REC])
        scatter_slot = sb("scatter_slot", [P, SR, SU], I32)

        def scatter(pool, tag, home, table, first=0, count=COLS // SU):
            v = sort_views(home)
            staged, passed = sem(f"{tag}_staged"), sem(f"{tag}_passed")
            sent = [sem(f"{tag}_sent{r}") for r in range(SR)]
            record = home[:, 0:COLS * REC]
            target = table[:, :].rearrange("p (t w) -> (p t) w", w=REC)

            def step(s, r):
                if within(s, count):
                    if past(s, SR):
                        pool.wait_ge(sent[r], ((s - r) // SR) * (16 * SU) if isinstance(s, int)
                                     else (s - r) * (16 * SU // SR))
                    pool.tensor_copy(scatter_rec[:, r, :],
                                     record[:, bass.ds(s * (SU * REC) + first * SU * REC, SU * REC)])
                    pool.tensor_copy(scatter_slot[:, r, :], v["slot"][:, bass.ds(s * SU + first * SU, SU)]
                                     ).then_inc(staged, 1)
                if past(s, 1):
                    before = (r - 1) % SR
                    pool.wait_ge(staged, s)
                    hold_wait(pool, passed)
                    for k in range(SU):
                        pool.indirect_dma_start(
                            out=target,
                            out_offset=bass.IndirectOffsetOnAxis(ap=scatter_slot[:, before, k:k + 1], axis=0),
                            in_=scatter_rec[:, before, k * REC:(k + 1) * REC], in_offset=None
                        ).then_inc(sent[before], 16)

            steps(pool, count, SR, 1, step)
            for r in range(SR):
                pool.wait_ge(sent[r], 16 * SU * (count // SR))

        def beside(block, program):
            if program:
                block.gpsimd(program)

        def is_in_order(eng):
            return nc.values_load_multi_w_load_instructions(
                in_order[0:1, 0:1], engines=[eng.engine], min_val=0, max_val=1,
                skip_runtime_bounds_check_because="it is the outcome of a comparison")[1][0]

        def load_source_order():
            got, rowed, widened, turned, named = (sem(f"ls_{n}") for n in ("got", "rowed", "widened", "turned", "named"))
            raw = slab_b[:, 0:TILES * REC]
            words = raw.rearrange("p (t w) -> p t w", w=REC)
            row_ints = slab_h[:, 0:CHUNKS * 2 * P].bitcast(I32)
            row_floats = slab_h[:, CHUNKS * 2 * P:CHUNKS * 4 * P]
            nbr = slab_h[:, CHUNKS * 4 * P:CHUNKS * 4 * P + TILES]
            loop = slab_h[:, CHUNKS * 4 * P + TILES:CHUNKS * 4 * P + 2 * TILES]
            tile_block = rows2[:, 0:TILES]
            with ExitStack() as local, nc.Block() as block:
                ends = [local.enter_context(nc.psum_tensor(f"ls_end{i}", [P, 1024], F32)) for i in range(2)]

                @block.sync
                def _(sp):
                    sp.dma_start(raw, sorted_src[:, 0:TILES * REC]).then_inc(got, 16)

                @block.gpsimd
                def _(pool):
                    ordered = is_in_order(pool)
                    with pool.If(ordered == 0):
                        scatter(pool, "sd", slab_a, sorted_dst)
                    with pool.Else():
                        for c in range(CHUNKS):
                            pool.indirect_dma_start(
                                out=row_ints[:, c * 2 * P:(c + 1) * 2 * P], out_offset=None, in_=pairs,
                                in_offset=bass.IndirectOffsetOnAxis(ap=row_idx[:, c:c + 1], axis=0)
                            ).then_inc(rowed, 16)

                @block.tensor
                def _(pe):
                    ordered = is_in_order(pe)
                    with pe.If(ordered == 1):
                        pe.wait_ge(widened, 1)
                        for c in range(CHUNKS):
                            for i in range(2):
                                last = pe.transpose(ends[i][:, c * P:(c + 1) * P],
                                                    row_floats[:, (2 * c + i) * P:(2 * c + i + 1) * P], ident[:])
                        last.then_inc(turned, 1)

                @block.vector
                def _(dve):
                    dve.wait_ge(got, 16)
                    dve.tensor_copy(by_src["idx"][:, :], words[:, :, 0])
                    dve.tensor_copy(by_src["lo"][:, :], words[:, :, 1])
                    ordered = is_in_order(dve)
                    with dve.If(ordered == 1):
                        dve.wait_ge(rowed, 16 * CHUNKS)
                        dve.tensor_copy(row_floats, row_ints).then_inc(widened, 1)
                        dve.wait_ge(turned, 1)
                        dve.tensor_copy(by_dst["idx"][:, :], ends[1][:, 0:TILES])
                        dve.tensor_copy(nbr, ends[1][:, 0:TILES])
                        dve.scalar_tensor_tensor(by_dst["lo"][:, :], tile_block, -float(P), ends[0][:, 0:TILES],
                                                 ALU.mult, ALU.add).then_inc(named, 1)
                        dve.wait_ge(named, 1)
                        dve.tensor_tensor(loop, ends[0][:, 0:TILES], nbr, ALU.is_equal).then_inc(named, 1)
                        dve.wait_ge(named, 2)
                        dve.scalar_tensor_tensor(by_dst["noloop"][:, :], loop, -1000.0, by_dst["lo"][:, :],
                                                 ALU.mult, ALU.add)

        def load_destination_order():
            got = sem("ld_got")
            raw = slab_b[:, 0:TILES * REC]
            words = raw.rearrange("p (t w) -> p t w", w=REC)
            with nc.Block() as block:
                @block.sync
                def _(sp):
                    ordered = is_in_order(sp)
                    with sp.If(ordered == 0):
                        sp.dma_start(raw, sorted_dst[:, 0:TILES * REC]).then_inc(got, 16)

                @block.vector
                def _(dve):
                    ordered = is_in_order(dve)
                    with dve.If(ordered == 0):
                        dve.wait_ge(got, 16)
                        dve.tensor_copy(by_dst["idx"][:, :], words[:, :, 0])
                        dve.tensor_copy(by_dst["lo"][:, :], words[:, :, 1])
                        dve.tensor_copy(by_dst["noloop"][:, :], words[:, :, 2])
                        dve.tensor_copy(by_dst["edge"][:, :], words[:, :, 3])

        def load_weights(pool_program=None):
            got, multiplied = sem("w_got"), sem("w_multiplied")
            w0 = slab_b[:, 0:128]
            w1t = slab_b[:, 128:256]
            a01 = slab_b[:, 256:260]
            cols = slab_b[:, 260:264]
            wct = slab_b[:, 512:896].rearrange("p (n f) -> p n f", f=D)
            top = slab_b[:, 896:1280].rearrange("p (n f) -> p n f", f=D)
            filled = sem("w_filled")
            with ExitStack() as local, nc.Block() as block:
                beside(block, pool_program)
                ps = [local.enter_context(nc.psum_tensor(f"w_ps{i}", [P, 512], F32)) for i in range(5)]
                loads = [(w0, io["w0"]), (w1t, io["watt_t"]), (a01[:, 0:2], io["a0"]), (a01[:, 2:4], io["a1"]),
                         (weights["l0"][:, 0:D], io["w0_t"]), (weights["l1"][:, 0:D], io["w1"]),
                         (weights["l1w2"][:, :], io["w2"]), (weights["pre"][:, :], io["wpre"]),
                         (cols[:, 0:1], io["batt"]), (cols[:, 1:4], io["bconv_t"])]
                for n in range(3):
                    loads += [(wct[:, n, :], io["wconv_t"][n]), (top[:, n, :], io["wupd"][n, 0:D, :]),
                              (weights[f"own{n}"][:, :], io["wupd"][n, D:2 * D, :]),
                              (biases[f"u{n}"][:, :], io["bupd"][n:n + 1, :].to_broadcast([P, D]))]
                for i, name in enumerate(("td", "ts", "edge")):
                    loads += [(weights[name][:, 0:D], io["wf"][i * D:(i + 1) * D, :]),
                              (weights[name][:, D:2 * D], io["ws"][i * D:(i + 1) * D, :])]
                loads += [(biases["l1"][:, 0:D], io["b1"].to_broadcast([P, D])),
                          (biases["l1w2"][:, :], io["b2"].to_broadcast([P, D])),
                          (biases["pre"][:, :], io["bpre"].to_broadcast([P, D])),
                          (biases["td"][:, 0:D], io["bf"].to_broadcast([P, D])),
                          (biases["td"][:, D:2 * D], io["bs"].to_broadcast([P, D]))]

                @block.sync
                def _(sp):
                    for dst, src in loads:
                        sp.dma_start(dst, src).then_inc(got, 16)

                @block.tensor
                def _(pe):
                    pe.wait_ge(got, 16 * len(loads))
                    pe.matmul(ps[0][:, 0:2], w0, a01[:, 0:2], start=True, stop=True)
                    pe.matmul(ps[1][:, 0:2], w1t, a01[:, 2:4], start=True, stop=True)
                    pe.matmul(ps[1][:, 2:4], cols[:, 0:1].to_broadcast([P, P]), a01[:, 2:4], start=True, stop=True)
                    for n in range(3):
                        pe.matmul(ps[2 + n][:, 0:D], wct[:, n, :], top[:, n, :], start=True, stop=True)
                        last = pe.matmul(ps[2 + n][:, D:2 * D], cols[:, 1 + n:2 + n].to_broadcast([P, P]),
                                         top[:, n, :], start=True, stop=True)
                    last.then_inc(multiplied, 1)

                @block.vector
                def _(dve):
                    dve.memset(biases["l0"][:, :], 0.0).then_inc(filled, 1)
                    dve.memset(weights["l0"][:, D:D + 1], 0.0)
                    dve.memset(weights["l1"][:, D:D + 1], 0.0)
                    dve.memset(biases["l1"][:, D:D + 1], 1.0)
                    dve.wait_ge(filled, 1)
                    dve.memset(biases["l0"][:, D:D + 1], 1.0)
                    dve.wait_ge(multiplied, 1)
                    dve.tensor_copy(weights["l0"][:, D + 1:W_ATT], ps[0][:, 0:2])
                    dve.tensor_copy(weights["l1"][:, D + 1:W_ATT], ps[1][:, 0:2])
                    dve.tensor_copy(biases["l1"][:, D + 1:W_ATT], ps[1][:, 2:4])
                    for n in range(3):
                        dve.tensor_copy(weights[f"agg{n}"][:, :], ps[2 + n][:, 0:D])
                        dve.tensor_tensor(biases[f"u{n}"][:, :], ps[2 + n][:, D:2 * D], biases[f"u{n}"][:, :],
                                          ALU.add)

        def norm(tag, pool_program=None):
            chain, rooted = sem(f"{tag}_chain"), sem(f"{tag}_rooted")
            sq = blocks(slab_b)
            mean, var, std, inv = (stats[:, i, :] for i in range(4))
            wide = lambda a: a.unsqueeze(2).to_broadcast([P, a.shape[1], D])
            halves = (slice(0, NB // 2), slice(NB // 2, NB))
            squared = sem(f"{tag}_squared")
            with nc.Block() as block:
                beside(block, pool_program)

                @block.vector
                def _(dve):
                    count = [0]

                    def link(ins):
                        count[0] += 1
                        ins.then_inc(chain, 1)
                        dve.wait_ge(chain, count[0])

                    link(dve.tensor_reduce(mean, x_v, AX.X, ALU.add))
                    link(dve.tensor_scalar(mean, mean, 1.0 / D, None, ALU.mult))
                    for part in halves:
                        link(dve.tensor_tensor(h_v[:, part, :], x_v[:, part, :], wide(mean[:, part]), ALU.subtract))
                    for i, part in enumerate(halves):
                        dve.wait_ge(squared, i + 1)
                        link(dve.tensor_reduce(var[:, part], sq[:, part, :], AX.X, ALU.add))
                    link(dve.tensor_scalar(var, var, 1.0 / D, 1e-5, ALU.mult, ALU.add))
                    dve.wait_ge(rooted, 1)
                    link(dve.reciprocal(inv, std))
                    link(dve.scalar_tensor_tensor(h_v, h_v, 0.0, wide(inv), ALU.max, ALU.mult))

                @block.scalar
                def _(act):
                    for i, part in enumerate(halves):
                        act.wait_ge(chain, 3 + i)
                        act.activation(sq[:, part, :], h_v[:, part, :], ACT.Square).then_inc(squared, 1)
                    act.wait_ge(chain, 7)
                    act.activation(std, var, ACT.Sqrt).then_inc(rooted, 1)

        def dense(tag, sources, mats, bias, width, target=None, target2=None, table=None, relu=False,
                  own_column=None, pool_program=None):
            staged, turned, copied = sem(f"{tag}_staged"), sem(f"{tag}_turned"), sem(f"{tag}_copied")
            produced, evacuated, added = sem(f"{tag}_produced"), sem(f"{tag}_evacuated"), sem(f"{tag}_added")
            stored = [sem(f"{tag}_stored{r}") for r in range(2)]
            ns = len(sources)
            stage = [rows[:, r * 512:r * 512 + ns * DB * D].rearrange("p (i u f) -> p i u f", i=ns, u=DB)
                     for r in range(2)]
            tsb = [rows[:, 1024 + r * 512:1024 + r * 512 + ns * DB * D].rearrange("p (i f) -> p i f", f=P)
                   for r in range(2)]
            oring = [rows[:, 2048 + r * 512:2048 + r * 512 + DB * width].rearrange("p (u f) -> p u f", u=DB)
                     for r in range(2)]
            with ExitStack() as local, nc.Block() as block:
                beside(block, pool_program)
                tp = [local.enter_context(nc.psum_tensor(f"{tag}_tp{r}", [P, 4, P], F32)) for r in range(2)]
                op = [local.enter_context(nc.psum_tensor(f"{tag}_op{r}", [P, DB, 256], F32)) for r in range(2)]

                @block.scalar
                def _(act):
                    def step(s, r):
                        if within(s, DBATCHES):
                            if past(s, 2):
                                act.wait_ge(turned, s - 1)
                            for i, src in enumerate(sources):
                                last = act.activation(stage[r][:, i, :, :], src[:, bass.ds(s * DB, DB), :], ACT.Copy)
                            last.then_inc(staged, 1)
                        if past(s, 1):
                            q = s - 1
                            act.wait_ge(turned, q + 1)
                            if past(s, 3):
                                act.wait_ge(produced, q - 1)
                            act.activation(tsb[1 - r], tp[1 - r][:, 0:ns * DB, :], ACT.Copy).then_inc(copied, 1)

                    steps(act, DBATCHES, 2, 1, step)

                @block.tensor
                def _(pe):
                    def step(s, r):
                        if within(s, DBATCHES):
                            pe.wait_ge(staged, s + 1)
                            if past(s, 2):
                                pe.wait_ge(copied, s - 1)
                            for i in range(ns):
                                for u in range(DB):
                                    last = pe.transpose(tp[r][:, i * DB + u, :], stage[r][:, i, u, :], ident[:])
                            last.then_inc(turned, 1)
                        if past(s, 1):
                            q = s - 1
                            pe.wait_ge(copied, q + 1)
                            if past(s, 3):
                                pe.wait_ge(evacuated, q - 1)
                            for u in range(DB):
                                for i in range(ns):
                                    last = pe.matmul(op[1 - r][:, u, 0:width], tsb[1 - r][:, i * DB + u, :],
                                                     mats[i][:, :], start=(i == 0), stop=(i == ns - 1))
                            last.then_inc(produced, 1)

                    steps(pe, DBATCHES, 2, 1, step)

                @block.vector
                def _(dve):
                    def step(q, r):
                        dve.wait_ge(produced, q + 1)
                        if target is None and past(q, 2):
                            dve.wait_ge(stored[r], (q - r) * 8)
                        halves = ([(oring[r], 0, width)] if target is None else
                                  [(target[:, bass.ds(q * DB, DB), :], 0, width)] if target2 is None else
                                  [(t[:, bass.ds(q * DB, DB), :], i * D, D) for i, t in enumerate((target, target2))])
                        for dst, at, w in halves:
                            if bias is None:
                                last = dve.tensor_copy(dst, op[r][:, :, at:at + w])
                            else:
                                last = dve.tensor_tensor(dst, op[r][:, :, at:at + w],
                                                         bias[:, at:at + w].unsqueeze(1).to_broadcast([P, DB, w]),
                                                         ALU.add)
                        if relu:
                            last.then_inc(added, 1)
                            dve.wait_ge(added, q + 1)
                            last = dve.tensor_scalar(halves[0][0], halves[0][0], 0.0, None, ALU.max)
                        if own_column is not None:
                            last = dve.tensor_tensor(own[:, bass.ds(q * DB, DB)], op[r][:, :, own_column],
                                                     bias[:, own_column:own_column + 1].to_broadcast([P, DB]),
                                                     ALU.add)
                        last.then_inc(evacuated, 1)

                    steps(dve, DBATCHES, 2, 0, step)

                if table is not None:
                    trows = table.rearrange("(b p) f -> p b f", p=P)

                    @block.sync
                    def _(sp):
                        def step(q, r):
                            sp.wait_ge(evacuated, q + 1)
                            src = oring[r] if target is None else target[:, bass.ds(q * DB, DB), :]
                            sp.dma_start(trows[:, bass.ds(q * DB, DB), :], src).then_inc(stored[r], 16)

                        steps(sp, DBATCHES, 2, 0, step)
                        for r in range(2):
                            sp.wait_ge(stored[r], 16 * (DBATCHES // 2))

        def gathers(pool, tag, sources, freed, ring=RING):
            staged, passed = sem(f"{tag}_staged"), sem(f"{tag}_passed")

            def step(s, r):
                if within(s, BATCHES):
                    if past(s, ring):
                        for table, idx, stage, place, got in sources:
                            pool.wait_ge(got[r], (s // ring if isinstance(s, int) else (s - r) // ring) * (16 * U))
                    for table, idx, stage, place, got in sources:
                        last = pool.tensor_copy(stage[:, r, :], idx[:, bass.ds(s * U, U)])
                    last.then_inc(staged, 1)
                if past(s, 1):
                    q, before = s - 1, (r - 1) % ring
                    if past(s, ring + 1):
                        pool.wait_ge(freed, q - (ring - 1))
                    pool.wait_ge(staged, q + 1)
                    hold_wait(pool, passed)
                    for k in range(U):
                        for table, idx, stage, place, got in sources:
                            pool.indirect_dma_start(
                                out=place[:, before, k, :], out_offset=None, in_=table,
                                in_offset=bass.IndirectOffsetOnAxis(ap=stage[:, before, k:k + 1], axis=0)
                            ).then_inc(got[before], 16)

            steps(pool, BATCHES, ring, 1, step, head=2)

        def arrived(eng, got, s, r, per):
            ring = len(got)
            eng.wait_ge(got[r], (s // ring + 1) * per if isinstance(s, int) else (s - r) // ring * per + per)

        def attention(tag, table, order, own, sums, floor_at_zero, maxima=None):
            mask_ready, scored, leaky = sem(f"{tag}_mask"), sem(f"{tag}_scored"), sem(f"{tag}_leaky")
            positive, passed = sem(f"{tag}_positive"), sem(f"{tag}_dve_passed")
            shift, chain, probs = sem(f"{tag}_shift"), sem(f"{tag}_chain"), sem(f"{tag}_probs")
            turned, copied, mixed = sem(f"{tag}_turned"), sem(f"{tag}_copied"), sem(f"{tag}_mixed")
            merged, cleared = sem(f"{tag}_merged"), sem(f"{tag}_cleared")
            ring = rings[:, 0:ARING * U * W_ATT].rearrange("p (r k f) -> p r k f", r=ARING, k=U)
            at = [0]

            def work(n):
                at[0] += n
                return slab_b[:, at[0] - n:at[0]]

            tiles4 = lambda a: a.rearrange("p (k e) -> p k e", k=U)
            mask = [tiles4(work(U * P // 2).bitcast(BF16)) for _ in range(2)]
            score = [tiles4(work(U * P)) for _ in range(2)]
            prob = [tiles4(work(U * P)) for _ in range(2)]
            prob_t = [tiles4(work(U * P)) for _ in range(2)]
            top = [work(U) for _ in range(2)]
            run = [work(U + 1) for _ in range(5)]
            drop = [work(U) for _ in range(2)]
            minus = [work(U) for _ in range(2)]
            decay = [work(U) for _ in range(5)]
            op0 = ALU.mult if floor_at_zero else ALU.add
            lanes_bf = lane_bf[:].unsqueeze(1).to_broadcast([P, U, P])
            K = 4
            with ExitStack() as local, nc.Block() as block:
                xp = [local.enter_context(nc.psum_tensor(f"{tag}_x{r}", [P, U, P], F32)) for r in range(2)]
                tp = local.enter_context(nc.psum_tensor(f"{tag}_t", [P, U, P], F32))
                op = [local.enter_context(nc.psum_tensor(f"{tag}_o{r}", [P, U, 256], F32)) for r in range(2)]
                got = [sem(f"{tag}_got{r}") for r in range(ARING)]

                @block.gpsimd
                def _(pool):
                    gathers(pool, tag, [(table, order["idx"], stage_idx, ring, got)], mixed, ARING)

                @block.vector
                def _(dve):
                    dve.memset(sums, 0.0)
                    if maxima is not None:
                        dve.memset(maxima, FAR)
                    dve.memset(run[4], 0.0).then_inc(cleared, 1)
                    dve.wait_ge(cleared, 1)
                    load = BlockWords(nc, dve, order["words"], 4)

                    def step(s, rr, word):
                        r = rr % 2
                        block_of = load.blocks(word) if past(s, 4) else None
                        if within(s, BATCHES):
                            lo = order["lo"][:, bass.ds(s * U, U)].unsqueeze(2).to_broadcast([P, U, P])
                            if past(s, 2):
                                dve.wait_ge(scored, s - 1)
                            dve.tensor_tensor(mask[r], lanes_bf, lo, ALU.not_equal).then_inc(mask_ready, 1)
                        if past(s, 4):
                            dve.wait_ge(mixed, s - 3)

                        def merge(k):
                            if not past(s, 4):
                                return
                            q = s - 4
                            acc = sums[:, bass.ds(block_of[k], 1), :].rearrange("p b f -> p (b f)")
                            dve.wait_ge(merged, q * U + k)
                            if maxima is not None:
                                dve.tensor_copy(maxima[:, bass.ds(block_of[k], 1)],
                                                run[(rr - 4) % 5][:, k + 1:k + 2])
                            dve.scalar_tensor_tensor(acc, acc, decay[(rr - 4) % 5][:, k:k + 1],
                                                     op[r][:, k, 0:D + 1], ALU.mult, ALU.add).then_inc(merged, 1)

                        if not (past(s, 1) and within(s, BATCHES + 1)):
                            for k in range(U):
                                merge(k)
                            return
                        merge(0)
                        q, c, now, before = s - 1, 1 - r, (rr - 1) % 5, (rr - 2) % 5
                        same = order["same"][:, bass.ds(q * U, U)]

                        def link(ins, n):
                            ins.then_inc(chain, 1)
                            return q * K + n

                        dve.wait_ge(positive, q + 1)
                        hold_wait(dve, passed)
                        for k in range(U):
                            last = dve.tensor_tensor_reduce(
                                out=score[c][:, k, :], in0=xp[c][:, k, :], in1=score[c][:, k, :], scale=1.0,
                                scalar=FLOOR, op0=ALU.add, op1=ALU.max, accum_out=top[c][:, k:k + 1])
                        last.then_inc(leaky, 1)
                        carried = link(dve.tensor_copy(run[now][:, 0:1], run[before][:, U:U + 1]), 1)
                        merge(1)
                        dve.wait_ge(leaky, q + 1)
                        dve.wait_ge(chain, carried)
                        scanned = link(dve.tensor_tensor_scan(run[now][:, 1:U + 1], same, top[c], run[now][:, 0:1],
                                                              op0, ALU.max), 2)
                        merge(2)
                        dve.wait_ge(chain, scanned)
                        if past(s, 3):
                            dve.wait_ge(probs, q - 1)
                        kept = link(dve.tensor_tensor(drop[c], run[now][:, 0:U], same, op0), 3)
                        dve.tensor_scalar(minus[c], run[now][:, 1:U + 1], -(1.0 - SLOPE), None, ALU.mult
                                          ).then_inc(shift, 1)
                        merge(3)
                        dve.wait_ge(chain, kept)
                        link(dve.tensor_tensor(drop[c], drop[c], run[now][:, 1:U + 1], ALU.subtract), 4)

                    steps(dve, BATCHES, ARING, 4, step, load)

                @block.tensor
                def _(pe):
                    load = BlockWords(nc, pe, order["words"], 0)

                    def step(s, rr, word):
                        r = rr % 2
                        if within(s, BATCHES):
                            block_of = load.blocks(word)
                            pe.wait_ge(mask_ready, s + 1)
                            arrived(pe, got, s, rr, 16 * U)
                            if past(s, 2):
                                pe.wait_ge(leaky, s - 1)
                            for k in range(U):
                                pe.matmul(xp[r][:, k, :], mask[r][:, k, :], far_bf[:], start=True, stop=False)
                                pe.matmul(xp[r][:, k, :], ring[:, rr, k, D + 1:D + 2].to_broadcast([P, P]),
                                          quarter[:], start=False, stop=False)
                                last = pe.matmul(xp[r][:, k, :], quarter[:],
                                                 own[:, bass.ds(block_of[k], 1)].to_broadcast([P, P]),
                                                 start=False, stop=True)
                            last.then_inc(scored, 1)
                        if past(s, 2) and within(s, BATCHES + 2):
                            q = s - 2
                            pe.wait_ge(probs, q + 1)
                            if past(s, 3):
                                pe.wait_ge(copied, q)
                            for k in range(U):
                                last = pe.transpose(tp[:, k, :], prob[r][:, k, :], ident[:])
                            last.then_inc(turned, 1)
                        if past(s, 3):
                            q, c = s - 3, 1 - r
                            pe.wait_ge(copied, q + 1)
                            if past(s, 5):
                                pe.wait_ge(merged, (q - 1) * U)
                            for k in range(U):
                                last = pe.matmul(op[c][:, k, 0:D + 1], prob_t[c][:, k, :],
                                                 ring[:, (rr - 3) % ARING, k, 0:D + 1], start=True, stop=True)
                            last.then_inc(mixed, 1)

                    steps(pe, BATCHES, ARING, 3, step, load)

                @block.scalar
                def _(act):
                    def step(s, rr):
                        r = rr % 2
                        if within(s, BATCHES):
                            act.wait_ge(scored, s + 1)
                            if past(s, 2):
                                act.wait_ge(probs, s - 1)
                            act.activation(score[r], xp[r][:], ACT.Relu, scale=4.0).then_inc(positive, 1)
                        if past(s, 1) and within(s, BATCHES + 1):
                            q, c = s - 1, 1 - r
                            act.wait_ge(shift, q + 1)
                            if past(s, 3):
                                act.wait_ge(turned, q - 1)
                            if past(s, 6):
                                act.wait_ge(merged, (q - 4) * U)
                            for k in range(U):
                                act.activation(prob[c][:, k, :], score[c][:, k, :], ACT.Exp,
                                               bias=minus[c][:, k:k + 1], scale=1.0 - SLOPE)
                            act.wait_ge(chain, (q + 1) * K)
                            act.activation(decay[(rr - 1) % 5], drop[c], ACT.Exp, scale=1.0 - SLOPE
                                           ).then_inc(probs, 1)
                        if past(s, 2):
                            q = s - 2
                            act.wait_ge(turned, q + 1)
                            if past(s, 4):
                                act.wait_ge(mixed, q - 1)
                            act.activation(prob_t[r], tp[:], ACT.Copy).then_inc(copied, 1)

                    steps(act, BATCHES, ARING, 2, step)

        def spread(tag, table, sums):
            hot_ready, mixed, merged, cleared = (sem(f"{tag}_{n}") for n in ("hot", "mixed", "merged", "cleared"))
            ring = rows[:, 0:RING * U * D].rearrange("p (r k f) -> p r k f", r=RING, k=U)
            hot = [rows2[:, r * U * P:(r + 1) * U * P].rearrange("p (k e) -> p k e", k=U) for r in range(2)]
            with ExitStack() as local, nc.Block() as block:
                op = [local.enter_context(nc.psum_tensor(f"{tag}_o{r}", [P, U, D], F32)) for r in range(2)]
                got = [sem(f"{tag}_got{r}") for r in range(RING)]

                @block.gpsimd
                def _(pool):
                    gathers(pool, tag, [(table, by_dst["idx"], stage_idx, ring, got)], mixed)

                @block.vector
                def _(dve):
                    dve.memset(sums, 0.0).then_inc(cleared, 1)
                    dve.wait_ge(cleared, 1)
                    load = BlockWords(nc, dve, by_dst["words"], 2)

                    def step(s, r, word):
                        r = r % 2
                        if past(s, 2):
                            dve.wait_ge(mixed, s - 1)
                        block_of = load.blocks(word) if past(s, 2) else None
                        for k in range(U):
                            if within(s, BATCHES):
                                last = dve.tensor_scalar(hot[r][:, k, :], lane[:],
                                                         by_dst["noloop"][:, bass.ds(s * U + k, 1)], None,
                                                         ALU.is_equal)
                                if k == U - 1:
                                    last.then_inc(hot_ready, 1)
                            if past(s, 2):
                                q = s - 2
                                acc = sums[:, bass.ds(block_of[k], 1), :].rearrange("p b f -> p (b f)")
                                dve.wait_ge(merged, q * U + k)
                                dve.tensor_tensor(acc, acc, op[r][:, k, :], ALU.add).then_inc(merged, 1)

                    steps(dve, BATCHES, RING, 2, step, load)

                @block.tensor
                def _(pe):
                    def step(s, r4):
                        r = r4 % 2
                        pe.wait_ge(hot_ready, s + 1)
                        arrived(pe, got, s, r4, 16 * U)
                        if past(s, 2):
                            pe.wait_ge(merged, (s - 1) * U)
                        for k in range(U):
                            last = pe.matmul(op[r][:, k, :], hot[r][:, k, :], ring[:, r4, k, :], start=True, stop=True)
                        last.then_inc(mixed, 1)

                    steps(pe, BATCHES, RING, 0, step)

        def gated(tag, table, edge_rows, own_gate, own_core, sums):
            hot_ready, turned, copied, joined = (sem(f"{tag}_{n}") for n in ("hot", "turned", "copied", "joined"))
            projected = sem(f"{tag}_projected")
            logged, split, gate_ready, sent = (sem(f"{tag}_{n}") for n in ("logged", "split", "gate", "sent"))
            mixed, merged, cleared, chain = (sem(f"{tag}_{n}") for n in ("mixed", "merged", "cleared", "chain"))
            ring = rows[:, :].rearrange("p (r k f) -> p r k f", r=RING, k=U)
            ering = rows2[:, :].rearrange("p (r k f) -> p r k f", r=RING, k=U)
            home = slab_h
            lanes = lambda a: a[:].unsqueeze(1).to_broadcast([P, U, P])
            pos = [0]

            def work(n):
                pos[0] += n
                assert pos[0] <= SLAB
                return home[:, pos[0] - n:pos[0]]

            tiles4 = lambda a: a.rearrange("p (k e) -> p k e", k=U)
            hot_bf = [tiles4(work(256).bitcast(BF16)) for _ in range(2)]
            hot = [tiles4(a[:, 0:512]) for a in (by_src["lo"], by_src["same"], by_dst["noloop"],
                                                 by_src["idx"][:, :].bitcast(F32))]
            hot_t = [tiles4(work(512)) for _ in range(2)]
            edge_t = [tiles4(work(512)) for _ in range(2)]
            soft = [tiles4(work(1024)) for _ in range(2)]
            both = [tiles4(work(1024)) for _ in range(2)]
            gate = [a[:, :, 0:D] for a in soft]
            core = [a[:, :, D:2 * D] for a in soft]
            with ExitStack() as local, nc.Block() as block:
                tp = [local.enter_context(nc.psum_tensor(f"{tag}_t{r}", [P, U, P], F32)) for r in range(2)]
                zp = [local.enter_context(nc.psum_tensor(f"{tag}_z{r}", [P, U, 2 * D], F32)) for r in range(2)]
                op = [local.enter_context(nc.psum_tensor(f"{tag}_o{r}", [P, U, D], F32)) for r in range(2)]
                got, edge_got = ([sem(f"{tag}_{what}{r}") for r in range(RING)] for what in ("got", "edge_got"))

                @block.gpsimd
                def _(pool):
                    from_table = (table, by_dst["idx"], stage_idx, ring, got)
                    from_edges = (edge_rows, by_dst["edge"], stage_edge, ering, edge_got)
                    ordered = is_in_order(pool)
                    with pool.If(ordered == 0):
                        gathers(pool, tag, [from_table, from_edges], joined)
                    with pool.Else():
                        gathers(pool, tag + "o", [from_table], joined)

                @block.sync
                def _(sp):
                    def step(s, r):
                        if past(s, RING):
                            sp.wait_ge(joined, s - (RING - 1))
                        first = nc.values_load_multi_w_load_instructions(
                            by_dst["edge"][0:1, bass.ds(s * U, U)], engines=[sp.engine], min_val=0, max_val=E - P,
                            skip_runtime_bounds_check_because="the first edges are clamped to E - P")[1]
                        for k in range(U):
                            sp.dma_start(ering[:, r, k, :], edge_rows[bass.ds(first[k], P), :]
                                         ).then_inc(edge_got[r], 16)

                    ordered = is_in_order(sp)
                    with sp.If(ordered == 1):
                        steps(sp, BATCHES, RING, 0, step)

                @block.vector
                def _(dve):
                    dve.memset(sums, 0.0).then_inc(cleared, 1)
                    dve.wait_ge(cleared, 1)
                    load = BlockWords(nc, dve, by_dst["words"], 5)

                    def numbers(s):
                        return by_dst["lo"][:, bass.ds(s * U, U)].unsqueeze(2).to_broadcast([P, U, P])

                    def step(s, r4, word):
                        r = r4 % 2
                        block_of = load.blocks(word) if past(s, 5) else None

                        def merge(*tiles):
                            for k in tiles if past(s, 5) else ():
                                acc = sums[:, bass.ds(block_of[k], 1), :].rearrange("p b f -> p (b f)")
                                dve.wait_ge(merged, (s - 5) * U + k)
                                dve.tensor_tensor(acc, acc, op[1 - r][:, k, :], ALU.add).then_inc(merged, 1)

                        if past(s, 4) and within(s, BATCHES + 4):
                            q = s - 4
                            dve.wait_ge(logged, q + 1)
                            dve.scalar_tensor_tensor(gate[r], both[r][:, :, 0:D], 0.0, soft[r][:, :, 0:D],
                                                     ALU.min, ALU.subtract)
                            dve.scalar_tensor_tensor(core[r], both[r][:, :, D:2 * D], 0.0, soft[r][:, :, D:2 * D],
                                                     ALU.max, ALU.add).then_inc(split, 1)
                        if past(s, 5):
                            dve.wait_ge(mixed, s - 4)
                        merge(0)
                        merge(1, 2)
                        if past(s, 4) and within(s, BATCHES + 4):
                            dve.wait_ge(gate_ready, q + 1)
                            dve.wait_ge(split, q + 1)
                            dve.tensor_tensor(core[r], core[r], gate[r], ALU.mult).then_inc(sent, 1)
                        merge(3)
                        if within(s, BATCHES):
                            if past(s, 2):
                                dve.wait_ge(copied, s - 1)
                            dve.tensor_tensor(hot_bf[r], lanes(lane_bf), numbers(s), ALU.is_equal
                                              ).then_inc(hot_ready, 1)
                        if past(s, 2) and within(s, BATCHES + 2):
                            dve.wait_ge(projected, s - 1)
                            dve.tensor_tensor(both[r], zp[r][:], ring[:, (r4 - 2) % RING, :, :], ALU.add
                                              ).then_inc(joined, 1)

                    steps(dve, BATCHES, RING, 5, step, load)

                @block.tensor
                def _(pe):
                    load = BlockWords(nc, pe, by_dst["words"], 1)

                    def step(s, r4, word):
                        r = r4 % 2
                        if within(s, BATCHES):
                            pe.wait_ge(hot_ready, s + 1)
                            arrived(pe, got, s, r4, 16 * U)
                            arrived(pe, edge_got, s, r4, 16 * U)
                            if past(s, 1):
                                pe.wait_ge(copied, s)
                            for k in range(U):
                                pe.matmul(tp[0][:, k, :], hot_bf[r][:, k, :], ident_bf[:], start=True, stop=True)
                                last = pe.transpose(tp[1][:, k, :], ering[:, r4, k, :], ident[:])
                            last.then_inc(turned, 1)
                        if past(s, 1) and within(s, BATCHES + 1):
                            q, c = s - 1, 1 - r
                            block_of = load.blocks(word)
                            pe.wait_ge(copied, q + 1)
                            if past(s, 3):
                                pe.wait_ge(joined, q - 1)
                            for k in range(U):
                                pe.matmul(zp[c][:, k, :], edge_t[c][:, k, :], weights["edge"][:, :],
                                          start=True, stop=False)
                                for half, own in ((0, own_gate), (D, own_core)):
                                    last = pe.matmul(
                                        zp[c][:, k, half:half + D], hot_t[c][:, k, :],
                                        own[:, bass.ds(block_of[k], 1), :].rearrange("p b f -> p (b f)"),
                                        start=False, stop=(half > 0))
                            last.then_inc(projected, 1)
                        if past(s, 3):
                            q, c = s - 3, 1 - r
                            pe.wait_ge(sent, q + 1)
                            if past(s, 5):
                                pe.wait_ge(merged, (q - 1) * U)
                            for k in range(U):
                                last = pe.matmul(op[c][:, k, :], hot[(r4 - 3) % RING][:, k, :], core[c][:, k, :],
                                                 start=True, stop=True)
                            last.then_inc(mixed, 1)

                    steps(pe, BATCHES, RING, 3, step, load)

                @block.scalar
                def _(act):
                    act.preload_act_table_set("natural_log_exp_and_others")

                    def step(s, r4):
                        r = r4 % 2
                        if within(s, BATCHES):
                            act.wait_ge(hot_ready, s + 1)
                            if past(s, RING):
                                act.wait_ge(mixed, s - (RING - 1))
                            act.activation(hot[r4], hot_bf[r], ACT.Copy)
                            act.wait_ge(turned, s + 1)
                            if past(s, 2):
                                act.wait_ge(projected, s - 1)
                            act.activation(hot_t[r], tp[0][:], ACT.Copy)
                            act.activation(edge_t[r], tp[1][:], ACT.Copy).then_inc(copied, 1)
                        if past(s, 3):
                            q, c = s - 3, 1 - r
                            act.wait_ge(split, q + 1)
                            act.activation(gate[c], gate[c], ACT.Exp).then_inc(gate_ready, 1)
                        if past(s, 2) and within(s, BATCHES + 2):
                            q = s - 2
                            act.wait_ge(joined, q + 1)
                            if past(s, 4):
                                act.wait_ge(mixed, q - 1)
                            act.activation(soft[r], both[r], ACT.Abs).then_inc(chain, 1)
                            act.wait_ge(chain, q * 2 + 1)
                            act.activation(soft[r], soft[r], ACT.Exp, scale=-1.0).then_inc(chain, 1)
                            act.wait_ge(chain, q * 2 + 2)
                            act.activation(soft[r], soft[r], ACT.Ln, bias=1.0).then_inc(logged, 1)

                    steps(act, BATCHES, RING, 3, step)

        def by_node(tag, program, pool_program=None, act_program=None):
            chain = sem(f"{tag}_chain")
            with nc.Block() as block:
                @block.vector
                def _(dve):
                    count = [0]

                    def link(ins):
                        count[0] += 1
                        ins.then_inc(chain, 1)
                        dve.wait_ge(chain, count[0])

                    program(dve, link)
                if pool_program:
                    block.gpsimd(pool_program)
                if act_program:
                    block.scalar(act_program)

        live = lambda v: v[:, 0:BLKS, :]
        sums1 = slab_acc[:, 0:BLKS * (D + 1)].rearrange("p (b f) -> p b f", f=D + 1)
        message, weight = sums1[:, :, 0:D], sums1[:, :, D]
        own = sb("own", [P, NB])
        maxima = sb("maxima", [P, BLKS])
        node = sb("node", [P, 4, BLKS])
        spread_out = lambda a: a.unsqueeze(2).to_broadcast([P, BLKS, D])

        constants()
        place_edges("ps", io["src"], io["dst"], slab_acc, sorted_src, by_src, False)
        place_edges("pd", io["dst"], io["src"], slab_a, sorted_dst, by_dst, True,
                    scatter_of=("ss0", slab_acc, sorted_src, 0, BESIDE[0]))

        def scatter_part(n):
            return lambda pool: scatter(pool, f"ss{n}", slab_acc, sorted_src, sum(BESIDE[:n]), BESIDE[n])

        load_weights(scatter_part(1))
        norm("n0", scatter_part(2))
        dense("d0", [h_v], [weights["l0"]], biases["l0"], W_ATT, table=tab0, own_column=D + 2,
              pool_program=scatter_part(3))
        load_source_order()
        load_destination_order()

        release()

        attention("a0", tab0, by_src, own, sums1, True)

        def finish0(dve, link):
            link(dve.tensor_scalar(node[:, 0, :], weight, 0.0, None, ALU.is_equal))
            link(dve.tensor_tensor(node[:, 1, :], weight, node[:, 0, :], ALU.add))
            link(dve.reciprocal(node[:, 2, :], node[:, 1, :]))
            link(dve.tensor_tensor(message, message, spread_out(node[:, 2, :]), ALU.mult))
            link(dve.tensor_tensor(live(x_v), live(x_v), message, ALU.add))

        by_node("f0", finish0)

        release()

        norm("n1")
        dense("d1", [h_v], [weights["l1"]], biases["l1"], W_ATT, table=tab1, own_column=D + 2)
        attention("a1", tab1, by_dst, own, sums1, False, maxima=maxima[:, :])

        topped, overall, scaled = sem("topped"), sem("overall"), sem("scaled")
        prod = blocks(slab_a)

        def finish1(dve, link):
            dve.tensor_reduce(node[:, 0, 0:1], maxima[:], AX.X, ALU.max).then_inc(topped, 1)
            dve.wait_ge(overall, 1)
            link(dve.tensor_scalar(node[:, 1, :], maxima[:], node[:, 0, 1:2], None, ALU.subtract))
            dve.wait_ge(scaled, 1)
            link(dve.tensor_tensor(node[:, 3, :], weight, node[:, 2, :], ALU.mult))
            link(dve.tensor_scalar(node[:, 3, :], node[:, 3, :], 1e-9, None, ALU.add))
            link(dve.reciprocal(node[:, 3, :], node[:, 3, :]))
            link(dve.tensor_tensor(node[:, 3, :], node[:, 3, :], node[:, 2, :], ALU.mult))
            link(dve.tensor_tensor(message, message, spread_out(node[:, 3, :]), ALU.mult))
            link(dve.memset(prod, 0.0))
            link(dve.tensor_tensor(live(prod), live(h_v), message, ALU.mult))

        def overall_max(pool):
            pool.wait_ge(topped, 1)
            pool.partition_all_reduce(node[:, 0, 1:2], node[:, 0, 0:1], P, RMAX).then_inc(overall, 1)

        def exp_scale(act):
            act.wait_ge(overall, 1)
            act.wait_ge(chain_of_f1[0], 1)
            act.activation(node[:, 2, :], node[:, 1, :], ACT.Exp, scale=1.0 - SLOPE).then_inc(scaled, 1)

        chain_of_f1 = [None]
        diff = sem("diff")

        def finish1_wrapped(dve, link):
            first = [True]

            def link1(ins):
                if first[0]:
                    first[0] = False
                    ins.then_inc(diff, 1)
                    return
                link(ins)

            finish1(dve, link1)

        chain_of_f1[0] = diff
        by_node("f1", finish1_wrapped, pool_program=overall_max, act_program=exp_scale)
        prod_w = blocks(slab_b)
        dense("d1b", [prod], [weights["l1w2"]], biases["l1w2"], D, target=prod_w)

        def finish1b(dve, link):
            link(dve.tensor_tensor(message, message, live(h_v), ALU.add))
            link(dve.tensor_tensor(message, message, live(prod_w), ALU.add))
            link(dve.scalar_tensor_tensor(message, message, SLOPE, message, ALU.mult, ALU.max))
            link(dve.tensor_tensor(live(x_v), live(x_v), message, ALU.add))

        by_node("f1b", finish1b)

        release()

        norm("n2")
        state = blocks(slab_a)
        sums2 = blocks(slab_acc)
        dense("d2", [h_v], [weights["pre"]], biases["pre"], D, target=state, table=tab2[0])
        for n in range(3):
            spread(f"r{n}", tab2[n], sums2)
            dense(f"u{n}", [sums2, state], [weights[f"agg{n}"], weights[f"own{n}"]], biases[f"u{n}"], D,
                  target=state, table=tab2[n + 1] if n < 2 else None, relu=True)
        by_node("f2", lambda dve, link: link(dve.tensor_tensor(x_v, x_v, state, ALU.add)))

        release()

        norm("n3")
        dense("d3s", [h_v], [weights["ts"]], None, 2 * D, table=tab3)
        own_gate, own_core = blocks(slab_a), blocks(slab_b)
        dense("d3d", [h_v], [weights["td"]], biases["td"], 2 * D, target=own_gate, target2=own_core)
        by_node("f3", lambda dve, link: link(dve.tensor_tensor(x_v, x_v, h_v, ALU.add)))
        gated("g3", tab3, io["edge"], own_gate, own_core, sums2)

        written, summed3 = sem("written"), sem("summed3")
        with nc.Block() as block:
            @block.vector
            def _(dve):
                dve.tensor_tensor(x_v, x_v, sums2, ALU.add).then_inc(summed3, 1)

            @block.sync
            def _(sp):
                sp.wait_ge(summed3, 1)
                sp.dma_start(out[0:(BLKS - 1) * P, :].rearrange("(b p) f -> p b f", p=P),
                             x_v[:, 0:BLKS - 1, :]).then_inc(written, 16)
                sp.dma_start(out[(BLKS - 1) * P:N, :], x_v[0:TAIL, BLKS - 1, :]).then_inc(written, 16)
                sp.wait_ge(written, 32)


def lay_out(inputs):
    import numpy as np
    c = np.ascontiguousarray
    i = {k: np.asarray(v) for k, v in inputs.items()}
    return {
        "x": c(i["x"]), "src": c(i["src"]), "dst": c(i["dst"]), "edge": c(i["edge_attr_128"]),
        "w0": c(i["L0_gnn_W"]), "w0_t": c(i["L0_gnn_W"].T),
        "a0": c(i["L0_gnn_a"].reshape(2, D)[::-1].T), "a1": c(i["L1_gnn_a"].reshape(2, D).T),
        "watt_t": c(i["L1_gnn_Watt_w"].T), "batt": c(i["L1_gnn_Watt_b"].reshape(D, 1)),
        "w1": c(i["L1_gnn_W1_w"]), "b1": c(i["L1_gnn_W1_b"].reshape(1, D)),
        "w2": c(i["L1_gnn_W2_w"]), "b2": c(i["L1_gnn_W2_b"].reshape(1, D)),
        "wpre": c(i["L2_gnn_W_pre"]), "bpre": c(i["L2_gnn_b_pre"].reshape(1, D)),
        "wconv_t": c(i["L2_gnn_W_conv"].transpose(0, 2, 1)), "bconv_t": c(i["L2_gnn_b_conv"].T),
        "wupd": c(i["L2_gnn_W_upd"]), "bupd": c(i["L2_gnn_b_upd"]),
        "wf": c(i["L3_gnn_W_f"]), "bf": c(i["L3_gnn_b_f"].reshape(1, D)),
        "ws": c(i["L3_gnn_W_s"]), "bs": c(i["L3_gnn_b_s"].reshape(1, D)),
    }


def kernel(**inputs):
    import concourse.bacc as bacc
    from concourse.bass_utils import run_bass_kernel_spmd

    nc = bacc.Bacc("TRN2", target_bir_lowering=False, num_devices=1)
    arrays, io = {}, {}
    for name, a in lay_out(inputs).items():
        arrays[f"in_{name}"] = a
        io[name] = nc.dram_tensor(f"in_{name}", a.shape, mybir.dt.from_np(a.dtype), kind="ExternalInput").ap()
    out = nc.dram_tensor("out", (N, D), F32, kind="ExternalOutput").ap()
    gnn(nc, io, out)
    r = run_bass_kernel_spmd(nc, [arrays], core_ids=[0])
    return r.results[0]["out"]
```
